# Optimizing a Trainium2 kernel written in Bass

```python
import numpy as np
import jax
import jax.numpy as jnp

def _softmax(x, axis=-1):
    return jax.nn.softmax(x, axis=axis)

def _gelu(x):
    return jax.nn.gelu(x, approximate=True)

def _silu(x):
    return jax.nn.silu(x)

def _sigmoid(x):
    return jax.nn.sigmoid(x)

def _layernorm(x, axis=-1, eps=1e-05):
    m = jnp.mean(x, axis=axis, keepdims=True)
    v = jnp.var(x, axis=axis, keepdims=True)
    return (x - m) / jnp.sqrt(v + eps)

def _scatter_add(tgt, idx, src, axis=0):
    return tgt.at[idx].add(src)

def _segment_sum(src, seg, n):
    return jax.ops.segment_sum(src, seg, n)
kernel_name = 'mk_decoder_preln_d2_seqx_r8_ea1fd4'

def setup_inputs(seed: int=0):
    np.random.seed(seed)
    _w = jnp.asarray

    def _rec_inputs():
        import jax
        import jax.numpy as jnp
        _rk = jax.random.key(seed)
        x = 7.22e-05 + 1 * jax.random.normal(jax.random.fold_in(_rk, 1), (16, 64, 256), jnp.float32)
        _lenS = 64 - jax.random.randint(jax.random.fold_in(_rk, 7), (16,), 0, max(1, 64 // 4) + 1, jnp.int32)
        _lenS2 = 64 - jax.random.randint(jax.random.fold_in(_rk, 8), (16,), 0, max(1, 64 // 4) + 1, jnp.int32)
        _ctx_2048P = jax.random.normal(jax.random.fold_in(_rk, 11), (16, 16, 256), jnp.float32)
        _ctx_2048c = jax.random.dirichlet(jax.random.fold_in(_rk, 511), 0.3 * jnp.ones((16,), jnp.float32), (16, 64))
        _ctx_2048t = jnp.einsum('bsk,bkd->bsd', _ctx_2048c, _ctx_2048P)
        _ctx_2048t = _ctx_2048t * jax.lax.rsqrt(jnp.mean(jnp.square(_ctx_2048t)) + 1e-12) * 0.953939
        ctx_2048 = 4.13588e-05 + 0.999923 * (_ctx_2048t + 0.3 * jax.random.normal(jax.random.fold_in(_rk, 611), (16, 64, 256), jnp.float32))
        _validS = jnp.arange(64)[None, :] < _lenS[:, None]
        _validS2 = jnp.arange(64)[None, :] < _lenS2[:, None]
        _causal = jnp.tril(jnp.ones((64, 64), dtype=bool))
        mask_BxSxS2_ff0 = jnp.where(jnp.ones((16, 64, 64), dtype=bool), 0.0, -1000000000.0).astype(jnp.float32)
        return (x, ctx_2048, mask_BxSxS2_ff0)
    x, ctx_2048, mask_BxSxS2_ff0 = _rec_inputs()

    def _L0_attn_setup():
        import jax, jax.numpy as jnp
        import numpy as np
        D_MODEL = 256
        N_HEADS = 16
        HEAD_DIM = D_MODEL // N_HEADS
        ROPE_THETA = 10000.0
        BATCH = 2
        SEQ_LEN = 256

        def _apply_rope(x):
            S = x.shape[2]
            inv_freq = 1.0 / ROPE_THETA ** (jnp.arange(0, HEAD_DIM, 2, dtype=jnp.float32) / HEAD_DIM)
            t = jnp.arange(S, dtype=jnp.float32)
            freqs = jnp.outer(t, inv_freq)
            cos = jnp.cos(freqs)
            sin = jnp.sin(freqs)
            x1 = x[..., 0::2]
            x2 = x[..., 1::2]
            rot = jnp.stack([x1 * cos - x2 * sin, x1 * sin + x2 * cos], axis=-1)
            return rot.reshape(x.shape)
        key = jax.random.key(seed)
        ks = jax.random.split(key, 5)
        scale = 1.0 / np.sqrt(D_MODEL)
        x = jax.random.normal(ks[0], (BATCH, SEQ_LEN, D_MODEL), dtype=jnp.float32)
        Wq = jax.random.normal(ks[1], (D_MODEL, D_MODEL), dtype=jnp.float32) * scale
        Wk = jax.random.normal(ks[2], (D_MODEL, D_MODEL), dtype=jnp.float32) * scale
        Wv = jax.random.normal(ks[3], (D_MODEL, D_MODEL), dtype=jnp.float32) * scale
        Wo = jax.random.normal(ks[4], (D_MODEL, D_MODEL), dtype=jnp.float32) * scale
        return {'x': x, 'Wq': Wq, 'Wk': Wk, 'Wv': Wv, 'Wo': Wo}
    _L0_attn_all = _L0_attn_setup()
    _L0_attn_in = {k: v for k, v in _L0_attn_all.items() if k in ('Wq', 'Wk', 'Wv', 'Wo')}
    del _L0_attn_all

    def _L0_xattn_setup():
        import jax, jax.numpy as jnp
        import numpy as np
        N_HEAD = 8
        key = jax.random.key(seed)
        k1, k2, k3 = jax.random.split(key, 3)
        B, D, L = (4, 128, 256)
        q = jax.random.normal(k1, (B, D, L), dtype=jnp.float32)
        k = jax.random.normal(k2, (B, D, L), dtype=jnp.float32)
        v = jax.random.normal(k3, (B, D, L), dtype=jnp.float32)
        gamma = jnp.ones((), dtype=jnp.float32)
        return {'q': q, 'k': k, 'v': v, 'gamma': gamma}
    _L0_xattn_all = _L0_xattn_setup()
    _L0_xattn_in = {k: v for k, v in _L0_xattn_all.items() if k in ('gamma',)}
    del _L0_xattn_all

    def _L0_ffn_setup():
        import jax, jax.numpy as jnp
        import numpy as np

        def _sparsify_2to4(h):
            B, S, I = h.shape
            g = h.reshape(B, S, I // 4, 4)
            a = jnp.abs(g)
            _, idx = jax.lax.top_k(a, 2)
            pos = jnp.arange(4)
            mask = (pos == idx[..., 0:1]) | (pos == idx[..., 1:2])
            return (g * mask.astype(g.dtype)).reshape(B, S, I)
        key = jax.random.key(seed)
        k1, k2, k3, k4 = jax.random.split(key, 4)
        B, S, H, I = (4, 256, 256, 1024)
        x = jax.random.normal(k1, (B, S, H), dtype=jnp.float32)
        w_gate = jax.random.normal(k2, (H, I), dtype=jnp.float32) / np.sqrt(H)
        w_up = jax.random.normal(k3, (H, I), dtype=jnp.float32) / np.sqrt(H)
        w_down = jax.random.normal(k4, (I, H), dtype=jnp.float32) / np.sqrt(I)
        return {'x': x, 'w_gate': w_gate, 'w_up': w_up, 'w_down': w_down}
    _L0_ffn_all = _L0_ffn_setup()
    _L0_ffn_in = {k: v for k, v in _L0_ffn_all.items() if k in ('w_gate', 'w_up', 'w_down')}
    del _L0_ffn_all

    def _L1_attn_setup():
        import jax, jax.numpy as jnp
        import numpy as np
        DIM = 256
        NUM_HEADS = 16
        HEAD_DIM = DIM // NUM_HEADS
        WINDOW_SIZE = 384
        SCALE = HEAD_DIM ** (-0.5)
        NEG_INF = -1000000000.0

        def _window_mask(q_len: int, kv_len: int) -> jnp.ndarray:
            i = jnp.arange(q_len)[:, None]
            j = jnp.arange(kv_len)[None, :]
            start = jnp.maximum(0, kv_len - WINDOW_SIZE + i)
            allowed = (j >= start) & (j <= i)
            return ~allowed
        key = jax.random.key(seed)
        ks = jax.random.split(key, 6)
        B, N = (2, 256)
        x = jax.random.normal(ks[0], (B, N, DIM), dtype=jnp.float32)
        w_init = 0.02
        Wq = jax.random.normal(ks[1], (DIM, DIM), dtype=jnp.float32) * w_init
        Wk = jax.random.normal(ks[2], (DIM, DIM), dtype=jnp.float32) * w_init
        Wv = jax.random.normal(ks[3], (DIM, DIM), dtype=jnp.float32) * w_init
        Wo = jax.random.normal(ks[4], (DIM, DIM), dtype=jnp.float32) * w_init
        zeros = jnp.zeros((DIM,), dtype=jnp.float32)
        return {'x': x, 'Wq': Wq, 'bq': zeros, 'Wk': Wk, 'bk': zeros, 'Wv': Wv, 'bv': zeros, 'Wo': Wo, 'bo': zeros}
    _L1_attn_all = _L1_attn_setup()
    _L1_attn_in = {k: v for k, v in _L1_attn_all.items() if k in ('Wq', 'bq', 'Wk', 'bk', 'Wv', 'bv', 'Wo', 'bo')}
    del _L1_attn_all

    def _L1_xattn_setup():
        import jax, jax.numpy as jnp
        import numpy as np
        NUM_HEADS = 16
        EPS = 1e-08

        def _dyn_quant(x):
            s = jnp.maximum(jnp.max(jnp.abs(x), axis=-1, keepdims=True) / 127.0, EPS)
            q = jnp.clip(jnp.round(x / s), -127.0, 127.0)
            return (q, s)

        def _quant_weight(w):
            s = jnp.maximum(jnp.max(jnp.abs(w), axis=1, keepdims=True) / 127.0, EPS)
            q = jnp.clip(jnp.round(w / s), -127.0, 127.0)
            return (q, s)

        def _w8a8_linear(x, w, b):
            qx, sx = _dyn_quant(x)
            qw, sw = _quant_weight(w)
            y = jnp.einsum('bnc,oc->bno', qx, qw) * (sx * sw[:, 0])
            return y + b
        key = jax.random.key(seed)
        ks = jax.random.split(key, 9)
        B, N, L, C = (2, 512, 64, 256)
        sc = 0.02
        return {'x': jax.random.normal(ks[0], (B, N, C), jnp.float32), 'cond': jax.random.normal(ks[1], (B, L, C), jnp.float32), 'mask': jnp.zeros((B, N, L), jnp.float32), 'wq': jax.random.normal(ks[2], (C, C), jnp.float32) * sc, 'bq': jnp.zeros((C,), jnp.float32), 'wk': jax.random.normal(ks[3], (C, C), jnp.float32) * sc, 'bk': jnp.zeros((C,), jnp.float32), 'wv': jax.random.normal(ks[4], (C, C), jnp.float32) * sc, 'bv': jnp.zeros((C,), jnp.float32), 'wo': jax.random.normal(ks[5], (C, C), jnp.float32) * sc, 'bo': jnp.zeros((C,), jnp.float32)}
    _L1_xattn_all = _L1_xattn_setup()
    _L1_xattn_in = {k: v for k, v in _L1_xattn_all.items() if k in ('wq', 'bq', 'wk', 'bk', 'wv', 'bv', 'wo', 'bo')}
    del _L1_xattn_all

    def _L1_ffn_setup():
        import jax, jax.numpy as jnp
        import numpy as np
        TOP_K = 4
        ROUTED_SCALE = 1.0
        NORM_TOPK = True
        B, S, H = (1, 256, 256)
        E, I = (16, 96)
        IS = 96
        key = jax.random.key(seed)
        ks = jax.random.split(key, 8)
        s = 0.02
        return {'hidden_states': jax.random.normal(ks[0], (B, S, H), jnp.float32), 'router_w': jax.random.normal(ks[1], (E, H), jnp.float32) * s, 'e_bias': jax.random.normal(ks[2], (E,), jnp.float32) * s, 'gate_up_proj': jax.random.normal(ks[3], (E, 2 * I, H), jnp.float32) * s, 'down_proj': jax.random.normal(ks[4], (E, H, I), jnp.float32) * s, 'shared_gate_w': jax.random.normal(ks[5], (IS, H), jnp.float32) * s, 'shared_up_w': jax.random.normal(ks[6], (IS, H), jnp.float32) * s, 'shared_down_w': jax.random.normal(ks[7], (H, IS), jnp.float32) * s}
    _L1_ffn_all = _L1_ffn_setup()
    _L1_ffn_in = {k: v for k, v in _L1_ffn_all.items() if k in ('router_w', 'e_bias', 'gate_up_proj', 'down_proj', 'shared_gate_w', 'shared_up_w', 'shared_down_w')}
    del _L1_ffn_all
    return {'x': x, 'ctx_2048': ctx_2048, 'mask_BxSxS2_ff0': mask_BxSxS2_ff0, 'L0_attn_Wq': _L0_attn_in['Wq'], 'L0_attn_Wk': _L0_attn_in['Wk'], 'L0_attn_Wv': _L0_attn_in['Wv'], 'L0_attn_Wo': _L0_attn_in['Wo'], 'L0_xattn_gamma': _L0_xattn_in['gamma'], 'L0_ffn_w_gate': _L0_ffn_in['w_gate'], 'L0_ffn_w_up': _L0_ffn_in['w_up'], 'L0_ffn_w_down': _L0_ffn_in['w_down'], 'L1_attn_Wq': _L1_attn_in['Wq'], 'L1_attn_bq': _L1_attn_in['bq'], 'L1_attn_Wk': _L1_attn_in['Wk'], 'L1_attn_bk': _L1_attn_in['bk'], 'L1_attn_Wv': _L1_attn_in['Wv'], 'L1_attn_bv': _L1_attn_in['bv'], 'L1_attn_Wo': _L1_attn_in['Wo'], 'L1_attn_bo': _L1_attn_in['bo'], 'L1_xattn_wq': _L1_xattn_in['wq'], 'L1_xattn_bq': _L1_xattn_in['bq'], 'L1_xattn_wk': _L1_xattn_in['wk'], 'L1_xattn_bk': _L1_xattn_in['bk'], 'L1_xattn_wv': _L1_xattn_in['wv'], 'L1_xattn_bv': _L1_xattn_in['bv'], 'L1_xattn_wo': _L1_xattn_in['wo'], 'L1_xattn_bo': _L1_xattn_in['bo'], 'L1_ffn_router_w': _L1_ffn_in['router_w'], 'L1_ffn_e_bias': _L1_ffn_in['e_bias'], 'L1_ffn_gate_up_proj': _L1_ffn_in['gate_up_proj'], 'L1_ffn_down_proj': _L1_ffn_in['down_proj'], 'L1_ffn_shared_gate_w': _L1_ffn_in['shared_gate_w'], 'L1_ffn_shared_up_w': _L1_ffn_in['shared_up_w'], 'L1_ffn_shared_down_w': _L1_ffn_in['shared_down_w']}

def reference(x, ctx_2048, mask_BxSxS2_ff0, L0_attn_Wq, L0_attn_Wk, L0_attn_Wv, L0_attn_Wo, L0_xattn_gamma, L0_ffn_w_gate, L0_ffn_w_up, L0_ffn_w_down, L1_attn_Wq, L1_attn_bq, L1_attn_Wk, L1_attn_bk, L1_attn_Wv, L1_attn_bv, L1_attn_Wo, L1_attn_bo, L1_xattn_wq, L1_xattn_bq, L1_xattn_wk, L1_xattn_bk, L1_xattn_wv, L1_xattn_bv, L1_xattn_wo, L1_xattn_bo, L1_ffn_router_w, L1_ffn_e_bias, L1_ffn_gate_up_proj, L1_ffn_down_proj, L1_ffn_shared_gate_w, L1_ffn_shared_up_w, L1_ffn_shared_down_w):
    import jax
    import jax.numpy as jnp

    def _L0_attn_ref(x, Wq, Wk, Wv, Wo):
        import jax, jax.numpy as jnp
        import numpy as np
        D_MODEL = 256
        N_HEADS = 16
        HEAD_DIM = D_MODEL // N_HEADS
        ROPE_THETA = 10000.0
        BATCH = 2
        SEQ_LEN = 256

        def _apply_rope(x):
            S = x.shape[2]
            inv_freq = 1.0 / ROPE_THETA ** (jnp.arange(0, HEAD_DIM, 2, dtype=jnp.float32) / HEAD_DIM)
            t = jnp.arange(S, dtype=jnp.float32)
            freqs = jnp.outer(t, inv_freq)
            cos = jnp.cos(freqs)
            sin = jnp.sin(freqs)
            x1 = x[..., 0::2]
            x2 = x[..., 1::2]
            rot = jnp.stack([x1 * cos - x2 * sin, x1 * sin + x2 * cos], axis=-1)
            return rot.reshape(x.shape)
        B, S, _ = x.shape
        q = (x @ Wq.T).reshape(B, S, N_HEADS, HEAD_DIM).transpose(0, 2, 1, 3)
        k = (x @ Wk.T).reshape(B, S, N_HEADS, HEAD_DIM).transpose(0, 2, 1, 3)
        v = (x @ Wv.T).reshape(B, S, N_HEADS, HEAD_DIM).transpose(0, 2, 1, 3)
        q = _apply_rope(q)
        k = _apply_rope(k)
        scores = jnp.einsum('bhqd,bhkd->bhqk', q, k) / np.sqrt(HEAD_DIM).astype(np.float32)
        causal = jnp.tril(jnp.ones((S, S), dtype=bool))
        scores = jnp.where(causal, scores, -jnp.inf)
        attn = jax.nn.softmax(scores, axis=-1)
        out = jnp.einsum('bhqk,bhkd->bhqd', attn, v)
        out = out.transpose(0, 2, 1, 3).reshape(B, S, N_HEADS * HEAD_DIM)
        return out @ Wo.T

    def _L0_xattn_ref(q, k, v, gamma):
        import jax, jax.numpy as jnp
        import numpy as np
        N_HEAD = 8
        B, Dq, Lq = q.shape
        Dv, Lk = (v.shape[-2], v.shape[-1])
        h = N_HEAD
        dq = Dq // h
        dv = Dv // h
        qh = q.reshape(B, h, dq, Lq)
        kh = k.reshape(B, h, dq, Lk)
        vh = v.reshape(B, h, dv, Lk)
        scale = 1.0 / jnp.sqrt(jnp.asarray(dq, dtype=q.dtype))
        qk = jnp.einsum('bhdq,bhdl->bhql', qh, kh) * scale
        sm = jax.nn.softmax(qk, axis=-1)
        ret = jnp.einsum('bhql,bhdl->bhdq', sm, vh)
        ret = ret.reshape(B, Dv, Lq)
        return gamma * ret

    def _L0_ffn_ref(x, w_gate, w_up, w_down):
        import jax, jax.numpy as jnp
        import numpy as np

        def _sparsify_2to4(h):
            B, S, I = h.shape
            g = h.reshape(B, S, I // 4, 4)
            a = jnp.abs(g)
            _, idx = jax.lax.top_k(a, 2)
            pos = jnp.arange(4)
            mask = (pos == idx[..., 0:1]) | (pos == idx[..., 1:2])
            return (g * mask.astype(g.dtype)).reshape(B, S, I)
        h = jax.nn.silu(jnp.einsum('bsh,hi->bsi', x, w_gate)) * jnp.einsum('bsh,hi->bsi', x, w_up)
        h_sparse = _sparsify_2to4(h)
        return jnp.einsum('bsi,ih->bsh', h_sparse, w_down)

    def _L1_attn_ref(x, Wq, bq, Wk, bk, Wv, bv, Wo, bo):
        import jax, jax.numpy as jnp
        import numpy as np
        DIM = 256
        NUM_HEADS = 16
        HEAD_DIM = DIM // NUM_HEADS
        WINDOW_SIZE = 384
        SCALE = HEAD_DIM ** (-0.5)
        NEG_INF = -1000000000.0

        def _window_mask(q_len: int, kv_len: int) -> jnp.ndarray:
            i = jnp.arange(q_len)[:, None]
            j = jnp.arange(kv_len)[None, :]
            start = jnp.maximum(0, kv_len - WINDOW_SIZE + i)
            allowed = (j >= start) & (j <= i)
            return ~allowed
        B, N, C = x.shape
        H, D = (NUM_HEADS, HEAD_DIM)
        q = (x @ Wq.T + bq).reshape(B, N, H, D).transpose(0, 2, 1, 3)
        k = (x @ Wk.T + bk).reshape(B, N, H, D).transpose(0, 2, 1, 3)
        v = (x @ Wv.T + bv).reshape(B, N, H, D).transpose(0, 2, 1, 3)
        scores = jnp.einsum('bhqd,bhkd->bhqk', q, k) * SCALE
        mask = _window_mask(N, N)
        scores = jnp.where(mask[None, None], NEG_INF, scores)
        attn = jax.nn.softmax(scores, axis=-1)
        out = jnp.einsum('bhqk,bhkd->bhqd', attn, v)
        out = out.transpose(0, 2, 1, 3).reshape(B, N, C)
        return out @ Wo.T + bo

    def _L1_xattn_ref(x, cond, mask, wq, bq, wk, bk, wv, bv, wo, bo):
        import jax, jax.numpy as jnp
        import numpy as np
        NUM_HEADS = 16
        EPS = 1e-08

        def _dyn_quant(x):
            s = jnp.maximum(jnp.max(jnp.abs(x), axis=-1, keepdims=True) / 127.0, EPS)
            q = jnp.clip(jnp.round(x / s), -127.0, 127.0)
            return (q, s)

        def _quant_weight(w):
            s = jnp.maximum(jnp.max(jnp.abs(w), axis=1, keepdims=True) / 127.0, EPS)
            q = jnp.clip(jnp.round(w / s), -127.0, 127.0)
            return (q, s)

        def _w8a8_linear(x, w, b):
            qx, sx = _dyn_quant(x)
            qw, sw = _quant_weight(w)
            y = jnp.einsum('bnc,oc->bno', qx, qw) * (sx * sw[:, 0])
            return y + b
        B, N, C = x.shape
        L = cond.shape[1]
        H = NUM_HEADS
        D = C // H
        inv_sqrt_d = np.float32(1.0 / np.sqrt(D))
        q = _w8a8_linear(x, wq, bq).reshape(B, N, H, D).transpose(0, 2, 1, 3)
        k = (cond @ wk.T + bk).reshape(B, L, H, D).transpose(0, 2, 1, 3)
        v = (cond @ wv.T + bv).reshape(B, L, H, D).transpose(0, 2, 1, 3)
        scores = jnp.einsum('bhnd,bhld->bhnl', q, k) * inv_sqrt_d + mask[:, None]
        attn = jax.nn.softmax(scores, axis=-1)
        o = jnp.einsum('bhnl,bhld->bhnd', attn, v)
        o = o.transpose(0, 2, 1, 3).reshape(B, N, C)
        return _w8a8_linear(o, wo, bo)

    def _L1_ffn_ref(hidden_states, router_w, e_bias, gate_up_proj, down_proj, shared_gate_w, shared_up_w, shared_down_w):
        import jax, jax.numpy as jnp
        import numpy as np
        TOP_K = 4
        ROUTED_SCALE = 1.0
        NORM_TOPK = True
        B, S, H = (1, 256, 256)
        E, I = (16, 96)
        IS = 96
        orig_shape = hidden_states.shape
        x = hidden_states.reshape(-1, orig_shape[-1])
        T = x.shape[0]
        scores = jax.nn.sigmoid(x @ router_w.T)
        _, topk_idx = jax.lax.top_k(scores + e_bias[None, :], TOP_K)
        topk_w = jnp.take_along_axis(scores, topk_idx, axis=1)
        if NORM_TOPK:
            topk_w = topk_w / (topk_w.sum(axis=-1, keepdims=True) + 1e-20)
        topk_w = topk_w * ROUTED_SCALE
        combine = jnp.zeros((T, E), x.dtype).at[jnp.arange(T)[:, None], topk_idx].add(topk_w)

        def step(acc, xs):
            gu_w, d_w, c = xs
            gu = x @ gu_w.T
            g, u = jnp.split(gu, 2, axis=1)
            y = jax.nn.silu(g) * u @ d_w.T
            return (acc + c[:, None] * y, None)
        routed, _ = jax.lax.scan(step, jnp.zeros_like(x), (gate_up_proj, down_proj, combine.T))
        shared = jax.nn.silu(x @ shared_gate_w.T) * (x @ shared_up_w.T) @ shared_down_w.T
        return (routed + shared).reshape(orig_shape)
    x = x + _L0_attn_ref(_layernorm(x, axis=-1), L0_attn_Wq, L0_attn_Wk, L0_attn_Wv, L0_attn_Wo)
    x = x + _L0_xattn_ref(_layernorm(x, axis=-1), ctx_2048, ctx_2048, L0_xattn_gamma)
    x = x + _L0_ffn_ref(_layernorm(x, axis=-1), L0_ffn_w_gate, L0_ffn_w_up, L0_ffn_w_down)
    x = x + _L1_attn_ref(_layernorm(x, axis=-1), L1_attn_Wq, L1_attn_bq, L1_attn_Wk, L1_attn_bk, L1_attn_Wv, L1_attn_bv, L1_attn_Wo, L1_attn_bo)
    x = x + _L1_xattn_ref(_layernorm(x, axis=-1), ctx_2048, mask_BxSxS2_ff0, L1_xattn_wq, L1_xattn_bq, L1_xattn_wk, L1_xattn_bk, L1_xattn_wv, L1_xattn_bv, L1_xattn_wo, L1_xattn_bo)
    x = x + _L1_ffn_ref(_layernorm(x, axis=-1), L1_ffn_router_w, L1_ffn_e_bias, L1_ffn_gate_up_proj, L1_ffn_down_proj, L1_ffn_shared_gate_w, L1_ffn_shared_up_w, L1_ffn_shared_down_w)
    return x

_drawn_inputs = setup_inputs


def setup_inputs(seed=0):
    import zlib

    import numpy as np

    out = dict(_drawn_inputs(seed))
    spreads = {'L1_attn_bq': (0.0, 0.8),
     'L1_attn_bk': (0.0, 0.8),
     'L1_attn_bv': (0.0, 0.404),
     'L1_attn_bo': (0.0, 0.1),
     'L1_xattn_bq': (0.0, 0.8),
     'L1_xattn_bk': (0.0, 0.8),
     'L1_xattn_bv': (0.0, 0.43),
     'L1_xattn_bo': (0.0, 0.1)}
    factors = {'L1_attn_Wq': 8.0,
     'L1_attn_Wk': 8.0,
     'L1_xattn_wq': 8.0,
     'L1_xattn_wk': 8.0,
     'L1_ffn_router_w': 8.0,
     'L1_ffn_e_bias': 8.0,
     'L1_ffn_gate_up_proj': 8.0,
     'L1_ffn_down_proj': 8.0,
     'L1_ffn_shared_gate_w': 8.0,
     'L1_ffn_shared_up_w': 8.0,
     'L1_ffn_shared_down_w': 8.0}
    for name, (base, spread) in spreads.items():
        noise = np.random.default_rng([zlib.crc32(name.encode()), seed]).standard_normal(out[name].shape)
        drawn = base * np.exp(spread * noise) if base else spread * noise
        out[name] = jnp.asarray(drawn.astype(out[name].dtype))
    for name, factor in factors.items():
        out[name] = (out[name] * factor).astype(out[name].dtype)
    return out
```

```python
import numpy as np
import concourse.bass as bass
from concourse import mybir
from contextlib import ExitStack

F32 = mybir.dt.float32
BF16 = mybir.dt.bfloat16
U32 = mybir.dt.uint32
ALU = mybir.AluOpType
ACT = mybir.ActivationFunctionType
AX = mybir.AxisListType

P = 128
B, S, D = 16, 64, 256
TILES = B * S // P
KC = D // P
H, HD = 16, 16
PAIRS = H // 2
NEG = -1e30
LN_EPS = 1e-5
Q_EPS = 1e-8
ROUND = 1.5 * 2.0 ** 23
XH, XD = 8, 8
XP = P // XD
XG = 2
XV = 32
XR = 9 * XD
I0 = 1024
E, EI, TOPK = 16, 96, 4
PL = 4
GB = I0 // (PL * P)
HALF = 4
MC = E * EI // P
MCS = MC + 1


def constants():
    pos = np.arange(S, dtype=np.float32)
    inv = (1.0 / np.float32(10000.0) ** (np.arange(0, HD, 2, dtype=np.float32) / np.float32(HD))).astype(np.float32)
    ang = np.outer(pos, inv).astype(np.float32)
    cos, sin = np.cos(ang).astype(np.float32), np.sin(ang).astype(np.float32)
    cs = np.stack([cos, cos], -1).reshape(S, HD)
    sn = np.stack([-sin, sin], -1).reshape(S, HD)
    causal = np.where(np.tril(np.ones((S, S), bool)), 0.0, NEG).astype(np.float32)
    head = np.arange(P) // HD
    unit = np.arange(MC * P) // EI
    row, col = np.arange(P)[:, None], np.arange(XV)[None, :]
    place = (row // XV == col // XD) & (row % XV == col % XD)
    total = (row // XV == col // XD) & (row % XV == XD)
    return {
        "c_ident": np.eye(P, dtype=np.float32),
        "c_rope": np.tile(np.concatenate([cs, sn], 1), (2, 1)).astype(np.float32),
        "c_causal": np.tile(causal, (2, 1)),
        "c_parity": np.stack([head % 2 == 0, head % 2 == 1], 1).astype(np.float32),
        "c_place": np.stack([place, total], 1).reshape(P, 2 * XV).astype(np.float32),
        "c_iota": np.tile(np.arange(E, dtype=np.float32), (P, 1)),
        "c_expert": np.tile(unit[None, :] == np.arange(E)[:, None], (3, 1)).astype("bfloat16"),
    }


class Kit:
    pass


def allocate(nc, ctx, dram):
    k = Kit()
    k.nc, k.dram = nc, dram

    def sb(name, shape, dt=F32):
        return ctx.enter_context(nc.sbuf_tensor(name, shape, dt))

    k.layer_sems = {}

    def sem(name):
        handle = nc.alloc_semaphore(name=name)
        k.layer_sems.setdefault(name.split("_")[0], []).append(handle)
        return handle

    k.sb, k.sem = sb, sem
    k.x = sb("x", [P, TILES, D])
    k.ctx = sb("ctx", [P, TILES, D])
    k.ident = sb("ident", [P, P])
    k.identb = sb("identb", [P, P], BF16)
    k.rope = sb("rope", [P, 2, HD])
    k.causal = sb("causal", [P, S])
    k.parity = sb("parity", [P, 2])
    k.halfpow = sb("halfpow", [P, 1])
    k.ones = sb("ones", [P, P])
    k.psum = ctx.enter_context(nc.psum_tensor("psum", [P, 8, 512], F32))
    k.stats = sb("stats", [P, 2, 6])
    k.moments = sb("moments", [P, 2, 2])
    k.varplus = sb("varplus", [P, 2, 1])
    k.pause = sb("pause", [P, 1])
    k.rstd = sb("rstd", [P, 2, 1])
    k.xn = [sb(f"xn{s}", [P, D]) for s in range(2)]
    k.xnT = [sb(f"xnT{s}", [P, KC, P]) for s in range(2)]
    k.xqT = [sb(f"xqT{s}", [P, KC, P], BF16) for s in range(2)]
    k.ctxs = [sb(f"ctxs{s}", [P, D]) for s in range(2)]
    k.ctxT = [sb(f"ctxT{s}", [P, KC, P]) for s in range(2)]
    k.qk = [sb(f"qk{s}", [P, 2 * D]) for s in range(2)]
    k.qkT = [sb(f"qkT{s}", [P, 4, P]) for s in range(2)]
    k.kTm = [sb(f"kTm{s}", [P, 2, 2, P]) for s in range(2)]
    k.probs = [sb(f"probs{s}", [P, H * S]) for s in range(2)]
    k.pT = [sb(f"pT{s}", [P, PAIRS, P]) for s in range(2)]
    k.vblk = [sb(f"vblk{s}", [P, 2, PAIRS, 34]) for s in range(2)]
    k.on = [sb(f"on{s}", [P, D]) for s in range(2)]
    k.oT = [sb(f"oT{s}", [P, KC, P]) for s in range(2)]
    k.oTb = [sb(f"oTb{s}", [P, KC, P], BF16) for s in range(2)]
    k.rot = sb("rot", [P, 2 * D])
    k.ytmp = sb("ytmp", [P, D])
    k.rowmax = sb("rowmax", [P, 2, H])
    k.rsum = sb("rsum", [P, 2, PAIRS, 2])
    k.qscr = sb("qscr", [P, 2])
    k.sx = sb("sx", [P, 2, 1])
    k.so = sb("so", [P, 2, 1])
    k.mask = sb("mask", [P, TILES, S])
    k.gamma = sb("gamma", [P, 1])
    k.xsrc = [k.qkT[s][:, :, :].rearrange("p (a b) n -> p a (b n)", a=2) for s in range(2)]
    k.xpart = [sb(f"xpart{s}", [P, 3, 2, D], BF16) for s in range(2)]
    k.rest = k.rot[:, :].rearrange("p (a n) -> p a n", a=2)
    k.vT = [k.pT[s][:, :, :].rearrange("p a n -> p (a n)").rearrange("p (c a d) -> p c a d", c=KC, d=XV) for s in range(2)]
    k.xout = [k.qk[s][:, :] for s in range(2)]
    k.place = sb("place", [P, 2, XV])
    k.negmax = sb("negmax", [P, 2 * XP])
    k.mpart = [sb(f"mpart{s}", [P, P // XP, XP], BF16) for s in range(2)]
    k.mrow = [sb(f"mrow{s}", [3 * XP, P], BF16) for s in range(2)]
    k.ffn_s = [k.probs[s][:, 0:PL * P] for s in range(2)]
    k.ffn_h = [k.probs[s][:, PL * P:2 * PL * P].rearrange("p (i n) -> p i n", i=PL) for s in range(2)]
    k.ffn_a = [k.pT[s][:, 0:PL, :] for s in range(2)]
    k.near, k.over, k.far = sb("near", [P, 3, P], BF16), sb("over", [P, 2, P], BF16), sb("far", [P, 1, P], BF16)
    k.outer, k.inner = sb("outer", [P, 2, P], BF16), sb("inner", [P, 2, P], BF16)
    region_a = sb("region_a", [P, 2 * MCS * D])
    k.raw_att = region_a[:, 0:8 * KC * D].rearrange("p (w k n) -> p w k n", w=8, k=KC)
    k.raw_gu = region_a[:, :].rearrange("p (u c n) -> p u c n", u=2, n=D)
    k.hid = region_a[:, :].rearrange("p (c n) -> p c n", n=HALF * P)
    operands = 2 * 2 * XP * D // 2
    region_b = sb("region_b", [P, max(operands + 2 * XG * KC * D, 2 * KC * MCS * P + MCS * D)])
    k.raw_first = region_b[:, 0:4 * KC * D].rearrange("p (w k n) -> p w k n", w=4, k=KC)
    both = region_b[:, 0:operands].bitcast(BF16).rearrange("p (o s a n) -> p o s a n", o=2, s=2, a=XP)
    k.qop, k.kop = [both[:, 0, s] for s in range(2)], [both[:, 1, s] for s in range(2)]
    k.xprob = [region_b[:, operands + s * XG * KC * D:operands + (s + 1) * XG * KC * D].rearrange("p (a c n) -> p a c n", a=XG, c=KC) for s in range(2)]
    k.wgu = region_b[:, 0:2 * KC * MCS * P].rearrange("p (k u n) -> p k u n", k=KC, u=2)
    k.wd = region_b[:, 2 * KC * MCS * P:].rearrange("p (c n) -> p c n", n=D)
    region_c = sb("region_c", [P, KC * TILES * P + 1024 + KC * (MC * P + EI)])
    assert 3 * KC * I0 <= KC * TILES * P + 1024 + KC * (MC * P + EI)
    k.w_ffn = {"gate": region_c[:, 0:KC * I0].rearrange("p (k n) -> p k n", k=KC),
               "up": region_c[:, KC * I0:2 * KC * I0].rearrange("p (k n) -> p k n", k=KC),
               "down": region_c[:, 2 * KC * I0:3 * KC * I0].rearrange("p (g i n) -> p g i n", g=GB, i=PL)}
    k.xall = region_c[:, 0:KC * TILES * P].rearrange("p (k t n) -> p k t n", k=KC, t=TILES)
    k.sg = [region_c[:, 2048 + g * 512:2560 + g * 512] for g in range(2)]
    k.raw_d = region_c[:, KC * TILES * P + 1024:].rearrange("p (k n) -> p k n", k=KC)
    k.raw_r, k.wr = sb("raw_r", [E, D]), sb("wr", [P, KC, E])
    k.score, k.pick = sb("score", [P, TILES * E]), sb("pick", [P, TILES * E])
    k.ebias, k.iota = sb("ebias", [P, E]), sb("iota", [P, E])
    k.best, k.besti, k.bestf = sb("best", [P, TILES, 8]), sb("besti", [P, TILES, 8], U32), sb("bestf", [P, TILES, TOPK])
    k.hit, k.wsum = sb("hit", [P, TILES, TOPK, E]), sb("wsum", [P, TILES, 2])
    k.parts = sb("parts", [P, TILES, 3, E], BF16)
    k.combT, k.expert = sb("combT", [3 * E, TILES * P], BF16), sb("expert", [3 * E, MC * P], BF16)
    return k


def wait(eng, sem, value):
    if isinstance(value, int) and value <= 0:
        return
    eng.wait_ge(sem, value)


def release(k, layer):
    k.nc.clear_and_free_semaphores(k.layer_sems.pop(layer))
    k.nc.all_engine_barrier()


class Steps:

    def __init__(self, eng, sem, t, per):
        self.eng, self.sem, self.t, self.per, self.n = eng, sem, t, per, 0

    def __call__(self, ins):
        self.n += 1
        ins.then_inc(self.sem, 1)
        self.eng.wait_ge(self.sem, self.t * self.per + self.n)

    def end(self):
        assert self.n == self.per, (self.n, self.per)


def pipeline(eng, tile):
    tile(0, 0, None, None)
    tile(1, 1, 0, 0)
    with eng.Fori(0, TILES // 2 - 1) as i:
        tile(2 * i + 2, 0, 2 * i + 1, 1)
        tile(2 * i + 3, 1, 2 * i + 2, 0)
    tile(None, None, TILES - 1, 1)



def norm_moments(k, nc, steps, t, s, stats_ready):
    steps(nc.vector.bn_stats(k.stats[:, s, :], k.x[:, t, :]))
    nc.vector.memset(k.pause[:, :], 0.0)
    steps(nc.vector.bn_aggr(k.moments[:, s, :], k.stats[:, s, :]))
    nc.vector.tensor_scalar(k.varplus[:, s, :], k.moments[:, s, 1:2], LN_EPS, None, ALU.add).then_inc(stats_ready, 1)


def norm_rstd(k, nc, pool, t, s, stats_ready, rstd_ready):
    pool.wait_ge(stats_ready, t + 1)
    nc.gpsimd.tensor_tensor(k.rstd[:, s, :], k.varplus[:, s, :], k.halfpow[:, :], ALU.pow).then_inc(rstd_ready, 1)



def transpose_weights(k, name, groups, ready=None):
    nc = k.nc
    turned = k.sem(name + "_turned")
    by_act, by_dve = k.sem(name + "_by_act"), k.sem(name + "_by_dve")
    copied = [by_act, by_dve]
    with nc.Block() as block:
        @block.tensor
        def _(pe):
            if ready is not None:
                pe.wait_ge(*ready)
            for g, (blocks, dst) in enumerate(groups):
                if g >= 4:
                    pe.wait_ge(copied[g % 2], (g - 4) // 2 + 1)
                for j, b in enumerate(blocks):
                    rows, cols = b.shape
                    last = nc.tensor.transpose(k.psum[0:cols, g % 4, j * P:j * P + rows], b, k.ident[0:rows, 0:rows])
                last.then_inc(turned, 1)

        def out_of(g):
            blocks, dst = groups[g]
            rows, cols = blocks[0].shape
            src = k.psum[0:cols, g % 4, 0:len(blocks) * P].rearrange("p (j r) -> p j r", r=P)[:, :, 0:rows]
            return dst, src

        @block.scalar
        def _(act):
            for g in range(0, len(groups), 2):
                act.wait_ge(turned, g + 1)
                dst, src = out_of(g)
                nc.scalar.activation(dst, src, ACT.Copy).then_inc(by_act, 1)

        @block.vector
        def _(dve):
            for g in range(1, len(groups), 2):
                dve.wait_ge(turned, g + 1)
                dst, src = out_of(g)
                nc.vector.tensor_copy(dst, src).then_inc(by_dve, 1)


def square_groups(raw, dst):
    return [([raw[:, j, kc * P:(kc + 1) * P] for j in range(KC)],
             dst[:, kc, :].rearrange("p (j n) -> p j n", n=P)) for kc in range(KC)]



ROPE, SELF, CROSS = "rope", "self", "cross"


def attention(k, name, kind, w):
    nc, sem = k.nc, k.sem
    bf = kind == CROSS
    names = ("stats_ready rstd_ready xn_ready xT_turned xnT_ready qk_done v_done qk_ready qkT_turned "
             "qkT_ready q_ready kTm_ready scores_done softmax_in exp_done pT_turned pT_ready v_ready pv_done on_ready "
             "oT_turned oT_ready y_done x_done front_steps back_steps ctx_ready ctxT_ready").split()
    m = {n: sem(f"{name}_{n}") for n in names}
    (stats_ready, rstd_ready, xn_ready, xT_turned, xnT_ready, qk_done, v_done, qk_ready, qkT_turned,
     qkT_ready, q_ready, kTm_ready, scores_done, softmax_in, exp_done, pT_turned, pT_ready, v_ready, pv_done, on_ready,
     oT_turned, oT_ready, y_done, x_done, front_steps, back_steps, ctx_ready, ctxT_ready) = (m[n] for n in names)
    SC = k.psum[:, 0:4, :]
    TB, QK, VB, OB = (k.psum[:, b, :] for b in range(4, 8))
    xnT = k.xqT if bf else k.xnT
    scale = 1.0 if bf else 0.25
    front_per = {ROPE: 3, SELF: 2, CROSS: 9}[kind]
    back_per = {ROPE: 3, SELF: 4, CROSS: 11}[kind]

    with nc.Block() as block:
        @block.gpsimd
        def _(pool):
            def tile(tf, sf, tb, sb):
                if tf is None:
                    return
                norm_rstd(k, nc, pool, tf, sf, stats_ready, rstd_ready)
            pipeline(pool, tile)

        @block.tensor
        def _(pe):
            def tile(tf, sf, tb, sb):
                if tf is not None:
                    pe.wait_ge(xn_ready, tf + 1)
                    if kind == SELF:
                        wait(pe, xnT_ready, tf)
                    else:
                        wait(pe, qkT_ready, tf)
                    for kc in range(KC):
                        last = nc.tensor.transpose(TB[:, kc * P:(kc + 1) * P], k.xn[sf][:, kc * P:(kc + 1) * P], k.ident[:, :])
                    if kind == CROSS:
                        pe.wait_ge(ctx_ready, tf + 1)
                        for kc in range(KC):
                            last = nc.tensor.transpose(TB[:, (2 + kc) * P:(3 + kc) * P], k.ctxs[sf][:, kc * P:(kc + 1) * P], k.ident[:, :])
                    last.then_inc(xT_turned, 1)
                if tb is not None:
                    pe.wait_ge(exp_done, tb + 1)
                    for p in range(PAIRS):
                        r, hh = p % 4, p // 4
                        c = sb * 256 + hh * P
                        last = nc.tensor.transpose(SC[:, r, c:c + P], k.probs[sb][:, (r * 2 + hh) * P:(r * 2 + hh + 1) * P], k.ident[:, :])
                    last.then_inc(pT_turned, 1)
                if tf is not None:
                    pe.wait_ge(xnT_ready, tf + 1)
                    wait(pe, qkT_ready if kind == SELF else q_ready, tf)
                    if kind == CROSS:
                        wait(pe, qk_ready, tf)
                    if kind == ROPE:
                        for kc in range(KC):
                            last = nc.tensor.matmul(QK[:, :], xnT[sf][:, kc, :], w["qk"][:, kc, :], start=kc == 0, stop=kc == KC - 1)
                    elif kind == SELF:
                        for c in range(4):
                            for kc in range(KC):
                                last = nc.tensor.matmul(QK[:, c * P:(c + 1) * P], w["qk"][:, kc, c * P:(c + 1) * P],
                                                        xnT[sf][:, kc, :], start=kc == 0, stop=kc == KC - 1)
                    else:
                        for kc in range(KC):
                            nc.tensor.matmul(QK[:, 0:D], xnT[sf][:, kc, :], w["q"][:, kc, :], start=kc == 0, stop=kc == KC - 1)
                        pe.wait_ge(ctxT_ready, tf + 1)
                        for c in range(2):
                            for kc in range(KC):
                                last = nc.tensor.matmul(QK[:, (2 + c) * P:(3 + c) * P], w["k"][:, kc, c * P:(c + 1) * P],
                                                        k.ctxT[sf][:, kc, :], start=kc == 0, stop=kc == KC - 1)
                    last.then_inc(qk_done, 1)
                    wait(pe, v_ready, tf)
                    src = k.ctxT[sf] if kind == CROSS else xnT[sf]
                    for kc in range(KC):
                        last = nc.tensor.matmul(VB[:, 0:D], src[:, kc, :], w["v"][:, kc, :], start=kc == 0, stop=kc == KC - 1)
                    last.then_inc(v_done, 1)
                if tb is not None:
                    pe.wait_ge(pT_ready, tb + 1)
                    pe.wait_ge(v_ready, tb + 1)
                    wait(pe, x_done, tb)
                    for p in range(PAIRS):
                        for b in range(2):
                            last = nc.tensor.matmul(OB[64 * b:64 * b + 64, 34 * p:34 * p + 34], k.pT[sb][:, p, 64 * b:64 * b + 64],
                                                    k.vblk[sb][:, b, p, :], start=True, stop=True)
                    last.then_inc(pv_done, 1)
                if tf is not None:
                    if kind != SELF:
                        pe.wait_ge(q_ready, tf + 1)
                        pe.wait_ge(ctxT_ready if kind == CROSS else xnT_ready, tf + 1)
                        for c in range(4 if kind == ROPE else 2):
                            last = nc.tensor.transpose(TB[:, c * P:(c + 1) * P], k.qk[sf][:, c * P:(c + 1) * P], k.ident[:, :])
                        last.then_inc(qkT_turned, 1)
                if tb is not None:
                    pe.wait_ge(on_ready, tb + 1)
                    for kc in range(KC):
                        last = nc.tensor.transpose(OB[:, kc * P:(kc + 1) * P], k.on[sb][:, kc * P:(kc + 1) * P], k.ident[:, :])
                    last.then_inc(oT_turned, 1)
                if tf is not None:
                    pe.wait_ge(kTm_ready, tf + 1)
                    pe.wait_ge(qkT_ready, tf + 1)
                    wait(pe, pT_ready, tf - 1)
                    for hh in range(2):
                        for r in range(4):
                            for b in range(2):
                                c = sf * 256 + hh * P
                                last = nc.tensor.matmul(
                                    SC[64 * b:64 * b + 64, r, c:c + P],
                                    k.qkT[sf][32 * r:32 * r + 32, hh, 64 * b:64 * b + 64],
                                    k.kTm[sf][32 * r:32 * r + 32, hh, :, 64 * b:64 * b + 64],
                                    start=True, stop=True)
                    last.then_inc(scores_done, 1)
                if tb is not None:
                    pe.wait_ge(oT_ready, tb + 1)
                    for kc in range(KC):
                        last = nc.tensor.matmul(OB[:, D:2 * D], (k.oTb if bf else k.oT)[sb][:, kc, :], w["o"][:, kc, :],
                                                start=kc == 0, stop=kc == KC - 1)
                    last.then_inc(y_done, 1)
            pipeline(pe, tile)

        @block.scalar
        def _(act):
            def tile(tf, sf, tb, sb):
                if tb is not None:
                    act.wait_ge(softmax_in, tb + 1)
                    nc.scalar.activation(k.probs[sb][:, :], k.probs[sb][:, :], ACT.Exp, scale=scale).then_inc(exp_done, 1)
                if tf is not None:
                    act.wait_ge(xT_turned, tf + 1)
                    wait(act, v_done, tf - 1)
                    ins = nc.scalar.activation(xnT[sf][:, :, :], TB[:, 0:D].rearrange("p (k n) -> p k n", n=P), ACT.Copy)
                    ins.then_inc(xnT_ready, 1)
                    if kind == CROSS:
                        nc.scalar.activation(k.ctxT[sf][:, :, :], TB[:, D:2 * D].rearrange("p (k n) -> p k n", n=P), ACT.Copy).then_inc(ctxT_ready, 1)
                if tb is not None:
                    act.wait_ge(pT_turned, tb + 1)
                    wait(act, pv_done, tb)
                    for hh in range(2):
                        c = sb * 256 + hh * P
                        ins = nc.scalar.activation(k.pT[sb][:, 4 * hh:4 * hh + 4, :], SC[:, :, c:c + P], ACT.Copy)
                    ins.then_inc(pT_ready, 1)
                if tf is not None:
                    if kind == ROPE:
                        act.wait_ge(v_done, tf + 1)
                        wait(act, pv_done, tf - 1)
                        for par in range(2):
                            for b in range(2):
                                ins = nc.scalar.activation(k.vblk[sf][64 * par:64 * par + 64, b, :, 16 * par:16 * par + 16],
                                                           VB[64 * b:64 * b + 64, 0:D].rearrange("k (p c d) -> k p c d", c=2, d=HD)[:, :, par, :],
                                                           ACT.Copy)
                        ins.then_inc(v_ready, 1)
                        act.wait_ge(qkT_turned, tf + 1)
                        wait(act, scores_done, tf - 1)
                        nc.scalar.activation(k.qkT[sf][:, :, :], TB[:, :].rearrange("p (c n) -> p c n", n=P), ACT.Copy).then_inc(qkT_ready, 1)
                    elif kind == SELF:
                        act.wait_ge(qk_done, tf + 1)
                        wait(act, scores_done, tf - 1)
                        for c in range(4):
                            ins = nc.scalar.activation(k.qkT[sf][:, c, :], QK[:, c * P:(c + 1) * P], ACT.Identity, bias=w["bqk"][:, c:c + 1])
                        ins.then_inc(qkT_ready, 1)
                    else:
                        act.wait_ge(q_ready, tf + 1)
                        wait(act, scores_done, tf - 1)
                        for c in range(2):
                            ins = nc.scalar.activation(k.qkT[sf][:, 2 + c, :], QK[:, (2 + c) * P:(3 + c) * P], ACT.Identity, bias=w["bk"][:, c:c + 1])
                        ins.then_inc(qk_ready, 1)
                        act.wait_ge(qkT_turned, tf + 1)
                        nc.scalar.activation(k.qkT[sf][:, 0:2, :], TB[:, 0:D].rearrange("p (c n) -> p c n", n=P), ACT.Copy, scale=0.25).then_inc(qkT_ready, 1)
                if tb is not None:
                    act.wait_ge(oT_turned, tb + 1)
                    wait(act, y_done, tb)
                    nc.scalar.activation((k.oTb if bf else k.oT)[sb][:, :, :], OB[:, 0:D].rearrange("p (k n) -> p k n", n=P), ACT.Copy).then_inc(oT_ready, 1)
            pipeline(act, tile)

        @block.vector
        def _(dve):
            def quantise(step, row, sx, scratch):
                step(nc.vector.tensor_reduce(scratch[:, 0:1], row, AX.X, ALU.max, apply_absolute_value=True))
                step(nc.vector.tensor_scalar(sx, scratch[:, 0:1], 1.0 / 127.0, Q_EPS, ALU.mult, ALU.max))
                step(nc.vector.reciprocal(scratch[:, 1:2], sx))
                step(nc.vector.tensor_scalar(row, row, scratch[:, 1:2], ROUND, ALU.mult, ALU.add))
                step(nc.vector.tensor_scalar(row, row, ROUND, 127.0, ALU.subtract, ALU.min))
                return nc.vector.tensor_scalar(row, row, -127.0, None, ALU.max)

            def tile(tf, sf, tb, sb):
                if tf is not None:
                    front = Steps(dve, front_steps, tf, front_per)
                    norm_moments(k, nc, front, tf, sf, stats_ready)
                    if kind == CROSS:
                        wait(dve, ctxT_ready, tf - 1)
                        nc.vector.tensor_scalar(k.ctxs[sf][:, :], k.ctx[:, tf, :], 1.0, None, ALU.mult).then_inc(ctx_ready, 1)
                if tb is not None:
                    back = Steps(dve, back_steps, tb, back_per)
                    dve.wait_ge(scores_done, tb + 1)
                    sc = SC[:, :, sb * 256:sb * 256 + 256].rearrange("p r (g n) -> p r g n", n=S)
                    pr = k.probs[sb][:, :].rearrange("p (r g n) -> p r g n", r=4, n=S)
                    msk = (k.mask[:, tb, :] if kind == CROSS else k.causal[:, :]).unsqueeze(1).unsqueeze(1).broadcast_to([P, 4, 4, S])
                    back(nc.vector.tensor_tensor(pr, sc, msk, ALU.add))
                    flat = k.probs[sb][:, :].rearrange("p (h n) -> p h n", n=S)
                    back(nc.vector.tensor_reduce(k.rowmax[:, sb, :], flat, AX.X, ALU.max))
                    nc.vector.tensor_tensor(flat, flat, k.rowmax[:, sb, :].unsqueeze(2).broadcast_to([P, H, S]), ALU.subtract).then_inc(softmax_in, 1)
                if tf is not None:
                    dve.wait_ge(rstd_ready, tf + 1)
                    wait(dve, xT_turned, tf - 1)
                    ins = nc.vector.tensor_scalar(k.xn[sf][:, :], k.x[:, tf, :], k.moments[:, sf, 0:1], k.rstd[:, sf, :],
                                                  ALU.subtract, ALU.mult)
                    if kind == CROSS:
                        front(ins)
                        ins = quantise(front, k.xn[sf][:, :], k.sx[:, sf, :], k.qscr)
                    ins.then_inc(xn_ready, 1)
                    if kind == ROPE:
                        dve.wait_ge(qk_done, tf + 1)
                        wait(dve, qkT_turned, tf - 1)
                        src = QK[:, :].rearrange("p (h f c) -> p h f c", f=HD // 2, c=2)
                        dst = k.rot[:, :].rearrange("p (h f c) -> p h f c", f=HD // 2, c=2)
                        cosv = k.rope[:, 0, :].unsqueeze(1).broadcast_to([P, 2 * H, HD])
                        sinv = k.rope[:, 1, :].rearrange("p (f c) -> p f c", c=2).unsqueeze(1).broadcast_to([P, 2 * H, HD // 2, 2])
                        nc.vector.tensor_tensor(k.qk[sf][:, :].rearrange("p (h f) -> p h f", f=HD),
                                                QK[:, :].rearrange("p (h f) -> p h f", f=HD), cosv, ALU.mult)
                        nc.vector.tensor_tensor(dst[:, :, :, 0], src[:, :, :, 1], sinv[:, :, :, 0], ALU.mult)
                        front(nc.vector.tensor_tensor(dst[:, :, :, 1], src[:, :, :, 0], sinv[:, :, :, 1], ALU.mult))
                        nc.vector.tensor_tensor(k.qk[sf][:, :], k.qk[sf][:, :], k.rot[:, :], ALU.add).then_inc(q_ready, 1)
                    elif kind == CROSS:
                        dve.wait_ge(qk_done, tf + 1)
                        wait(dve, qkT_turned, tf - 1)
                        q = k.qk[sf][:, 0:D]
                        front(nc.vector.scalar_tensor_tensor(q, QK[:, 0:D], k.sx[:, sf, :], w["swq"][:, :], ALU.mult, ALU.mult))
                        nc.vector.tensor_tensor(q, q, w["bq"][:, :], ALU.add).then_inc(q_ready, 1)
                    if kind != ROPE:
                        dve.wait_ge(v_done, tf + 1)
                        wait(dve, pv_done, tf - 1)
                        for par in range(2):
                            for b in range(2):
                                ins = nc.vector.tensor_tensor(
                                    k.vblk[sf][64 * par:64 * par + 64, b, :, 16 * par:16 * par + 16],
                                    VB[64 * b:64 * b + 64, 0:D].rearrange("k (p c d) -> k p c d", c=2, d=HD)[:, :, par, :],
                                    w["bv"][64 * b:64 * b + 64, :].rearrange("k (p c d) -> k p c d", c=2, d=HD)[:, :, par, :], ALU.add)
                        ins.then_inc(v_ready, 1)
                if tb is not None:
                    dve.wait_ge(pv_done, tb + 1)
                    ov = OB[:, 0:34 * PAIRS].rearrange("p (a c) -> p a c", c=34)
                    back(nc.vector.reciprocal(k.rsum[:, sb, :, :], ov[:, :, 32:34]))
                    ins = nc.vector.tensor_tensor(k.on[sb][:, :].rearrange("p (a c d) -> p a c d", c=2, d=HD),
                                                  ov[:, :, 0:32].rearrange("p a (c d) -> p a c d", d=HD),
                                                  k.rsum[:, sb, :, :].unsqueeze(3).broadcast_to([P, PAIRS, 2, HD]), ALU.mult)
                    if kind == CROSS:
                        back(ins)
                        ins = quantise(back, k.on[sb][:, :], k.so[:, sb, :], k.qscr)
                    ins.then_inc(on_ready, 1)
                if tf is not None:
                    dve.wait_ge(qkT_ready, tf + 1)
                    for par in range(2):
                        ins = nc.vector.tensor_scalar(k.kTm[sf][:, :, par, :], k.qkT[sf][:, 2:4, :], k.parity[:, par:par + 1], None, ALU.mult)
                    ins.then_inc(kTm_ready, 1)
                    front.end()
                if tb is not None:
                    dve.wait_ge(y_done, tb + 1)
                    y = OB[:, D:2 * D]
                    if kind == CROSS:
                        back(nc.vector.scalar_tensor_tensor(k.ytmp[:, :], y, k.so[:, sb, :], w["swo"][:, :], ALU.mult, ALU.mult))
                        y = k.ytmp[:, :]
                    if kind != ROPE:
                        back(nc.vector.tensor_tensor(k.ytmp[:, :], y, w["bo"][:, :], ALU.add))
                        y = k.ytmp[:, :]
                    nc.vector.tensor_tensor(k.x[:, tb, :], k.x[:, tb, :], y, ALU.add).then_inc(x_done, 1)
                    back.end()
            pipeline(dve, tile)



def pipeline3(eng, step):
    step(0, None, None, 0)
    step(1, 0, None, 1)
    step(2, 1, 0, 0)
    with eng.Fori(0, 2) as i:
        step(2 * i + 3, 2 * i + 2, 2 * i + 1, 1)
        step(2 * i + 4, 2 * i + 3, 2 * i + 2, 0)
    step(7, 6, 5, 1)
    step(None, 7, 6, 0)
    step(None, None, 7, 1)


def channel_attention(k):
    assert TILES == 8
    nc, sem = k.nc, k.sem
    names = ("stats_ready rstd_ready src_ready highs_ready rests_ready mids_ready lows_ready written0 written1 first_loaded0 first_loaded1 last_loaded0 last_loaded1 ctx_turned v_ready "
             "s_done max_ready negmax_parts mt_turned mrow_ready first_rows_in last_rows_in st_done exp_done pv_done xout_ready placed x_done "
             "front_steps part_steps back_steps ones_set sync_waits").split()
    (stats_ready, rstd_ready, src_ready, highs_ready, rests_ready, mids_ready, lows_ready, written0, written1, first_loaded0, first_loaded1, last_loaded0, last_loaded1, ctx_turned, v_ready,
     s_done, max_ready, negmax_parts, mt_turned, mrow_ready, first_rows_in, last_rows_in, st_done, exp_done, pv_done, xout_ready, placed, x_done,
     front_steps, part_steps, back_steps, ones_set, sync_waits) = (sem("c0_" + n) for n in names)
    written = [written0, written1]
    loaded = [[first_loaded0, first_loaded1], [last_loaded0, last_loaded1]]
    rows_in = [first_rows_in, last_rows_in]

    def nth(t, s, each):
        return (t - s) // 2 * each + each if isinstance(t, int) else t * (each // 2) + (each - s * (each // 2))
    SB = [k.psum[:, g, :].rearrange("p (c n) -> p c n", c=KC) for g in range(2)]
    ST = [k.psum[:, 2 + 2 * g:4 + 2 * g, :] for g in range(2)]
    OB, TB = k.psum[:, 6, :], k.psum[:, 7, :]
    MT = TB[:, 0:64].bitcast(BF16)
    GR = XP // XG
    HP = XP // 2
    SCALE = float(1.0 / np.sqrt(np.float32(XD)))
    scratch = [[nc.dram_tensor(f"scratch_{o}{s}", (3 * XD, XP, D), BF16).ap() for s in range(2)] for o in "qk"]
    operand = [k.qop, k.kop]

    with nc.Block() as block:
        @block.sync
        def _(sp):
            def hold(sem, value):
                sp.wait_ge(sem, value)
                sp.sem_inc(sync_waits, 1)

            def write(t, s):
                hold(lows_ready, t + 1)
                for o in range(2):
                    for j in range(3):
                        rows = slice(j * XD, (j + 1) * XD) if o == 0 else slice(j, 3 * XD, 3)
                        sp.dma_start(scratch[o][s][rows, :, :].rearrange("d a n -> a d n"), k.xpart[s][:, j, o, :]).then_inc(written[s], 16)

            def read(t, s, half):
                hold(written[s], nth(t, s, 96))
                cut = slice(half * HP, (half + 1) * HP)
                for o in range(2):
                    src = scratch[o][s].rearrange("r a n -> r (a n)")[:, half * HP * D:(half + 1) * HP * D].unsqueeze(1 - o)
                    src = src.broadcast_to([3 * XD, 3, HP * D] if o == 0 else [3, 3 * XD, HP * D])
                    sp.dma_start(operand[o][s][0:XR, cut, :], src).then_inc(loaded[half][s], 16)

            def rows(t, s, half):
                hold(mrow_ready, 2 * t + half + 1)
                for j in range(3):
                    dst = k.qop[s][XR + j:XR + j + 1, half * HP:(half + 1) * HP, :].rearrange("r a (c n) -> r (a c) n", c=KC)
                    sp.dma_start(dst, k.mrow[half][2 * HP * j:2 * HP * (j + 1), :]).then_inc(rows_in[half], 16)

            def step(tp, tf, tb, a):
                if tb is not None:
                    rows(tb, a, 1)
                if tp is not None:
                    write(tp, a)
                    if tb is not None:
                        hold(st_done, GR * tb + GR // 2)
                    else:
                        sp.wait_ge(ones_set, 1)
                    read(tp, a, 0)
                if tf is not None:
                    rows(tf, 1 - a, 0)
                if tp is not None:
                    if tb is not None:
                        hold(st_done, GR * tb + GR)
                    read(tp, a, 1)
            pipeline3(sp, step)

        @block.gpsimd
        def _(pool):
            def step(tp, tf, tb, a):
                if tp is None:
                    return
                norm_rstd(k, nc, pool, tp, a, stats_ready, rstd_ready)
                pool.wait_ge(highs_ready, tp + 1)
                nc.gpsimd.tensor_tensor(k.rest[:, :, :], k.xsrc[a][:, :, :], k.xpart[a][:, 0, :, :], ALU.subtract).then_inc(rests_ready, 1)
                pool.wait_ge(mids_ready, tp + 1)
                nc.gpsimd.tensor_tensor(k.xpart[a][:, 2, :, :], k.rest[:, :, :], k.xpart[a][:, 1, :, :], ALU.subtract).then_inc(lows_ready, 1)
            pipeline3(pool, step)

        @block.tensor
        def _(pe):
            def turn_max(t, half):
                pe.wait_ge(negmax_parts, 2 * t + half + 1)
                if half == 0:
                    wait(pe, mrow_ready, 2 * t)
                    wait(pe, x_done, t - 1)
                else:
                    pe.wait_ge(v_ready, t + 1)
                nc.tensor.transpose(MT[:, :], k.mpart[half][:, :, :].rearrange("p j m -> p (j m)"), k.identb[:, :]).then_inc(mt_turned, 1)

            def values(t, s, g):
                u = GR * t + g
                pe.wait_ge(exp_done, u + 1)
                if g == 0:
                    pe.wait_ge(v_ready, t + 1)
                if g % (GR // 2) == 0:
                    wait(pe, xout_ready, 2 * t + g // (GR // 2))
                for a in range(XG):
                    p = XG * g + a
                    b, c = p // 4 % 2, p % 4
                    for lc in range(KC):
                        last = nc.tensor.matmul(OB[XV * c:XV * (c + 1), b * D:(b + 1) * D], k.vT[s][:, lc, p, :],
                                                k.xprob[g % 2][:, a, lc, :], start=lc == 0, stop=lc == KC - 1)
                last.then_inc(pv_done, 1)

            def to_tokens(t):
                pe.wait_ge(xout_ready, 2 * t + 2)
                for b in range(4):
                    for o in range(2):
                        last = nc.tensor.matmul(TB[XV * b:XV * (b + 1), o * D:(o + 1) * D], k.place[:, o, :],
                                                k.xout[b // 2][:, (b % 2) * D:(b % 2 + 1) * D], start=True, stop=True)
                last.then_inc(placed, 1)

            def turn_context(t, s):
                pe.wait_ge(src_ready, t + 1)
                pe.wait_ge(mrow_ready, 2 * t + 1)
                for lc in range(KC):
                    last = nc.tensor.transpose(TB[:, (2 + lc) * P:(3 + lc) * P], k.xsrc[s][:, 1, lc * P:(lc + 1) * P], k.ident[:, :])
                last.then_inc(ctx_turned, 1)

            def step(tp, tf, tb, a):
                before = tb - 1 if tb is not None and not (isinstance(tb, int) and tb == 0) else None
                for g in range(GR):
                    if tb is not None:
                        if g == 1:
                            turn_max(tb, 1)
                        u = GR * tb + g
                        if g % (GR // 2) == 0:
                            pe.wait_ge(rows_in[g // (GR // 2)], 48 * tb + 48)
                        wait(pe, exp_done, u - 1)
                        for j in range(XG):
                            for lc in range(KC):
                                last = nc.tensor.matmul(ST[g % 2][:, j, lc * D:(lc + 1) * D], k.kop[a][0:XR + 3, XG * g + j, lc * P:(lc + 1) * P],
                                                        k.qop[a][0:XR + 3, XG * g + j, :], start=True, stop=True)
                        last.then_inc(st_done, 1)
                    if tf is not None:
                        if g % (GR // 2) == 0:
                            pe.wait_ge(loaded[g // (GR // 2)][1 - a], nth(tf, 1 - a, 32))
                        for j in range(XG):
                            p = XG * g + j
                            wait(pe, max_ready, XP * tf + p - 1)
                            for qc in range(KC):
                                last = nc.tensor.matmul(SB[p % 2][:, qc, :], k.qop[1 - a][0:XR, p, qc * P:(qc + 1) * P],
                                                        k.kop[1 - a][0:XR, p, :], start=True, stop=True)
                            last.then_inc(s_done, 1)
                        if g == 5:
                            turn_max(tf, 0)
                        if g == 6:
                            turn_context(tf, 1 - a)
                    if before is not None and g == 2:
                        pe.wait_ge(mrow_ready, 2 * tb + 2)
                        to_tokens(before)
                    if tb is not None and g >= 1:
                        values(tb, a, g - 1)
                if tb is not None:
                    values(tb, a, GR - 1)
            pipeline3(pe, step)
            pe.wait_ge(x_done, TILES - 1)
            to_tokens(TILES - 1)

        @block.scalar
        def _(act):
            def max_rows(t, half):
                act.wait_ge(mt_turned, 2 * t + half + 1)
                wait(act, rows_in[half], 48 * t)
                nc.scalar.activation(k.mrow[half][:, :], MT[0:6 * HP, :], ACT.Copy).then_inc(mrow_ready, 1)

            def turned_values(t, s):
                act.wait_ge(ctx_turned, t + 1)
                wait(act, pv_done, GR * (t - 1))
                nc.scalar.activation(k.vT[s][:, :, :, 0:XD], TB[:, D:2 * D].rearrange("p (c a d) -> p c a d", c=KC, d=XD), ACT.Copy).then_inc(v_ready, 1)

            def half_out(t, half):
                act.wait_ge(pv_done, GR * t + (half + 1) * GR // 2)
                wait(act, placed, t)
                nc.scalar.activation(k.xout[half], OB, ACT.Copy).then_inc(xout_ready, 1)

            def step(tp, tf, tb, a):
                if tp is not None:
                    act.wait_ge(src_ready, tp + 1)
                    wait(act, written[a], nth(tp, a, 96) - 96)
                    nc.scalar.activation(k.xpart[a][:, 0, :, :], k.xsrc[a][:, :, :], ACT.Copy).then_inc(highs_ready, 1)
                for g in range(GR):
                    if tb is not None:
                        u = GR * tb + g
                        act.wait_ge(st_done, u + 1)
                        wait(act, pv_done, u - 1)
                        nc.scalar.activation(k.xprob[g % 2][:, :, :, :], ST[g % 2], ACT.Exp, scale=SCALE).then_inc(exp_done, 1)
                        if g == 1:
                            max_rows(tb, 1)
                        if g == GR // 2:
                            half_out(tb, 0)
                    if tp is not None and g == 0:
                        act.wait_ge(rests_ready, tp + 1)
                        nc.scalar.activation(k.xpart[a][:, 1, :, :], k.rest[:, :, :], ACT.Copy).then_inc(mids_ready, 1)
                    if tf is not None and g == 5:
                        max_rows(tf, 0)
                    if tf is not None and g == 6:
                        turned_values(tf, 1 - a)
                if tb is not None:
                    half_out(tb, 1)
            pipeline3(act, step)

        @block.vector
        def _(dve):
            for s in range(2):
                nc.vector.memset(k.vT[s][:, :, :, XD:XD + 1], 1.0)
                nc.vector.memset(k.vT[s][:, :, :, XD + 1:], 0.0)
                nc.vector.memset(k.mpart[s][:, 3:, :], 0.0)
                ins = nc.vector.memset(k.kop[s][64:96, :, :], 1.0)
            ins.then_inc(ones_set, 1)

            def prepare(t, s):
                front = Steps(dve, front_steps, t, 2)
                norm_moments(k, nc, front, t, s, stats_ready)
                wait(dve, lows_ready, t - 1)
                wait(dve, ctx_turned, t - 1)
                nc.vector.tensor_scalar(k.xsrc[s][:, 1, :], k.ctx[:, t, :], 1.0, None, ALU.mult)
                dve.wait_ge(rstd_ready, t + 1)
                nc.vector.tensor_scalar(k.xsrc[s][:, 0, :], k.x[:, t, :], k.moments[:, s, 0:1], k.rstd[:, s, :],
                                        ALU.subtract, ALU.mult).then_inc(src_ready, 1)

            def split_max(t, half):
                own = Steps(dve, part_steps, 2 * t + half, 3)
                src = k.negmax[:, half * 2 * HP:(half + 1) * 2 * HP]
                dve.wait_ge(max_ready, XP * t + HP * (half + 1))
                wait(dve, mt_turned, 2 * t + half - 1)
                own(nc.vector.tensor_copy(k.mpart[half][:, 0, :], src))
                own(nc.vector.tensor_tensor(src, src, k.mpart[half][:, 0, :], ALU.subtract))
                own(nc.vector.tensor_copy(k.mpart[half][:, 1, :], src))
                nc.vector.tensor_tensor(k.mpart[half][:, 2, :], src, k.mpart[half][:, 1, :], ALU.subtract).then_inc(negmax_parts, 1)
                own.end()

            def add_out(t):
                back = Steps(dve, back_steps, t, 2)
                dve.wait_ge(placed, t + 1)
                back(nc.vector.reciprocal(k.ytmp[:, :], TB[:, D:2 * D]))
                back(nc.vector.scalar_tensor_tensor(k.ytmp[:, :], TB[:, 0:D], k.gamma[:, :], k.ytmp[:, :], ALU.mult, ALU.mult))
                nc.vector.tensor_tensor(k.x[:, t, :], k.x[:, t, :], k.ytmp[:, :], ALU.add).then_inc(x_done, 1)
                back.end()

            def step(tp, tf, tb, a):
                before = tb - 1 if tb is not None and not (isinstance(tb, int) and tb == 0) else None
                if tp is not None:
                    prepare(tp, a)
                if tf is not None:
                    for p in range(XP):
                        dve.wait_ge(s_done, XP * tf + p + 1)
                        nc.vector.tensor_reduce(k.negmax[:, 2 * p:2 * p + 2], SB[p % 2], AX.X, ALU.max, negate=True).then_inc(max_ready, 1)
                        if p % HP == HP - 1:
                            split_max(tf, p // HP)
                        if before is not None and p == 2 * XG + 1:
                            add_out(before)
                elif before is not None:
                    add_out(before)
            pipeline3(dve, step)
            add_out(TILES - 1)




def sparse_ffn(k, w):
    nc, sem = k.nc, k.sem
    names = ("stats_ready rstd_ready xn_ready xT_turned xnT_ready gate_done up_done silu_ready prod_ready abs_ready kept_ready "
             "down_done x_done front_steps unit_steps").split()
    (stats_ready, rstd_ready, xn_ready, xT_turned, xnT_ready, gate_done, up_done, silu_ready, prod_ready, abs_ready, kept_ready,
     down_done, x_done, front_steps, unit_steps) = (sem("f0_" + n) for n in names)
    G = [k.psum[:, g, :] for g in range(GB)]
    U = [k.psum[:, 2 + g, :] for g in range(GB)]
    TB, Y = k.psum[:, 4, :], k.psum[:, 5, 0:D]
    hid = [k.ffn_h[g][:, :, :] for g in range(GB)]
    mag = [k.ffn_a[g][:, :, :] for g in range(GB)]
    flat = [k.ffn_h[g][:, :, :].rearrange("p i n -> p (i n)") for g in range(GB)]

    with nc.Block() as block:
        @block.gpsimd
        def _(pool):
            def tile(tf, sf, tb, sb):
                if tf is not None:
                    norm_rstd(k, nc, pool, tf, sf, stats_ready, rstd_ready)
            pipeline(pool, tile)

        @block.tensor
        def _(pe):
            def gate_up(t, s, g):
                wait(pe, silu_ready, 2 * t + g - 1)
                for bank, wt, done in ((G[g], w["gate"], gate_done), (U[g], w["up"], up_done)):
                    if wt is w["up"]:
                        wait(pe, prod_ready, 2 * t + g - 1)
                    for i in range(PL):
                        for kc in range(KC):
                            last = nc.tensor.matmul(bank[:, i * P:(i + 1) * P], wt[:, kc, g * PL * P + i:(g + 1) * PL * P:PL],
                                                    k.xnT[s][:, kc, :], start=kc == 0, stop=kc == KC - 1)
                    last.then_inc(done, 1)

            def down(t, g):
                pe.wait_ge(kept_ready, 2 * t + g + 1)
                if g == 0:
                    wait(pe, x_done, t)
                for i in range(PL):
                    last = nc.tensor.matmul(Y, k.ffn_h[g][:, i, :], w["down"][:, g, i, :], start=g == 0 and i == 0, stop=g == GB - 1 and i == PL - 1)
                last.then_inc(down_done, 1)

            def tile(tf, sf, tb, sb):
                if tb is not None:
                    if isinstance(tb, int) and tb == 0:
                        pe.wait_ge(k.ffn_in, 3 * 16)
                    pe.wait_ge(xnT_ready, tb + 1)
                    gate_up(tb, sb, 0)
                    if not (isinstance(tb, int) and tb == 0):
                        down(tb - 1, 1)
                if tf is not None:
                    pe.wait_ge(xn_ready, tf + 1)
                    wait(pe, xnT_ready, tf)
                    for kc in range(KC):
                        last = nc.tensor.transpose(TB[:, kc * P:(kc + 1) * P], k.xn[sf][:, kc * P:(kc + 1) * P], k.ident[:, :])
                    last.then_inc(xT_turned, 1)
                if tb is not None:
                    gate_up(tb, sb, 1)
                    down(tb, 0)
            pipeline(pe, tile)
            down(TILES - 1, 1)

        @block.scalar
        def _(act):
            def unit(t, g):
                u = 2 * t + g
                act.wait_ge(gate_done, u + 1)
                wait(act, prod_ready, u - 1)
                nc.scalar.activation(k.ffn_s[g][:, :], G[g], ACT.Silu).then_inc(silu_ready, 1)

            def magnitude(t, g):
                u = 2 * t + g
                act.wait_ge(prod_ready, u + 1)
                wait(act, kept_ready, u - 1)
                nc.scalar.activation(mag[g], hid[g], ACT.Abs).then_inc(abs_ready, 1)

            def tile(tf, sf, tb, sb):
                if tf is not None:
                    act.wait_ge(xT_turned, tf + 1)
                    wait(act, up_done, 2 * tf - 2)
                    nc.scalar.activation(k.xnT[sf][:, :, :], TB[:, 0:D].rearrange("p (k n) -> p k n", n=P), ACT.Copy).then_inc(xnT_ready, 1)

            def whole(tf, sf, tb, sb):
                if tb is not None:
                    unit(tb, 0)
                    magnitude(tb, 0)
                tile(tf, sf, tb, sb)
                if tb is not None:
                    unit(tb, 1)
                    magnitude(tb, 1)
            pipeline(act, whole)

        @block.vector
        def _(dve):
            def unit(t, g):
                u = 2 * t + g
                own = Steps(dve, unit_steps, u, 3)
                dve.wait_ge(silu_ready, u + 1)
                dve.wait_ge(up_done, u + 1)
                wait(dve, down_done, u - 1)
                nc.vector.tensor_tensor(flat[g], k.ffn_s[g][:, :], U[g], ALU.mult).then_inc(prod_ready, 1)
                dve.wait_ge(abs_ready, u + 1)
                a = mag[g]
                nc.vector.tensor_tensor(k.near[:, :, :], a[:, 0:3, :], a[:, 1:4, :], ALU.is_ge)
                nc.vector.tensor_tensor(k.over[:, :, :], a[:, 0:2, :], a[:, 2:4, :], ALU.is_ge)
                own(nc.vector.tensor_tensor(k.far[:, :, :], a[:, 0:1, :], a[:, 3:4, :], ALU.is_ge))
                nc.vector.tensor_tensor(k.outer[:, :, :], k.near[:, 0:3:2, :], k.over[:, :, :], ALU.add)
                own(nc.vector.tensor_tensor(k.inner[:, :, :], k.over[:, :, :], k.near[:, 1:2, :].broadcast_to([P, 2, P]), ALU.add))
                nc.vector.tensor_tensor(k.outer[:, :, :], k.outer[:, :, :], k.far[:, :, :].broadcast_to([P, 2, P]), ALU.add)
                nc.vector.tensor_tensor(k.inner[:, 0, :], k.inner[:, 0, :], k.near[:, 2, :], ALU.subtract)
                own(nc.vector.tensor_tensor(k.inner[:, 1, :], k.inner[:, 1, :], k.near[:, 0, :], ALU.subtract))
                own.end()
                h = hid[g]
                nc.vector.scalar_tensor_tensor(h[:, 0, :], k.outer[:, 0, :], 1.5, h[:, 0, :], ALU.is_gt, ALU.mult)
                nc.vector.scalar_tensor_tensor(h[:, 1, :], k.inner[:, 1, :], 0.5, h[:, 1, :], ALU.is_gt, ALU.mult)
                nc.vector.scalar_tensor_tensor(h[:, 2, :], k.inner[:, 0, :], 0.5, h[:, 2, :], ALU.is_lt, ALU.mult)
                nc.vector.scalar_tensor_tensor(h[:, 3, :], k.outer[:, 1, :], 1.5, h[:, 3, :], ALU.is_lt, ALU.mult).then_inc(kept_ready, 1)

            def add_out(t):
                dve.wait_ge(down_done, 2 * t + 2)
                nc.vector.tensor_tensor(k.x[:, t, :], k.x[:, t, :], Y, ALU.add).then_inc(x_done, 1)

            def tile(tf, sf, tb, sb):
                if tf is not None:
                    front = Steps(dve, front_steps, tf, 2)
                    norm_moments(k, nc, front, tf, sf, stats_ready)
                    dve.wait_ge(rstd_ready, tf + 1)
                    wait(dve, xT_turned, tf - 1)
                    nc.vector.tensor_scalar(k.xn[sf][:, :], k.x[:, tf, :], k.moments[:, sf, 0:1], k.rstd[:, sf, :],
                                            ALU.subtract, ALU.mult).then_inc(xn_ready, 1)
                if tb is not None:
                    unit(tb, 0)
                    if not (isinstance(tb, int) and tb == 0):
                        add_out(tb - 1)
                    unit(tb, 1)
            pipeline(dve, tile)
            add_out(TILES - 1)




def expert_weights(k):
    nc = k.nc
    groups = []
    for u in range(2):
        for kc in range(KC):
            cut = slice(kc * P, (kc + 1) * P)
            for c in range(0, MC, 4):
                groups.append(([k.raw_gu[:, u, c + j, cut] for j in range(4)],
                               k.wgu[:, kc, u, c * P:(c + 4) * P].rearrange("p (j n) -> p j n", n=P)))
            groups.append(([k.raw_gu[0:EI, u, MC, cut]], k.wgu[:, kc, u, MC * P:MC * P + EI].unsqueeze(1)))
    for c in range(0, MC, 2):
        groups.append(([k.raw_d[:, nb, (c + j) * P:(c + j + 1) * P] for j in range(2) for nb in range(2)],
                       k.wd[:, c:c + 2, :].rearrange("p c (b n) -> p (c b) n", n=P)))
    groups.append(([k.raw_d[:, nb, MC * P:MC * P + EI] for nb in range(2)], k.wd[0:EI, MC, :].rearrange("p (b n) -> p b n", n=P)))
    groups.append(([k.raw_r[:, kc * P:(kc + 1) * P] for kc in range(KC)], k.wr[:, :, :]))
    transpose_weights(k, "w3", groups, (k.moe_in, k.moe_loads * 16))


def fetch_experts(k):
    with k.nc.Block() as block:
        @block.sync
        def _(sp):
            k.moe_loads = load_experts(k, sp)


def experts(k, out):
    nc, sem = k.nc, k.sem
    names = ("stats_ready rstd_ready xn_ready xT_turned xnT_ready xall_ready logits_done front_steps").split()
    (stats_ready, rstd_ready, xn_ready, xT_turned, xnT_ready, xall_ready, logits_done, front_steps) = (sem("m0_" + n) for n in names)
    TB, LB = k.psum[:, 4, :], k.psum[:, 5, 0:TILES * E]

    with nc.Block() as block:
        @block.gpsimd
        def _(pool):
            def tile(tf, sf, tb, sb):
                if tf is not None:
                    norm_rstd(k, nc, pool, tf, sf, stats_ready, rstd_ready)
            pipeline(pool, tile)

        @block.tensor
        def _(pe):
            def tile(tf, sf, tb, sb):
                if tf is not None:
                    pe.wait_ge(xn_ready, tf + 1)
                    wait(pe, xnT_ready, tf)
                    for kc in range(KC):
                        last = nc.tensor.transpose(TB[:, kc * P:(kc + 1) * P], k.xn[sf][:, kc * P:(kc + 1) * P], k.ident[:, :])
                    last.then_inc(xT_turned, 1)
                if tb is not None:
                    pe.wait_ge(xnT_ready, tb + 1)
                    for kc in range(KC):
                        last = nc.tensor.matmul(LB[:, bass.ds(tb * E, E)], k.xnT[sb][:, kc, :], k.wr[:, kc, :],
                                                start=kc == 0, stop=kc == KC - 1)
                    last.then_inc(logits_done, 1)
            pipeline(pe, tile)

        @block.scalar
        def _(act):
            def tile(tf, sf, tb, sb):
                if tf is not None:
                    act.wait_ge(xT_turned, tf + 1)
                    wait(act, logits_done, tf - 1)
                    wait(act, xall_ready, tf - 1)
                    nc.scalar.activation(k.xnT[sf][:, :, :], TB[:, 0:D].rearrange("p (k n) -> p k n", n=P), ACT.Copy).then_inc(xnT_ready, 1)
            pipeline(act, tile)

        @block.vector
        def _(dve):
            def tile(tf, sf, tb, sb):
                if tf is not None:
                    front = Steps(dve, front_steps, tf, 2)
                    norm_moments(k, nc, front, tf, sf, stats_ready)
                    dve.wait_ge(rstd_ready, tf + 1)
                    wait(dve, xT_turned, tf - 1)
                    nc.vector.tensor_scalar(k.xn[sf][:, :], k.x[:, tf, :], k.moments[:, sf, 0:1], k.rstd[:, sf, :],
                                            ALU.subtract, ALU.mult).then_inc(xn_ready, 1)
                if tb is not None:
                    dve.wait_ge(xnT_ready, tb + 1)
                    nc.vector.tensor_scalar(k.xall[:, :, tb, :], k.xnT[sb][:, :, :], 1.0, None, ALU.mult).then_inc(xall_ready, 1)
            pipeline(dve, tile)

    route(k)

    names = "gate_done up_done comb_done silu_ready hid_ready down_done x_done prod_done stored".split()
    (gate_done, up_done, comb_done, silu_ready, hid_ready, down_done, x_done, prod_done, stored) = (sem("m2_" + n) for n in names)
    G = [k.psum[:, g, :] for g in range(2)]
    U = [k.psum[:, 2 + g, :] for g in range(2)]
    C = [k.psum[:, 4 + g, :] for g in range(2)]
    Y = [k.psum[:, 6 + g, 0:D] for g in range(2)]
    rows = [P] * MC + [EI]
    tok = HALF * P

    with nc.Block() as block:
        @block.tensor
        def _(pe):
            def half(v):
                for c in range(MCS):
                    n, g = rows[c], c % 2
                    units = v * MCS + c
                    cols = slice(c * P, c * P + n)
                    xs = k.xall[:, :, :, :].rearrange("p k t n -> p k (t n)")
                    wait(pe, silu_ready, units - 1)
                    for kc in range(KC):
                        last = nc.tensor.matmul(G[g][0:n, :], k.wgu[:, kc, 0, cols], xs[:, kc, bass.ds(v * tok, tok)], start=kc == 0, stop=kc == KC - 1)
                    last.then_inc(gate_done, 1)
                    wait(pe, hid_ready, units - 1)
                    for kc in range(KC):
                        last = nc.tensor.matmul(U[g][0:n, :], k.wgu[:, kc, 1, cols], xs[:, kc, bass.ds(v * tok, tok)], start=kc == 0, stop=kc == KC - 1)
                    last.then_inc(up_done, 1)
                    if c < MC:
                        nc.tensor.matmul(C[g], k.expert[:, cols], k.combT[:, bass.ds(v * tok, tok)], start=True, stop=True).then_inc(comb_done, 1)
                for j in range(HALF):
                    pe.wait_ge(hid_ready, v * MCS + MCS)
                    wait(pe, x_done, v * HALF + j - 1)
                    for c in range(MCS):
                        last = nc.tensor.matmul(Y[j % 2], k.hid[0:rows[c], c, j * P:(j + 1) * P], k.wd[0:rows[c], c, :], start=c == 0, stop=c == MCS - 1)
                    last.then_inc(down_done, 1)
            for v in range(TILES // HALF):
                half(v)

        @block.scalar
        def _(act):
            def half(v):
                for c in range(MCS):
                    n, g = rows[c], c % 2
                    units = v * MCS + c
                    act.wait_ge(gate_done, units + 1)
                    wait(act, prod_done, units - 1)
                    nc.scalar.activation(k.sg[g][0:n, :], G[g][0:n, :], ACT.Silu).then_inc(silu_ready, 1)
            for v in range(TILES // HALF):
                half(v)

        @block.vector
        def _(dve):
            def half(v):
                for c in range(MCS):
                    n, g = rows[c], c % 2
                    units = v * MCS + c
                    dve.wait_ge(silu_ready, units + 1)
                    dve.wait_ge(up_done, units + 1)
                    wait(dve, down_done, v * HALF)
                    ins = nc.vector.tensor_tensor(k.hid[0:n, c, :], k.sg[g][0:n, :], U[g][0:n, :], ALU.mult).then_inc(prod_done, 1)
                    dve.wait_ge(prod_done, units + 1)
                    if c < MC:
                        dve.wait_ge(comb_done, v * MC + c + 1)
                        nc.vector.tensor_tensor(k.hid[:, c, :], k.hid[:, c, :], C[g], ALU.mult).then_inc(hid_ready, 1)
                    else:
                        nc.vector.memset(k.pause[:, :], 0.0).then_inc(hid_ready, 1)
                for j in range(HALF):
                    t = v * HALF + j
                    dve.wait_ge(down_done, t + 1)
                    nc.vector.tensor_tensor(k.x[:, t, :], k.x[:, t, :], Y[j % 2], ALU.add).then_inc(x_done, 1)
            for v in range(TILES // HALF):
                half(v)

        @block.sync
        def _(sp):
            for t in range(TILES):
                sp.wait_ge(x_done, t + 1)
                sp.dma_start(tiles_of(out)[:, t, :], k.x[:, t, :]).then_inc(stored, 16)
            sp.wait_ge(stored, TILES * 16)


def route(k):
    nc, sem = k.nc, k.sem
    scored, parted, turned, own_steps, copied = (sem("r_" + n) for n in "scored parted turned own_steps copied".split())
    LB, CB = k.psum[:, 5, 0:TILES * E], k.psum[0:3 * E, 6, :].bitcast(BF16)
    with nc.Block() as block:
        @block.scalar
        def _(act):
            nc.scalar.activation(k.score[:, :], LB, ACT.Sigmoid).then_inc(scored, 1)

        @block.vector
        def _(dve):
            own = Steps(dve, own_steps, 0, 13)
            score = k.score[:, :].rearrange("p (t e) -> p t e", e=E)
            pick = k.pick[:, :].rearrange("p (t e) -> p t e", e=E)
            dve.wait_ge(scored, 1)
            own(nc.vector.tensor_tensor(pick, score, k.ebias[:, :].unsqueeze(1).broadcast_to([P, TILES, E]), ALU.add))
            for t in range(TILES):
                ins = nc.vector.max(k.best[:, t, :], pick[:, t, :])
            own(ins)
            for t in range(TILES):
                ins = nc.vector.max_index(k.besti[:, t, :], k.best[:, t, :], pick[:, t, :])
            own(ins)
            own(nc.vector.tensor_copy(k.bestf[:, :, :], k.besti[:, :, 0:TOPK]))
            own(nc.vector.tensor_tensor(k.hit[:, :, :, :], k.bestf[:, :, :].unsqueeze(3).broadcast_to([P, TILES, TOPK, E]),
                                        k.iota[:, :].unsqueeze(1).unsqueeze(1).broadcast_to([P, TILES, TOPK, E]), ALU.is_equal))
            own(nc.vector.tensor_reduce(pick, k.hit[:, :, :, :].rearrange("p t r e -> p t e r"), AX.X, ALU.add))
            own(nc.vector.tensor_tensor(k.pick[:, :], k.pick[:, :], k.score[:, :], ALU.mult))
            own(nc.vector.tensor_reduce(k.wsum[:, :, 0], pick, AX.X, ALU.add))
            own(nc.vector.tensor_scalar(k.wsum[:, :, 0], k.wsum[:, :, 0], 1e-20, None, ALU.add))
            own(nc.vector.reciprocal(k.wsum[:, :, 1], k.wsum[:, :, 0]))
            own(nc.vector.tensor_tensor(pick, pick, k.wsum[:, :, 1:2].broadcast_to([P, TILES, E]), ALU.mult))
            parts = k.parts[:, :, :, :]
            nc.vector.tensor_copy(parts[:, :, 0, :], pick).then_inc(own_steps, 1)
            own.n += 1
            dve.wait_ge(own_steps, own.n)
            own(nc.vector.tensor_tensor(pick, pick, parts[:, :, 0, :], ALU.subtract))
            own.end()
            nc.vector.tensor_copy(parts[:, :, 1, :], pick).then_inc(parted, 1)
            dve.wait_ge(parted, 1)
            nc.vector.tensor_tensor(parts[:, :, 2, :], pick, parts[:, :, 1, :], ALU.subtract).then_inc(parted, 1)

            dve.wait_ge(turned, 1)
            nc.vector.tensor_copy(k.combT[:, :], CB[:, :]).then_inc(copied, 1)

        @block.tensor
        def _(pe):
            pe.wait_ge(parted, 2)
            for t in range(TILES):
                last = nc.tensor.transpose(CB[:, t * P:(t + 1) * P], k.parts[:, t, :, :].rearrange("p s e -> p (s e)"), k.identb[:, :])
            last.then_inc(turned, 1)


def tiles_of(ap):
    return ap.rearrange("b s n -> (b s) n").rearrange("(t p) n -> p t n", p=P)


def rows_of(ap):
    return ap.rearrange("(j p) n -> p j n", p=P)


ATT_RAW = ("L0_attn_Wq", "L0_attn_Wk", "L0_attn_Wv", "L0_attn_Wo", "L1_attn_Wq", "L1_attn_Wk", "L1_attn_Wv", "L1_attn_Wo",
           "L1_xattn_wq", "L1_xattn_wk", "L1_xattn_wv", "L1_xattn_wo")


def load_experts(k, sp):
    d, loads = k.dram, 0
    for u in range(2):
        for f in range(4):
            i = 0
            while i < EI:
                row = EI * f + i
                n = min(EI - i, P - row % P)
                src = d["L1_ffn_gate_up_proj"][:, u * EI + i:u * EI + i + n, :].rearrange("(g f) i n -> f i g n", f=4)[f]
                sp.dma_start(k.raw_gu[row % P:row % P + n, u, row // P:MC:3, :], src).then_inc(k.moe_in, 16)
                loads += 1
                i += n
    for u, n in enumerate(("L1_ffn_shared_gate_w", "L1_ffn_shared_up_w")):
        sp.dma_start(k.raw_gu[0:EI, u, MC, :], d[n]).then_inc(k.moe_in, 16)
    for nb in range(KC):
        sp.dma_start(k.raw_d[:, nb, 0:MC * P].rearrange("p (e i) -> p e i", i=EI),
                     d["L1_ffn_down_proj"][:, nb * P:(nb + 1) * P, :].rearrange("e p i -> p e i")).then_inc(k.moe_in, 16)
    sp.dma_start(k.raw_d[:, :, MC * P:], rows_of(d["L1_ffn_shared_down_w"])).then_inc(k.moe_in, 16)
    sp.dma_start(k.raw_r[:, :], d["L1_ffn_router_w"]).then_inc(k.moe_in, 16)
    sp.dma_start(k.ebias[:, :], d["L1_ffn_e_bias"].partition_broadcast(P)).then_inc(k.moe_in, 16)
    sp.dma_start(k.iota[:, :], d["c_iota"]).then_inc(k.moe_in, 16)
    sp.dma_start(k.expert[:, :], d["c_expert"]).then_inc(k.moe_in, 16)
    return loads + 2 + KC + 5


def setup(k):
    nc, d = k.nc, k.dram
    k.raw = {n: k.raw_first[:, i] for i, n in enumerate(ATT_RAW[0:4])}
    k.raw.update({n: k.raw_att[:, i] for i, n in enumerate(ATT_RAW[4:])})
    k.w1_bqk, k.w1_bv, k.w1_bo = k.sb("w1_bqk", [P, 4]), k.sb("w1_bv", [P, D]), k.sb("w1_bo", [P, D])
    k.w2_bq, k.w2_bk, k.w2_bv, k.w2_bo = k.sb("w2_bq", [P, D]), k.sb("w2_bk", [P, 2]), k.sb("w2_bv", [P, D]), k.sb("w2_bo", [P, D])
    k.bias_in, k.ffn_in, k.moe_in = k.sem("bias_in"), k.sem("ffn_in"), k.sem("moe_in")
    k.first_in, k.ctx_in, k.att_in, k.made = k.sem("first_in"), k.sem("ctx_in"), k.sem("att_in"), k.sem("made")
    with nc.Block() as block:
        @block.sync
        def _(sp):
            for n in ATT_RAW[0:4]:
                sp.dma_start(k.raw[n][:, :, :], rows_of(d[n])).then_inc(k.first_in, 16)
            sp.dma_start(k.ident[:, :], d["c_ident"]).then_inc(k.first_in, 16)
            sp.dma_start(k.x[:, :, :], tiles_of(d["x"])).then_inc(k.first_in, 16)
            sp.dma_start(k.rope[:, :, :], d["c_rope"].rearrange("p (a f) -> p a f", a=2)).then_inc(k.first_in, 16)
            sp.dma_start(k.causal[:, :], d["c_causal"]).then_inc(k.first_in, 16)
            sp.dma_start(k.parity[:, :], d["c_parity"]).then_inc(k.first_in, 16)
            sp.dma_start(k.ctx[:, :, :], tiles_of(d["ctx_2048"])).then_inc(k.ctx_in, 16)
            sp.dma_start(k.place[:, :, :], d["c_place"].rearrange("p (a n) -> p a n", a=2)).then_inc(k.ctx_in, 16)
            sp.dma_start(k.mask[:, :, :], tiles_of(d["mask_BxSxS2_ff0"])).then_inc(k.ctx_in, 16)
            for n in ATT_RAW[4:]:
                sp.dma_start(k.raw[n][:, :, :], rows_of(d[n])).then_inc(k.att_in, 16)
            for buf, n in ((k.w1_bv, "L1_attn_bv"), (k.w1_bo, "L1_attn_bo"), (k.w2_bq, "L1_xattn_bq"), (k.w2_bv, "L1_xattn_bv"), (k.w2_bo, "L1_xattn_bo"), (k.gamma, "L0_xattn_gamma")):
                sp.dma_start(buf[:, :], d[n].partition_broadcast(P)).then_inc(k.bias_in, 16)
            with nc.allow_non_contiguous_dma(reason="256 biases, one to a partition"):
                for buf, n in ((k.w1_bqk[:, 0:2], "L1_attn_bq"), (k.w1_bqk[:, 2:4], "L1_attn_bk"), (k.w2_bk[:, :], "L1_xattn_bk")):
                    sp.dma_start(buf, d[n].rearrange("(c p) -> p c", p=P)).then_inc(k.bias_in, 16)
            for n, i in (("L0_ffn_w_gate", "gate"), ("L0_ffn_w_up", "up")):
                sp.dma_start(k.w_ffn[i], rows_of(d[n])).then_inc(k.ffn_in, 16)
            sp.dma_start(k.w_ffn["down"].rearrange("p g i n -> p g (i n)"),
                         d["L0_ffn_w_down"].rearrange("(g p i) n -> p g (i n)", g=GB, i=PL)).then_inc(k.ffn_in, 16)
            sp.wait_ge(k.first_in, 9 * 16)
            sp.wait_ge(k.ctx_in, 3 * 16)
            sp.wait_ge(k.bias_in, 9 * 16)

        @block.vector
        def _(dve):
            nc.vector.memset(k.halfpow[:, :], -0.5)
            nc.vector.memset(k.ones[:, :], 1.0)
            for s in range(2):
                ins = nc.vector.memset(k.vblk[s][:, :, :, :], 0.0)
            ins.then_inc(k.made, 1)
            dve.wait_ge(k.made, 1)
            for s in range(2):
                nc.vector.memset(k.vblk[s][0:64, :, :, 32:33], 1.0)
                nc.vector.memset(k.vblk[s][64:128, :, :, 33:34], 1.0)
            dve.wait_ge(k.first_in, 9 * 16)
            nc.vector.tensor_copy(k.identb[:, :], k.ident[:, :])


def quantise_weights(k, raws, scales):
    nc = k.nc
    steps_done, diag_ready, spread_done = (k.sem("wq_" + n) for n in "steps_done diag_ready spread_done".split())
    with nc.Block() as block:
        @block.vector
        def _(dve):
            dve.wait_ge(k.att_in, 8 * 16)
            own = Steps(dve, steps_done, 0, 7)
            for i, raw in enumerate(raws):
                nc.vector.tensor_reduce(k.wabs[:, 2 * i:2 * i + 2], raw[:, :, :], AX.X, ALU.max, apply_absolute_value=True)
            n = 2 * len(raws)
            own(nc.vector.memset(k.pause[:, :], 0.0))
            own(nc.vector.tensor_scalar(k.wscale[:, 0:n], k.wabs[:, 0:n], 1.0 / 127.0, Q_EPS, ALU.mult, ALU.max))
            own(nc.vector.reciprocal(k.wabs[:, 0:n], k.wscale[:, 0:n]))
            for first, last, op0, op1 in ((None, ROUND, ALU.mult, ALU.add), (ROUND, 127.0, ALU.subtract, ALU.min), (-127.0, None, ALU.max, None)):
                for i, raw in enumerate(raws):
                    for j in range(KC):
                        row = raw[:, j, :]
                        by = k.wabs[:, 2 * i + j:2 * i + j + 1] if first is None else first
                        ins = nc.vector.tensor_scalar(row, row, by, last, op0, *([op1] if op1 else []))
                own(ins)
            for i in range(n):
                ins = nc.vector.tensor_scalar(k.diag[:, i, :], k.ident[:, :], k.wscale[:, i:i + 1], None, ALU.mult)
            ins.then_inc(diag_ready, 1)
            dve.wait_ge(spread_done, 1)
            for i, scale in enumerate(scales):
                ins = nc.vector.tensor_copy(scale[:, :], k.psum[:, i, 0:D])
            own(ins)
            own.end()

        @block.tensor
        def _(pe):
            pe.wait_ge(diag_ready, 1)
            for i in range(2 * len(raws)):
                last = nc.tensor.matmul(k.psum[:, i // 2, (i % 2) * P:(i % 2 + 1) * P], k.ones[:, :], k.diag[:, i, :], start=True, stop=True)
            last.then_inc(spread_done, 1)


def attention_weights(k, w0):
    nc, d, raw, sb = k.nc, k.dram, k.raw, k.sb
    w1 = {"qk": w0["qk"], "v": w0["v"], "o": w0["o"], "bqk": k.w1_bqk, "bv": k.w1_bv, "bo": k.w1_bo}
    w2 = {"q": sb("w2_q", [P, KC, D], BF16), "k": sb("w2_k", [P, KC, D]), "v": sb("w2_v", [P, KC, D]), "o": sb("w2_o", [P, KC, D], BF16),
          "swq": sb("w2_swq", [P, D]), "swo": sb("w2_swo", [P, D]), "bq": k.w2_bq, "bk": k.w2_bk, "bv": k.w2_bv, "bo": k.w2_bo}
    k.wabs, k.wscale, k.diag = sb("wabs", [P, 4]), sb("wscale", [P, 4]), sb("diag", [P, 4, P])
    quantise_weights(k, [raw["L1_xattn_wq"], raw["L1_xattn_wo"]], [w2["swq"], w2["swo"]])
    groups = []
    for n, dst in (("L1_attn_Wq", w1["qk"][:, :, 0:D]), ("L1_attn_Wk", w1["qk"][:, :, D:2 * D]), ("L1_attn_Wv", w1["v"]), ("L1_attn_Wo", w1["o"]),
                   ("L1_xattn_wq", w2["q"]), ("L1_xattn_wk", w2["k"]), ("L1_xattn_wv", w2["v"]), ("L1_xattn_wo", w2["o"])):
        groups += square_groups(raw[n], dst)
    transpose_weights(k, "w1", groups)
    return w1, w2


def decoder(nc, dram, out, layers="012345"):
    ctx = ExitStack()
    with ctx:
        k = allocate(nc, ctx, dram)
        setup(k)
        w0 = {"qk": k.sb("w0_qk", [P, KC, 2 * D]), "v": k.sb("w0_v", [P, KC, D]), "o": k.sb("w0_o", [P, KC, D])}
        raw = k.raw
        if "0" in layers:
            transpose_weights(k, "w0", square_groups(raw["L0_attn_Wq"], w0["qk"][:, :, 0:D]) + square_groups(raw["L0_attn_Wk"], w0["qk"][:, :, D:2 * D])
                              + square_groups(raw["L0_attn_Wv"], w0["v"]) + square_groups(raw["L0_attn_Wo"], w0["o"]))
            attention(k, "a0", ROPE, w0)
        if "1" in layers:
            channel_attention(k)
        if "2" in layers:
            sparse_ffn(k, k.w_ffn)
        if "3" in layers:
            release(k, "c0")
            w1, w2 = attention_weights(k, w0)
        fetch_experts(k)
        if "3" in layers:
            attention(k, "a1", SELF, w1)
            attention(k, "a2", CROSS, w2)
        expert_weights(k)
        experts(k, out)



LAYERS = "012345"
_INS = ['x', 'ctx_2048', 'mask_BxSxS2_ff0', 'L0_attn_Wq', 'L0_attn_Wk', 'L0_attn_Wv', 'L0_attn_Wo', 'L0_xattn_gamma',
        'L0_ffn_w_gate', 'L0_ffn_w_up', 'L0_ffn_w_down', 'L1_attn_Wq', 'L1_attn_bq', 'L1_attn_Wk', 'L1_attn_bk',
        'L1_attn_Wv', 'L1_attn_bv', 'L1_attn_Wo', 'L1_attn_bo', 'L1_xattn_wq', 'L1_xattn_bq', 'L1_xattn_wk',
        'L1_xattn_bk', 'L1_xattn_wv', 'L1_xattn_bv', 'L1_xattn_wo', 'L1_xattn_bo', 'L1_ffn_router_w', 'L1_ffn_e_bias',
        'L1_ffn_gate_up_proj', 'L1_ffn_down_proj', 'L1_ffn_shared_gate_w', 'L1_ffn_shared_up_w', 'L1_ffn_shared_down_w']


def kernel(**inputs):
    import concourse.bacc as bacc
    from concourse.bass_utils import run_bass_kernel_spmd as run

    nc = bacc.Bacc("TRN2", target_bir_lowering=False, num_devices=1)
    arrays, dram = {}, {}
    for name, a in {**{n: inputs[n] for n in _INS}, **constants()}.items():
        a = np.ascontiguousarray(a)
        arrays[name + "_dram"] = a
        dram[name] = nc.dram_tensor(name + "_dram", a.shape, mybir.dt.from_np(a.dtype), kind="ExternalInput").ap()
    out = nc.dram_tensor("out_dram", (B, S, D), F32, kind="ExternalOutput").ap()
    decoder(nc, dram, out, LAYERS)
    return run(nc, [arrays], core_ids=[0]).results[0]["out_dram"]
```

```python
import numpy as np
import concourse.bass as bass
from concourse import mybir
from contextlib import ExitStack

F32 = mybir.dt.float32
BF16 = mybir.dt.bfloat16
U32 = mybir.dt.uint32
ALU = mybir.AluOpType
ACT = mybir.ActivationFunctionType
AX = mybir.AxisListType

P = 128
B, S, D = 16, 64, 256
TILES = B * S // P
KC = D // P
H, HD = 16, 16
PAIRS = H // 2
NEG = -1e30
LN_EPS = 1e-5
Q_EPS = 1e-8
ROUND = 1.5 * 2.0 ** 23
XH, XD = 8, 8
XP = P // XD
XG = 2
XV = 32
XC = 4 * XD + 4
XR = 9 * XD
I0 = 1024
E, EI, TOPK = 16, 96, 4
PL = 4
GB = I0 // (PL * P)
HALF = 4
MC = E * EI // P
MCS = MC + 1


def constants():
    pos = np.arange(S, dtype=np.float32)
    inv = (1.0 / np.float32(10000.0) ** (np.arange(0, HD, 2, dtype=np.float32) / np.float32(HD))).astype(np.float32)
    ang = np.outer(pos, inv).astype(np.float32)
    cos, sin = np.cos(ang).astype(np.float32), np.sin(ang).astype(np.float32)
    cs = np.stack([cos, cos], -1).reshape(S, HD)
    sn = np.stack([-sin, sin], -1).reshape(S, HD)
    causal = np.where(np.tril(np.ones((S, S), bool)), 0.0, NEG).astype(np.float32)
    head = np.arange(P) // HD
    unit = np.arange(MC * P) // EI
    row, token, pair = np.arange(P)[:, None], np.arange(4 * XD)[None, :], np.arange(4)[None, :]
    place = (row // XV == token // XD) & (row % XV == token % XD)
    total = (row // XV == pair) & (row % XV == XD)
    return {
        "c_ident": np.eye(P, dtype=np.float32),
        "c_rope": np.tile(np.concatenate([cs, sn], 1), (2, 1)).astype(np.float32),
        "c_causal": np.tile(causal, (2, 1)),
        "c_parity": np.stack([head % 2 == 0, head % 2 == 1], 1).astype(np.float32),
        "c_place": np.concatenate([place, total], 1).astype(np.float32),
        "c_iota": np.tile(np.arange(E, dtype=np.float32), (P, 1)),
        "c_expert": np.tile(unit[None, :] == np.arange(E)[:, None], (3, 1)).astype("bfloat16"),
    }


class Kit:
    pass


def allocate(nc, ctx, dram):
    k = Kit()
    k.nc, k.dram = nc, dram

    def sb(name, shape, dt=F32):
        return ctx.enter_context(nc.sbuf_tensor(name, shape, dt))

    k.layer_sems = {}

    def sem(name):
        handle = nc.alloc_semaphore(name=name)
        k.layer_sems.setdefault(name.split("_")[0], []).append(handle)
        return handle

    k.sb, k.sem = sb, sem
    k.x = sb("x", [P, TILES, D])
    k.ctx = sb("ctx", [P, TILES, D])
    k.ident = sb("ident", [P, P])
    k.identb = sb("identb", [P, P], BF16)
    k.rope = sb("rope", [P, 2, HD])
    k.causal = sb("causal", [P, S])
    k.parity = sb("parity", [P, 2])
    k.halfpow = sb("halfpow", [P, 1])
    k.zero = sb("zero", [P, 1])
    k.ones = sb("ones", [P, P])
    k.psum = ctx.enter_context(nc.psum_tensor("psum", [P, 8, 512], F32))
    k.stats = sb("stats", [P, 2, 6])
    k.moments = sb("moments", [P, 2, 2])
    k.varplus = sb("varplus", [P, 2, 1])
    k.pause = sb("pause", [P, 1])
    k.unround = sb("unround", [P, 1])
    k.rstd = sb("rstd", [P, 2, 1])
    k.xn = [sb(f"xn{s}", [P, D]) for s in range(2)]
    k.xnT = [sb(f"xnT{s}", [P, KC, P]) for s in range(2)]
    k.xqT = [sb(f"xqT{s}", [P, KC, P], BF16) for s in range(2)]
    k.ctxs = [sb(f"ctxs{s}", [P, D]) for s in range(2)]
    k.ctxT = [sb(f"ctxT{s}", [P, KC, P]) for s in range(2)]
    k.qk = [sb(f"qk{s}", [P, 2 * D]) for s in range(2)]
    k.qkT = [sb(f"qkT{s}", [P, 4, P]) for s in range(2)]
    k.kTm = [sb(f"kTm{s}", [P, 2, 2, P]) for s in range(2)]
    k.probs = [sb(f"probs{s}", [P, H * S]) for s in range(2)]
    k.pT = [sb(f"pT{s}", [P, PAIRS, P]) for s in range(2)]
    k.vblk = [sb(f"vblk{s}", [P, 2, PAIRS, 34]) for s in range(2)]
    k.on = [sb(f"on{s}", [P, D]) for s in range(2)]
    k.oT = [sb(f"oT{s}", [P, KC, P]) for s in range(2)]
    k.oTb = [sb(f"oTb{s}", [P, KC, P], BF16) for s in range(2)]
    k.rot = sb("rot", [P, 2 * D])
    k.ytmp = sb("ytmp", [P, D])
    k.rowmax = sb("rowmax", [P, 2, H])
    k.rsum = sb("rsum", [P, 2, PAIRS, 2])
    k.qscr = sb("qscr", [P, 2])
    k.sx = sb("sx", [P, 2, 1])
    k.so = sb("so", [P, 2, 1])
    k.mask = sb("mask", [P, TILES, S])
    k.gamma = sb("gamma", [P, 1])
    k.xsrc = [k.qkT[s][:, :, :].rearrange("p (a b) n -> p a (b n)", a=2) for s in range(2)]
    k.xpart = [sb(f"xpart{s}", [P, 3, 2, D], BF16) for s in range(2)]
    k.rest = k.rot[:, :].rearrange("p (a n) -> p a n", a=2)
    k.vT = [k.pT[s][:, :, :].rearrange("p a n -> p (a n)").rearrange("p (c a d) -> p c a d", c=KC, d=XV) for s in range(2)]
    k.xout = [k.qk[s][:, :] for s in range(2)]
    k.place = sb("place", [P, XC])
    k.xrs = sb("xrs", [P, KC, 4, 4, 1])
    k.negmax = sb("negmax", [P, 2 * XP])
    k.mpart = [sb(f"mpart{s}", [P, P // XP, XP], BF16) for s in range(2)]
    k.mrow = [sb(f"mrow{s}", [3 * XP, P], BF16) for s in range(2)]
    k.ffn_s = [k.probs[s][:, 0:PL * P] for s in range(2)]
    k.ffn_h = [k.probs[s][:, PL * P:2 * PL * P].rearrange("p (i n) -> p i n", i=PL) for s in range(2)]
    k.ffn_a = [k.pT[s][:, 0:PL, :] for s in range(2)]
    k.near, k.over, k.far = sb("near", [P, 3, P], BF16), sb("over", [P, 2, P], BF16), sb("far", [P, 1, P], BF16)
    k.outer, k.inner = sb("outer", [P, 2, P], BF16), sb("inner", [P, 2, P], BF16)
    region_a = sb("region_a", [P, 2 * MCS * D])
    k.raw_att = region_a[:, 0:8 * KC * D].rearrange("p (w k n) -> p w k n", w=8, k=KC)
    k.raw_gu = region_a[:, :].rearrange("p (u c n) -> p u c n", u=2, n=D)
    k.hid = region_a[:, :].rearrange("p (c n) -> p c n", n=HALF * P)
    operands = 2 * 2 * XP * D // 2
    region_b = sb("region_b", [P, max(operands + 2 * XG * KC * D, 2 * KC * MCS * P + MCS * D)])
    k.raw_first = region_b[:, 0:4 * KC * D].rearrange("p (w k n) -> p w k n", w=4, k=KC)
    both = region_b[:, 0:operands].bitcast(BF16).rearrange("p (o s a n) -> p o s a n", o=2, s=2, a=XP)
    k.qop, k.kop = [both[:, 0, s] for s in range(2)], [both[:, 1, s] for s in range(2)]
    k.xprob = [region_b[:, operands + s * XG * KC * D:operands + (s + 1) * XG * KC * D].rearrange("p (a c n) -> p a c n", a=XG, c=KC) for s in range(2)]
    k.wgu = region_b[:, 0:2 * KC * MCS * P].rearrange("p (k u n) -> p k u n", k=KC, u=2)
    k.wd = region_b[:, 2 * KC * MCS * P:].rearrange("p (c n) -> p c n", n=D)
    region_c = sb("region_c", [P, KC * TILES * P + 1024 + KC * (MC * P + EI)])
    assert 3 * KC * I0 <= KC * TILES * P + 1024 + KC * (MC * P + EI)
    k.w_ffn = {"gate": region_c[:, 0:KC * I0].rearrange("p (k n) -> p k n", k=KC),
               "up": region_c[:, KC * I0:2 * KC * I0].rearrange("p (k n) -> p k n", k=KC),
               "down": region_c[:, 2 * KC * I0:3 * KC * I0].rearrange("p (g i n) -> p g i n", g=GB, i=PL)}
    k.xall = region_c[:, 0:KC * TILES * P].rearrange("p (k t n) -> p k t n", k=KC, t=TILES)
    k.sg = [region_c[:, 2048 + g * 512:2560 + g * 512] for g in range(2)]
    k.raw_d = region_c[:, KC * TILES * P + 1024:].rearrange("p (k n) -> p k n", k=KC)
    k.raw_r, k.wr = sb("raw_r", [E, D]), sb("wr", [P, KC, E])
    k.score, k.pick = sb("score", [P, TILES * E]), sb("pick", [P, TILES * E])
    k.ebias, k.iota = sb("ebias", [P, E]), sb("iota", [P, E])
    k.best, k.besti, k.bestf = sb("best", [P, TILES, 8]), sb("besti", [P, TILES, 8], U32), sb("bestf", [P, TILES, TOPK])
    k.hit, k.wsum = sb("hit", [P, TILES, TOPK, E]), sb("wsum", [P, TILES, 2])
    k.parts = sb("parts", [P, TILES, 3, E], BF16)
    k.combT, k.expert = sb("combT", [3 * E, TILES * P], BF16), sb("expert", [3 * E, MC * P], BF16)
    return k


def wait(eng, sem, value):
    if isinstance(value, int) and value <= 0:
        return
    eng.wait_ge(sem, value)


def release(k, layer):
    k.nc.clear_and_free_semaphores(k.layer_sems.pop(layer))
    k.nc.all_engine_barrier()


class Steps:

    def __init__(self, eng, sem, t, per):
        self.eng, self.sem, self.t, self.per, self.n = eng, sem, t, per, 0

    def __call__(self, ins):
        self.n += 1
        ins.then_inc(self.sem, 1)
        self.eng.wait_ge(self.sem, self.t * self.per + self.n)

    def end(self):
        assert self.n == self.per, (self.n, self.per)


def pipeline(eng, tile):
    tile(0, 0, None, None)
    tile(1, 1, 0, 0)
    with eng.Fori(0, TILES // 2 - 1) as i:
        tile(2 * i + 2, 0, 2 * i + 1, 1)
        tile(2 * i + 3, 1, 2 * i + 2, 0)
    tile(None, None, TILES - 1, 1)



def norm_moments(k, nc, steps, t, s, stats_ready):
    steps(nc.vector.bn_stats(k.stats[:, s, :], k.x[:, t, :]))
    nc.vector.memset(k.pause[:, :], 0.0)
    steps(nc.vector.bn_aggr(k.moments[:, s, :], k.stats[:, s, :]))
    nc.vector.tensor_scalar(k.varplus[:, s, :], k.moments[:, s, 1:2], LN_EPS, None, ALU.add).then_inc(stats_ready, 1)


def norm_rstd(k, nc, pool, t, s, stats_ready, rstd_ready):
    pool.wait_ge(stats_ready, t + 1)
    nc.gpsimd.tensor_tensor(k.rstd[:, s, :], k.varplus[:, s, :], k.halfpow[:, :], ALU.pow).then_inc(rstd_ready, 1)



def transpose_weights(k, name, groups, ready=None):
    nc = k.nc
    turned = k.sem(name + "_turned")
    by_act, by_dve = k.sem(name + "_by_act"), k.sem(name + "_by_dve")
    copied = [by_act, by_dve]
    with nc.Block() as block:
        @block.tensor
        def _(pe):
            if ready is not None:
                pe.wait_ge(*ready)
            for g, (blocks, dst) in enumerate(groups):
                if g >= 4:
                    pe.wait_ge(copied[g % 2], (g - 4) // 2 + 1)
                for j, b in enumerate(blocks):
                    rows, cols = b.shape
                    last = nc.tensor.transpose(k.psum[0:cols, g % 4, j * P:j * P + rows], b, k.ident[0:rows, 0:rows])
                last.then_inc(turned, 1)

        def out_of(g):
            blocks, dst = groups[g]
            rows, cols = blocks[0].shape
            src = k.psum[0:cols, g % 4, 0:len(blocks) * P].rearrange("p (j r) -> p j r", r=P)[:, :, 0:rows]
            return dst, src

        @block.scalar
        def _(act):
            for g in range(0, len(groups), 2):
                act.wait_ge(turned, g + 1)
                dst, src = out_of(g)
                nc.scalar.activation(dst, src, ACT.Copy).then_inc(by_act, 1)

        @block.vector
        def _(dve):
            for g in range(1, len(groups), 2):
                dve.wait_ge(turned, g + 1)
                dst, src = out_of(g)
                nc.vector.tensor_copy(dst, src).then_inc(by_dve, 1)


def square_groups(raw, dst):
    return [([raw[:, j, kc * P:(kc + 1) * P] for j in range(KC)],
             dst[:, kc, :].rearrange("p (j n) -> p j n", n=P)) for kc in range(KC)]



ROPE, SELF, CROSS = "rope", "self", "cross"


def pipeline5(eng, iteration):
    def stages(i):
        return [i - d if 0 <= i - d < TILES else None for d in range(5)]
    for i in range(4):
        iteration(*stages(i), i % 2)
    with eng.Fori(0, TILES // 2 - 2) as i:
        for j in range(2):
            iteration(*(2 * i + (4 + j - d) for d in range(5)), j)
    for i in range(TILES, TILES + 4):
        iteration(*stages(i), i % 2)


def attention(k, name, kind, w, load=None, fill=None):
    nc, sem = k.nc, k.sem
    bf = kind == CROSS
    names = ("stats_ready rstd_ready xn_ready xT_turned xnT_ready qk_done v_done q_ready qkT_turned qT_ready kTm_ready "
             "scores_done softmax_in exp_done pT_turned pT_ready v_ready pv_done on_ready oT_turned oT_ready y_done "
             "x_done norm_steps q_steps masked max_ready last_steps ctx_ready ctxT_ready").split()
    m = {n: sem(f"{name}_{n}") for n in names}
    (stats_ready, rstd_ready, xn_ready, xT_turned, xnT_ready, qk_done, v_done, q_ready, qkT_turned, qT_ready, kTm_ready,
     scores_done, softmax_in, exp_done, pT_turned, pT_ready, v_ready, pv_done, on_ready, oT_turned, oT_ready, y_done,
     x_done, norm_steps, q_steps, masked, max_ready, last_steps, ctx_ready, ctxT_ready) = (m[n] for n in names)
    SC = k.psum[:, 0:4, :]
    TB, QK, VB, OB = (k.psum[:, b, :] for b in range(4, 8))
    xnT = k.xqT if bf else k.xnT
    scale = 1.0 if bf else 0.25
    norm_per = {ROPE: 2, SELF: 2, CROSS: 7}[kind]
    last_per = {ROPE: 1, SELF: 3, CROSS: 9}[kind]

    with nc.Block() as block:
        @block.sync
        def _(sp):
            if load is not None:
                load(sp)

        @block.gpsimd
        def _(pool):
            def iteration(tn, tf, ts, tb, tl, s):
                if tn is not None:
                    norm_rstd(k, nc, pool, tn, s, stats_ready, rstd_ready)
            pipeline5(pool, iteration)
            if fill is not None:
                pool.wait_ge(rstd_ready, TILES)
                fill(pool)

        @block.tensor
        def _(pe):
            def products(t, s):
                pe.wait_ge(xnT_ready, t + 1)
                if kind != SELF:
                    wait(pe, q_ready, t)
                if kind != ROPE:
                    wait(pe, kTm_ready, t)
                if kind == ROPE:
                    for kc in range(KC):
                        last = nc.tensor.matmul(QK, xnT[s][:, kc, :], w["qk"][:, kc, :], start=kc == 0, stop=kc == KC - 1)
                elif kind == SELF:
                    for c in range(4):
                        for kc in range(KC):
                            last = nc.tensor.matmul(QK[:, c * P:(c + 1) * P], w["qk"][:, kc, c * P:(c + 1) * P],
                                                    xnT[s][:, kc, :], start=kc == 0, stop=kc == KC - 1)
                else:
                    for kc in range(KC):
                        last = nc.tensor.matmul(QK[:, 0:D], xnT[s][:, kc, :], w["q"][:, kc, :], start=kc == 0, stop=kc == KC - 1)
                last.then_inc(qk_done, 1)
                wait(pe, v_ready, t)
                if kind == CROSS:
                    pe.wait_ge(ctxT_ready, t + 1)
                    for c in range(2):
                        for kc in range(KC):
                            nc.tensor.matmul(VB[:, (2 + c) * P:(3 + c) * P], w["k"][:, kc, c * P:(c + 1) * P],
                                             k.ctxT[s][:, kc, :], start=kc == 0, stop=kc == KC - 1)
                src = k.ctxT[s] if kind == CROSS else xnT[s]
                for kc in range(KC):
                    last = nc.tensor.matmul(VB[:, 0:D], src[:, kc, :], w["v"][:, kc, :], start=kc == 0, stop=kc == KC - 1)
                last.then_inc(v_done, 1)

            def turn_out(t, s):
                pe.wait_ge(on_ready, t + 1)
                for kc in range(KC):
                    last = nc.tensor.transpose(OB[:, kc * P:(kc + 1) * P], k.on[s][:, kc * P:(kc + 1) * P], k.ident[:, :])
                last.then_inc(oT_turned, 1)

            def turn_probs(t, s):
                pe.wait_ge(exp_done, t + 1)
                for r in range(4):
                    for hh in range(2):
                        c = s * 256 + hh * P
                        last = nc.tensor.transpose(SC[:, r, c:c + P], k.probs[s][:, (r * 2 + hh) * P:(r * 2 + hh + 1) * P], k.ident[:, :])
                    if r % 2 == 1:
                        last.then_inc(pT_turned, 1)

            def project(t, s):
                pe.wait_ge(oT_ready, t + 1)
                for kc in range(KC):
                    last = nc.tensor.matmul(OB[:, D:2 * D], (k.oTb if bf else k.oT)[s][:, kc, :], w["o"][:, kc, :],
                                            start=kc == 0, stop=kc == KC - 1)
                last.then_inc(y_done, 1)

            def turn_qk(t, s):
                pe.wait_ge(q_ready, t + 1)
                for c in range(4 if kind == ROPE else 2):
                    last = nc.tensor.transpose(TB[:, c * P:(c + 1) * P], k.qk[s][:, c * P:(c + 1) * P], k.ident[:, :])
                last.then_inc(qkT_turned, 1)

            def turn_x(t, s):
                pe.wait_ge(xn_ready, t + 1)
                if kind == SELF:
                    wait(pe, xnT_ready, t)
                elif kind == ROPE:
                    wait(pe, kTm_ready, t)
                else:
                    wait(pe, qT_ready, t)
                for kc in range(KC):
                    last = nc.tensor.transpose(TB[:, kc * P:(kc + 1) * P], k.xn[s][:, kc * P:(kc + 1) * P], k.ident[:, :])
                if kind == CROSS:
                    pe.wait_ge(ctx_ready, t + 1)
                    for kc in range(KC):
                        last = nc.tensor.transpose(TB[:, (2 + kc) * P:(3 + kc) * P], k.ctxs[s][:, kc * P:(kc + 1) * P], k.ident[:, :])
                last.then_inc(xT_turned, 1)

            def attend(t, s):
                pe.wait_ge(pT_ready, 2 * t + 2)
                pe.wait_ge(v_ready, t + 1)
                wait(pe, x_done, t)
                for p in range(PAIRS):
                    for b in range(2):
                        last = nc.tensor.matmul(OB[64 * b:64 * b + 64, 34 * p:34 * p + 34], k.pT[s][:, p, 64 * b:64 * b + 64],
                                                k.vblk[s][:, b, p, :], start=True, stop=True)
                last.then_inc(pv_done, 1)

            def scores(t, s):
                pe.wait_ge(qT_ready, t + 1)
                pe.wait_ge(kTm_ready, t + 1)
                wait(pe, masked, t)
                wait(pe, pT_ready, 2 * t - 2)
                for hh in range(2):
                    for r in range(4):
                        for b in range(2):
                            c = s * 256 + hh * P
                            last = nc.tensor.matmul(
                                SC[64 * b:64 * b + 64, r, c:c + P],
                                k.qkT[s][32 * r:32 * r + 32, hh, 64 * b:64 * b + 64],
                                k.kTm[s][32 * r:32 * r + 32, hh, :, 64 * b:64 * b + 64],
                                start=True, stop=True)
                last.then_inc(scores_done, 1)

            def iteration(tn, tf, ts, tb, tl, s):
                if tf is not None:
                    products(tf, 1 - s)
                if ts is not None:
                    pe.wait_ge(masked, ts + 1)
                if tb is not None:
                    turn_probs(tb, 1 - s)
                if tf is not None and kind != SELF:
                    turn_qk(tf, 1 - s)
                if tl is not None:
                    turn_out(tl, s)
                    project(tl, s)
                if tf is not None:
                    scores(tf, 1 - s)
                if tn is not None:
                    turn_x(tn, s)
                if tb is not None:
                    attend(tb, 1 - s)
            pipeline5(pe, iteration)

        @block.scalar
        def _(act):
            def masked_k(t, s, srcs):
                for c, src in enumerate(srcs):
                    for par in range(2):
                        ins = nc.scalar.activation(k.kTm[s][:, c, par, :], src, ACT.Identity, bias=w["bkm"][:, par, c:c + 1], scale=k.parity[:, par:par + 1])
                ins.then_inc(kTm_ready, 1)

            def values(t, s):
                act.wait_ge(v_done, t + 1)
                wait(act, pv_done, t - 1)
                for par in range(2):
                    for b in range(2):
                        ins = nc.scalar.activation(k.vblk[s][64 * par:64 * par + 64, b, :, 16 * par:16 * par + 16],
                                                   VB[64 * b:64 * b + 64, 0:D].rearrange("k (p c d) -> k p c d", c=2, d=HD)[:, :, par, :],
                                                   ACT.Copy)
                ins.then_inc(v_ready, 1)

            def turned_q(t, s):
                act.wait_ge(qkT_turned, t + 1)
                wait(act, scores_done, t - 1)
                turned = TB.rearrange("p (c n) -> p c n", n=P)
                nc.scalar.activation(k.qkT[s][:, 0:2, :], turned[:, 0:2, :], ACT.Copy, scale=1.0 if kind == ROPE else 0.25).then_inc(qT_ready, 1)

            def turned_k(t, s):
                turned = TB.rearrange("p (c n) -> p c n", n=P)
                for par in range(2):
                    ins = nc.scalar.activation(k.kTm[s][:, :, par, :], turned[:, 2:4, :], ACT.Copy, scale=k.parity[:, par:par + 1])
                ins.then_inc(kTm_ready, 1)

            def products(t, s):
                if kind == SELF:
                    act.wait_ge(qk_done, t + 1)
                    wait(act, scores_done, t - 1)
                    for c in range(2):
                        ins = nc.scalar.activation(k.qkT[s][:, c, :], QK[:, c * P:(c + 1) * P], ACT.Identity, bias=w["bq"][:, c:c + 1])
                    ins.then_inc(qT_ready, 1)
                    masked_k(t, s, [QK[:, (2 + c) * P:(3 + c) * P] for c in range(2)])
                if kind == CROSS:
                    act.wait_ge(v_done, t + 1)
                    wait(act, scores_done, t - 1)
                    masked_k(t, s, [VB[:, (2 + c) * P:(3 + c) * P] for c in range(2)])

            def turned_out(t, s):
                act.wait_ge(oT_turned, t + 1)
                src = OB[:, 0:D].rearrange("p (k n) -> p k n", n=P)
                if bf:
                    nc.scalar.activation(k.oTb[s][:, :, :], src, ACT.Identity, bias=k.unround[:, :]).then_inc(oT_ready, 1)
                else:
                    nc.scalar.activation(k.oT[s][:, :, :], src, ACT.Copy).then_inc(oT_ready, 1)

            def turned_probs(t, s):
                wait(act, pv_done, t)
                for half in range(2):
                    act.wait_ge(pT_turned, 2 * t + half + 1)
                    banks = slice(2 * half, 2 * half + 2)
                    dst = k.pT[s][:, :, :].rearrange("p (h r) n -> p r h n", h=2)[:, banks, :, :]
                    src = SC[:, banks, s * 256:s * 256 + 256].rearrange("p r (h n) -> p r h n", h=2)
                    nc.scalar.activation(dst, src, ACT.Copy).then_inc(pT_ready, 1)

            def turned_x(t, s):
                act.wait_ge(xT_turned, t + 1)
                wait(act, v_done, t - 1)
                src = TB.rearrange("p (k n) -> p k n", n=P)
                if kind == CROSS:
                    nc.scalar.activation(k.ctxT[s][:, :, :], src[:, 2:4, :], ACT.Copy).then_inc(ctxT_ready, 1)
                    nc.scalar.activation(xnT[s][:, :, :], src[:, 0:2, :], ACT.Identity, bias=k.unround[:, :]).then_inc(xnT_ready, 1)
                else:
                    nc.scalar.activation(xnT[s][:, :, :], src[:, 0:2, :], ACT.Copy).then_inc(xnT_ready, 1)

            def iteration(tn, tf, ts, tb, tl, s):
                if tn is not None and kind == CROSS:
                    wait(act, xT_turned, tn - 1)
                    nc.scalar.activation(k.ctxs[s][:, :], k.ctx[:, tn, :], ACT.Copy).then_inc(ctx_ready, 1)
                if tf is not None:
                    products(tf, 1 - s)
                if tb is not None:
                    turned_probs(tb, 1 - s)
                if tf is not None and kind != SELF:
                    turned_q(tf, 1 - s)
                if tl is not None:
                    turned_out(tl, s)
                if tf is not None and kind == ROPE:
                    turned_k(tf, 1 - s)
                if ts is not None:
                    act.wait_ge(softmax_in, ts + 1)
                    nc.scalar.activation(k.probs[s][:, :], k.probs[s][:, :], ACT.Exp, scale=scale).then_inc(exp_done, 1)
                if tn is not None:
                    turned_x(tn, s)
                if tf is not None:
                    values(tf, 1 - s)
            pipeline5(act, iteration)

        @block.vector
        def _(dve):
            def quantise(step, row, sx, scratch):
                step(nc.vector.tensor_reduce(scratch[:, 0:1], row, AX.X, ALU.max, apply_absolute_value=True))
                step(nc.vector.tensor_scalar(sx, scratch[:, 0:1], 1.0 / 127.0, Q_EPS, ALU.mult, ALU.max))
                step(nc.vector.reciprocal(scratch[:, 1:2], sx))
                step(nc.vector.tensor_scalar(row, row, scratch[:, 1:2], ROUND, ALU.mult, ALU.add))
                return nc.vector.tensor_scalar(row, row, ROUND + 127.0, ROUND - 127.0, ALU.min, ALU.max)

            def mask_scores(t, s):
                dve.wait_ge(scores_done, t + 1)
                sc = SC[:, :, s * 256:s * 256 + 256].rearrange("p r (g n) -> p r g n", n=S)
                pr = k.probs[s][:, :].rearrange("p (r g n) -> p r g n", r=4, n=S)
                msk = (k.mask[:, t, :] if kind == CROSS else k.causal[:, :]).unsqueeze(1).unsqueeze(1).broadcast_to([P, 4, 4, S])
                nc.vector.tensor_tensor(pr, sc, msk, ALU.add).then_inc(masked, 1)

            def maximum(t, s):
                dve.wait_ge(masked, t + 1)
                flat = k.probs[s][:, :].rearrange("p (h n) -> p h n", n=S)
                nc.vector.tensor_reduce(k.rowmax[:, s, :], flat, AX.X, ALU.max).then_inc(max_ready, 1)

            def less_maximum(t, s):
                dve.wait_ge(max_ready, t + 1)
                flat = k.probs[s][:, :].rearrange("p (h n) -> p h n", n=S)
                nc.vector.tensor_tensor(flat, flat, k.rowmax[:, s, :].unsqueeze(2).broadcast_to([P, H, S]), ALU.subtract).then_inc(softmax_in, 1)

            def normalise(t, s, own):
                dve.wait_ge(rstd_ready, t + 1)
                wait(dve, xT_turned, t - 1)
                ins = nc.vector.tensor_scalar(k.xn[s][:, :], k.x[:, t, :], k.moments[:, s, 0:1], k.rstd[:, s, :],
                                              ALU.subtract, ALU.mult)
                if kind == CROSS:
                    own(ins)
                    ins = quantise(own, k.xn[s][:, :], k.sx[:, s, :], k.qscr)
                ins.then_inc(xn_ready, 1)
                own.end()

            def finish_q(t, s):
                own = Steps(dve, q_steps, t, 1)
                dve.wait_ge(qk_done, t + 1)
                wait(dve, qkT_turned, t - 1)
                if kind == ROPE:
                    src = QK.rearrange("p (h f c) -> p h f c", f=HD // 2, c=2)
                    dst = k.rot[:, :].rearrange("p (h f c) -> p h f c", f=HD // 2, c=2)
                    cosv = k.rope[:, 0, :].unsqueeze(1).broadcast_to([P, 2 * H, HD])
                    sinv = k.rope[:, 1, :].rearrange("p (f c) -> p f c", c=2).unsqueeze(1).broadcast_to([P, 2 * H, HD // 2, 2])
                    nc.vector.tensor_tensor(k.qk[s][:, :].rearrange("p (h f) -> p h f", f=HD),
                                            QK.rearrange("p (h f) -> p h f", f=HD), cosv, ALU.mult)
                    nc.vector.tensor_tensor(dst[:, :, :, 0], src[:, :, :, 1], sinv[:, :, :, 0], ALU.mult)
                    own(nc.vector.tensor_tensor(dst[:, :, :, 1], src[:, :, :, 0], sinv[:, :, :, 1], ALU.mult))
                    nc.vector.tensor_tensor(k.qk[s][:, :], k.qk[s][:, :], k.rot[:, :], ALU.add).then_inc(q_ready, 1)
                else:
                    q = k.qk[s][:, 0:D]
                    own(nc.vector.scalar_tensor_tensor(q, QK[:, 0:D], k.sx[:, s, :], w["swq"][:, :], ALU.mult, ALU.mult))
                    nc.vector.tensor_tensor(q, q, w["bq"][:, :], ALU.add).then_inc(q_ready, 1)
                own.end()

            def divide(t, s, last):
                dve.wait_ge(pv_done, t + 1)
                ov = OB[:, 0:34 * PAIRS].rearrange("p (a c) -> p a c", c=34)
                last(nc.vector.reciprocal(k.rsum[:, s, :, :], ov[:, :, 32:34]))
                ins = nc.vector.tensor_tensor(k.on[s][:, :].rearrange("p (a c d) -> p a c d", c=2, d=HD),
                                              ov[:, :, 0:32].rearrange("p a (c d) -> p a c d", d=HD),
                                              k.rsum[:, s, :, :].unsqueeze(3).broadcast_to([P, PAIRS, 2, HD]), ALU.mult)
                if kind != ROPE:
                    last(ins)
                    ins = nc.vector.tensor_tensor(k.on[s][:, :], k.on[s][:, :], w["bv"][:, :], ALU.add)
                if kind == CROSS:
                    last(ins)
                    ins = quantise(last, k.on[s][:, :], k.so[:, s, :], k.qscr)
                ins.then_inc(on_ready, 1)

            def add_out(t, s, last):
                dve.wait_ge(y_done, t + 1)
                y = OB[:, D:2 * D]
                if kind == CROSS:
                    last(nc.vector.scalar_tensor_tensor(k.ytmp[:, :], y, k.so[:, s, :], w["swo"][:, :], ALU.mult, ALU.mult))
                    y = k.ytmp[:, :]
                if kind != ROPE:
                    last(nc.vector.tensor_tensor(k.ytmp[:, :], y, w["bo"][:, :], ALU.add))
                    y = k.ytmp[:, :]
                nc.vector.tensor_tensor(k.x[:, t, :], k.x[:, t, :], y, ALU.add).then_inc(x_done, 1)
                last.end()

            def iteration(tn, tf, ts, tb, tl, s):
                if ts is not None:
                    mask_scores(ts, s)
                if tf is not None and kind != SELF:
                    finish_q(tf, 1 - s)
                if tl is not None:
                    last = Steps(dve, last_steps, tl, last_per)
                    divide(tl, s, last)
                if tn is not None:
                    norm = Steps(dve, norm_steps, tn, norm_per)
                    norm_moments(k, nc, norm, tn, s, stats_ready)
                if ts is not None:
                    maximum(ts, s)
                if tn is not None:
                    normalise(tn, s, norm)
                if ts is not None:
                    less_maximum(ts, s)
                if tl is not None:
                    add_out(tl, s, last)
            pipeline5(dve, iteration)



def pipeline3(eng, step, after_first=None):
    step(0, None, None, 0)
    if after_first is not None:
        after_first()
    step(1, 0, None, 1)
    step(2, 1, 0, 0)
    with eng.Fori(0, 2) as i:
        step(2 * i + 3, 2 * i + 2, 2 * i + 1, 1)
        step(2 * i + 4, 2 * i + 3, 2 * i + 2, 0)
    step(7, 6, 5, 1)
    step(None, 7, 6, 0)
    step(None, None, 7, 1)


def set_ones(k, pool):
    k.nc.gpsimd.memset(k.kop[0][64:96, :, :], 1.0).then_inc(k.made, 1)
    pool.wait_ge(k.made, 2)
    k.nc.gpsimd.memset(k.kop[1][64:96, :, :], 1.0)


def channel_attention(k):
    assert TILES == 8
    nc, sem = k.nc, k.sem
    names = ("stats_ready rstd_ready src_ready highs_ready rests_ready mids_ready lows_ready written0 written1 first_loaded0 first_loaded1 last_loaded0 last_loaded1 ctx_turned v_ready "
             "s_done max_ready negmax_parts mt_turned mrow_ready first_rows_in last_rows_in st_done exp_done pv_done xout_ready placed on_ready oT_turned x_done "
             "front_steps part_steps back_steps context_ready ones_set sync_waits").split()
    (stats_ready, rstd_ready, src_ready, highs_ready, rests_ready, mids_ready, lows_ready, written0, written1, first_loaded0, first_loaded1, last_loaded0, last_loaded1, ctx_turned, v_ready,
     s_done, max_ready, negmax_parts, mt_turned, mrow_ready, first_rows_in, last_rows_in, st_done, exp_done, pv_done, xout_ready, placed, on_ready, oT_turned, x_done,
     front_steps, part_steps, back_steps, context_ready, ones_set, sync_waits) = (sem("c0_" + n) for n in names)
    written = [written0, written1]
    loaded = [[first_loaded0, first_loaded1], [last_loaded0, last_loaded1]]
    rows_in = [first_rows_in, last_rows_in]

    def nth(t, s, each):
        return (t - s) // 2 * each + each if isinstance(t, int) else t * (each // 2) + (each - s * (each // 2))
    SB = [k.psum[:, g, :].rearrange("p (c n) -> p c n", c=KC) for g in range(2)]
    ST = [k.psum[:, 2 + 2 * g:4 + 2 * g, :] for g in range(2)]
    OB, TB = k.psum[:, 6, :], k.psum[:, 7, :]
    MT = TB[:, 0:64].bitcast(BF16)
    GR = XP // XG
    HP = XP // 2
    SCALE = float(1.0 / np.sqrt(np.float32(XD)))
    scratch = [[nc.dram_tensor(f"scratch_{o}{s}", (3 * XD, XP, D), BF16).ap() for s in range(2)] for o in "qk"]
    operand = [k.qop, k.kop]

    with nc.Block() as block:
        @block.sync
        def _(sp):
            def hold(sem, value):
                sp.wait_ge(sem, value)
                sp.sem_inc(sync_waits, 1)

            def write(t, s):
                for j, part_ready in enumerate((highs_ready, mids_ready, lows_ready)):
                    hold(part_ready, t + 1)
                    for o in range(2):
                        rows = slice(j * XD, (j + 1) * XD) if o == 0 else slice(j, 3 * XD, 3)
                        sp.dma_start(scratch[o][s][rows, :, :].rearrange("d a n -> a d n"), k.xpart[s][:, j, o, :]).then_inc(written[s], 16)

            def read(t, s, half):
                hold(written[s], nth(t, s, 96))
                cut = slice(half * HP, (half + 1) * HP)
                for o in range(2):
                    src = scratch[o][s].rearrange("r a n -> r (a n)")[:, half * HP * D:(half + 1) * HP * D].unsqueeze(1 - o)
                    src = src.broadcast_to([3 * XD, 3, HP * D] if o == 0 else [3, 3 * XD, HP * D])
                    sp.dma_start(operand[o][s][0:XR, cut, :], src).then_inc(loaded[half][s], 16)

            def rows(t, s, half):
                hold(mrow_ready, 2 * t + half + 1)
                dst = k.qop[s][XR:XR + 3, half * HP:(half + 1) * HP, :].rearrange("r a (c n) -> r (a c) n", c=KC)
                sp.dma_start(dst, k.mrow[half][:, :]).then_inc(rows_in[half], 16)

            def step(tp, tf, tb, a):
                if tb is not None:
                    rows(tb, a, 1)
                if tp is not None:
                    write(tp, a)
                    if tb is not None:
                        hold(st_done, GR * tb + GR // 2)
                    read(tp, a, 0)
                if tf is not None:
                    rows(tf, 1 - a, 0)
                if tp is not None:
                    if tb is not None:
                        hold(st_done, GR * tb + GR)
                    read(tp, a, 1)
            pipeline3(sp, step)

        @block.gpsimd
        def _(pool):
            def split_max(t, half):
                own = Steps(pool, part_steps, 2 * t + half, 3)
                zero = k.zero[:, :].broadcast_to([P, 2 * HP])
                src = k.negmax[:, half * 2 * HP:(half + 1) * 2 * HP]
                pool.wait_ge(max_ready, XP * t + HP * (half + 1))
                wait(pool, mt_turned, 2 * t + half - 1)
                own(nc.gpsimd.tensor_tensor(k.mpart[half][:, 0, :], src, zero, ALU.add))
                own(nc.gpsimd.tensor_tensor(src, src, k.mpart[half][:, 0, :], ALU.subtract))
                own(nc.gpsimd.tensor_tensor(k.mpart[half][:, 1, :], src, zero, ALU.add))
                nc.gpsimd.tensor_tensor(k.mpart[half][:, 2, :], src, k.mpart[half][:, 1, :], ALU.subtract).then_inc(negmax_parts, 1)
                own.end()

            def context(t, s):
                wait(pool, lows_ready, t - 1)
                wait(pool, ctx_turned, t - 1)
                nc.gpsimd.tensor_tensor(k.xsrc[s][:, 1, :], k.ctx[:, t, :], k.zero[:, :].broadcast_to([P, D]), ALU.add).then_inc(context_ready, 1)

            def step(tp, tf, tb, a):
                if tp is not None:
                    norm_rstd(k, nc, pool, tp, a, stats_ready, rstd_ready)
                    context(tp, a)
                    pool.wait_ge(highs_ready, tp + 1)
                    pool.wait_ge(context_ready, tp + 1)
                    nc.gpsimd.tensor_tensor(k.rest[:, :, :], k.xsrc[a][:, :, :], k.xpart[a][:, 0, :, :], ALU.subtract).then_inc(rests_ready, 1)
                    pool.wait_ge(mids_ready, tp + 1)
                    nc.gpsimd.tensor_tensor(k.xpart[a][:, 2, :, :], k.rest[:, :, :], k.xpart[a][:, 1, :, :], ALU.subtract).then_inc(lows_ready, 1)
                if tf is not None:
                    split_max(tf, 0)
                    split_max(tf, 1)
            pipeline3(pool, step)

        @block.tensor
        def _(pe):
            def turn_max(t, half):
                pe.wait_ge(negmax_parts, 2 * t + half + 1)
                if half == 0:
                    wait(pe, mrow_ready, 2 * t)
                    wait(pe, x_done, t - 1)
                else:
                    pe.wait_ge(v_ready, t + 1)
                nc.tensor.transpose(MT[:, :], k.mpart[half][:, :, :].rearrange("p j m -> p (j m)"), k.identb[:, :]).then_inc(mt_turned, 1)

            def values(t, s, g):
                u = GR * t + g
                pe.wait_ge(exp_done, u + 1)
                if g == 0:
                    pe.wait_ge(v_ready, t + 1)
                if g % (GR // 2) == 0:
                    wait(pe, xout_ready, 2 * t + g // (GR // 2))
                for a in range(XG):
                    p = XG * g + a
                    b, c = p // 4 % 2, p % 4
                    for lc in range(KC):
                        last = nc.tensor.matmul(OB[XV * c:XV * (c + 1), b * D:(b + 1) * D], k.vT[s][:, lc, p, :],
                                                k.xprob[g % 2][:, a, lc, :], start=lc == 0, stop=lc == KC - 1)
                last.then_inc(pv_done, 1)

            def turn_values(t):
                pe.wait_ge(xout_ready, 2 * t + 2)
                for b in range(4):
                    for qc in range(KC):
                        c = (qc * 4 + b) * XC
                        last = nc.tensor.matmul(TB[:, c:c + XC], k.xout[b // 2][:, (b % 2) * D + qc * P:(b % 2) * D + (qc + 1) * P],
                                                k.place[:, :], start=True, stop=True)
                last.then_inc(placed, 1)

            def turn_out(t):
                pe.wait_ge(on_ready, t + 1)
                for qc in range(KC):
                    last = nc.tensor.transpose(TB[:, qc * P:(qc + 1) * P], k.on[0][:, qc * P:(qc + 1) * P], k.ident[:, :])
                last.then_inc(oT_turned, 1)

            def turn_context(t, s):
                pe.wait_ge(context_ready, t + 1)
                pe.wait_ge(mrow_ready, 2 * t + 1)
                for lc in range(KC):
                    last = nc.tensor.transpose(TB[:, (2 + lc) * P:(3 + lc) * P], k.xsrc[s][:, 1, lc * P:(lc + 1) * P], k.ident[:, :])
                last.then_inc(ctx_turned, 1)

            def step(tp, tf, tb, a):
                before = tb - 1 if tb is not None and not (isinstance(tb, int) and tb == 0) else None
                for g in range(GR):
                    if tb is not None:
                        if g == 1:
                            turn_max(tb, 1)
                        u = GR * tb + g
                        if g % (GR // 2) == 0:
                            pe.wait_ge(rows_in[g // (GR // 2)], 16 * tb + 16)
                        wait(pe, exp_done, u - 1)
                        for j in range(XG):
                            for lc in range(KC):
                                last = nc.tensor.matmul(ST[g % 2][:, j, lc * D:(lc + 1) * D], k.kop[a][0:XR + 3, XG * g + j, lc * P:(lc + 1) * P],
                                                        k.qop[a][0:XR + 3, XG * g + j, :], start=True, stop=True)
                        last.then_inc(st_done, 1)
                    if tf is not None:
                        if g % (GR // 2) == 0:
                            pe.wait_ge(loaded[g // (GR // 2)][1 - a], nth(tf, 1 - a, 32))
                        for j in range(XG):
                            p = XG * g + j
                            wait(pe, max_ready, XP * tf + p - 1)
                            for qc in range(KC):
                                last = nc.tensor.matmul(SB[p % 2][:, qc, :], k.qop[1 - a][0:XR, p, qc * P:(qc + 1) * P],
                                                        k.kop[1 - a][0:XR, p, :], start=True, stop=True)
                            last.then_inc(s_done, 1)
                        if g == 5:
                            turn_max(tf, 0)
                        if g == 6:
                            turn_context(tf, 1 - a)
                    if before is not None and g == 2:
                        pe.wait_ge(mrow_ready, 2 * tb + 2)
                        turn_values(before)
                    if before is not None and g == 3:
                        turn_out(before)
                    if tb is not None and g >= 1:
                        values(tb, a, g - 1)
                if tb is not None:
                    values(tb, a, GR - 1)
            pe.wait_ge(ones_set, 1)
            pipeline3(pe, step)
            pe.wait_ge(x_done, TILES - 1)
            turn_values(TILES - 1)
            turn_out(TILES - 1)

        @block.scalar
        def _(act):
            def max_rows(t, half):
                act.wait_ge(mt_turned, 2 * t + half + 1)
                wait(act, rows_in[half], 16 * t)
                nc.scalar.activation(k.mrow[half][:, :], MT[0:6 * HP, :], ACT.Copy).then_inc(mrow_ready, 1)

            def turned_values(t, s):
                act.wait_ge(ctx_turned, t + 1)
                wait(act, pv_done, GR * (t - 1))
                nc.scalar.activation(k.vT[s][:, :, :, 0:XD], TB[:, D:2 * D].rearrange("p (c a d) -> p c a d", c=KC, d=XD), ACT.Copy).then_inc(v_ready, 1)

            def half_out(t, half):
                act.wait_ge(pv_done, GR * t + (half + 1) * GR // 2)
                wait(act, placed, t)
                nc.scalar.activation(k.xout[half], OB, ACT.Copy).then_inc(xout_ready, 1)

            def step(tp, tf, tb, a):
                for g in range(GR):
                    if tb is not None:
                        u = GR * tb + g
                        act.wait_ge(st_done, u + 1)
                        wait(act, pv_done, u - 1)
                        nc.scalar.activation(k.xprob[g % 2][:, :, :, :], ST[g % 2], ACT.Exp, scale=SCALE).then_inc(exp_done, 1)
                        if g == 1:
                            max_rows(tb, 1)
                        if g == GR // 2:
                            half_out(tb, 0)
                    if tp is not None and g == 1:
                        act.wait_ge(src_ready, tp + 1)
                        act.wait_ge(context_ready, tp + 1)
                        wait(act, written[a], nth(tp, a, 96) - 96)
                        nc.scalar.activation(k.xpart[a][:, 0, :, :], k.xsrc[a][:, :, :], ACT.Copy).then_inc(highs_ready, 1)
                    if tp is not None and g == 2:
                        act.wait_ge(rests_ready, tp + 1)
                        nc.scalar.activation(k.xpart[a][:, 1, :, :], k.rest[:, :, :], ACT.Copy).then_inc(mids_ready, 1)
                    if tf is not None and g == 5:
                        max_rows(tf, 0)
                    if tf is not None and g == 6:
                        turned_values(tf, 1 - a)
                if tb is not None:
                    half_out(tb, 1)
            pipeline3(act, step)

        @block.vector
        def _(dve):
            nc.vector.tensor_scalar(k.place[:, 0:4 * XD], k.place[:, 0:4 * XD], k.gamma[:, :], None, ALU.mult)

            def constants():
                for s in range(2):
                    nc.vector.memset(k.vT[s][:, :, :, XD:XD + 1], 1.0)
                    nc.vector.memset(k.vT[s][:, :, :, XD + 1:], 0.0)
                    ins = nc.vector.memset(k.mpart[s][:, 3:, :], 0.0)
                ins.then_inc(ones_set, 1)

            def normalise(t, s):
                wait(dve, lows_ready, t - 1)
                dve.wait_ge(rstd_ready, t + 1)
                nc.vector.tensor_scalar(k.xsrc[s][:, 0, :], k.x[:, t, :], k.moments[:, s, 0:1], k.rstd[:, s, :],
                                        ALU.subtract, ALU.mult).then_inc(src_ready, 1)

            def add_out(t):
                dve.wait_ge(oT_turned, t + 1)
                nc.vector.tensor_tensor(k.x[:, t, :], k.x[:, t, :], TB[:, 0:D], ALU.add).then_inc(x_done, 1)

            def divide(t):
                dve.wait_ge(placed, t + 1)
                tv = TB[:, 0:KC * 4 * XC].rearrange("p (q b c) -> p q b c", q=KC, b=4)
                nc.vector.reciprocal(k.xrs[:, :, :, :, 0], tv[:, :, :, 4 * XD:]).then_inc(back_steps, 1)
                dve.wait_ge(back_steps, t + 1)
                for qc in range(KC):
                    ins = nc.vector.tensor_tensor(k.on[0][:, qc * P:(qc + 1) * P].rearrange("p (b a d) -> p b a d", b=4, d=XD),
                                                  tv[:, qc, :, 0:4 * XD].rearrange("p b (a d) -> p b a d", d=XD),
                                                  k.xrs[:, qc, :, :, :].broadcast_to([P, 4, 4, XD]), ALU.mult)
                ins.then_inc(on_ready, 1)

            def step(tp, tf, tb, a):
                before = tb - 1 if tb is not None and not (isinstance(tb, int) and tb == 0) else None
                if tp is not None:
                    norm_moments(k, nc, Steps(dve, front_steps, tp, 2), tp, a, stats_ready)
                    if tf is None:
                        normalise(tp, a)
                if tf is not None:
                    for p in range(XP):
                        dve.wait_ge(s_done, XP * tf + p + 1)
                        if p % HP == 0:
                            wait(dve, negmax_parts, 2 * tf + p // HP - 1)
                        nc.vector.tensor_reduce(k.negmax[:, 2 * p:2 * p + 2], SB[p % 2], AX.X, ALU.max, negate=True).then_inc(max_ready, 1)
                        if tp is not None and p == XG:
                            normalise(tp, a)
                        if before is not None and p == 3 * XG - 1:
                            divide(before)
                        if before is not None and p == 4 * XG - 1:
                            add_out(before)
                elif before is not None:
                    divide(before)
                    add_out(before)
            pipeline3(dve, step, constants)
            divide(TILES - 1)
            add_out(TILES - 1)




def sparse_ffn(k, w):
    nc, sem = k.nc, k.sem
    names = ("stats_ready rstd_ready xn_ready xT_turned xnT_ready gate_done up_done silu_ready prod_ready abs_ready kept_ready "
             "down_done x_done front_steps unit_steps").split()
    (stats_ready, rstd_ready, xn_ready, xT_turned, xnT_ready, gate_done, up_done, silu_ready, prod_ready, abs_ready, kept_ready,
     down_done, x_done, front_steps, unit_steps) = (sem("f0_" + n) for n in names)
    G = [k.psum[:, g, :] for g in range(GB)]
    U = [k.psum[:, 2 + g, :] for g in range(GB)]
    TB, Y = k.psum[:, 4, :], k.psum[:, 5, 0:D]
    hid = [k.ffn_h[g][:, :, :] for g in range(GB)]
    mag = [k.ffn_a[g][:, :, :] for g in range(GB)]
    flat = [k.ffn_h[g][:, :, :].rearrange("p i n -> p (i n)") for g in range(GB)]

    with nc.Block() as block:
        @block.gpsimd
        def _(pool):
            def tile(tf, sf, tb, sb):
                if tf is not None:
                    norm_rstd(k, nc, pool, tf, sf, stats_ready, rstd_ready)
            pipeline(pool, tile)

        @block.tensor
        def _(pe):
            def gate_up(t, s, g):
                wait(pe, silu_ready, 2 * t + g - 1)
                for bank, wt, done in ((G[g], w["gate"], gate_done), (U[g], w["up"], up_done)):
                    if wt is w["up"]:
                        wait(pe, prod_ready, 2 * t + g - 1)
                    for i in range(PL):
                        for kc in range(KC):
                            last = nc.tensor.matmul(bank[:, i * P:(i + 1) * P], wt[:, kc, g * PL * P + i:(g + 1) * PL * P:PL],
                                                    k.xnT[s][:, kc, :], start=kc == 0, stop=kc == KC - 1)
                    last.then_inc(done, 1)

            def down(t, g):
                pe.wait_ge(kept_ready, 2 * t + g + 1)
                if g == 0:
                    wait(pe, x_done, t)
                for i in range(PL):
                    last = nc.tensor.matmul(Y, k.ffn_h[g][:, i, :], w["down"][:, g, i, :], start=g == 0 and i == 0, stop=g == GB - 1 and i == PL - 1)
                last.then_inc(down_done, 1)

            def tile(tf, sf, tb, sb):
                if tb is not None:
                    if isinstance(tb, int) and tb == 0:
                        pe.wait_ge(k.ffn_in, 3 * 16)
                    pe.wait_ge(xnT_ready, tb + 1)
                    gate_up(tb, sb, 0)
                    if not (isinstance(tb, int) and tb == 0):
                        down(tb - 1, 1)
                if tf is not None:
                    pe.wait_ge(xn_ready, tf + 1)
                    wait(pe, xnT_ready, tf)
                    for kc in range(KC):
                        last = nc.tensor.transpose(TB[:, kc * P:(kc + 1) * P], k.xn[sf][:, kc * P:(kc + 1) * P], k.ident[:, :])
                    last.then_inc(xT_turned, 1)
                if tb is not None:
                    gate_up(tb, sb, 1)
                    down(tb, 0)
            pipeline(pe, tile)
            down(TILES - 1, 1)

        @block.scalar
        def _(act):
            def unit(t, g):
                u = 2 * t + g
                act.wait_ge(gate_done, u + 1)
                wait(act, prod_ready, u - 1)
                nc.scalar.activation(k.ffn_s[g][:, :], G[g], ACT.Silu).then_inc(silu_ready, 1)

            def magnitude(t, g):
                u = 2 * t + g
                act.wait_ge(prod_ready, u + 1)
                wait(act, kept_ready, u - 1)
                nc.scalar.activation(mag[g], hid[g], ACT.Abs).then_inc(abs_ready, 1)

            def tile(tf, sf, tb, sb):
                if tf is not None:
                    act.wait_ge(xT_turned, tf + 1)
                    wait(act, up_done, 2 * tf - 2)
                    nc.scalar.activation(k.xnT[sf][:, :, :], TB[:, 0:D].rearrange("p (k n) -> p k n", n=P), ACT.Copy).then_inc(xnT_ready, 1)

            def whole(tf, sf, tb, sb):
                if tb is not None:
                    unit(tb, 0)
                    magnitude(tb, 0)
                tile(tf, sf, tb, sb)
                if tb is not None:
                    unit(tb, 1)
                    magnitude(tb, 1)
            pipeline(act, whole)

        @block.vector
        def _(dve):
            def unit(t, g):
                u = 2 * t + g
                own = Steps(dve, unit_steps, u, 3)
                dve.wait_ge(silu_ready, u + 1)
                dve.wait_ge(up_done, u + 1)
                wait(dve, down_done, u - 1)
                nc.vector.tensor_tensor(flat[g], k.ffn_s[g][:, :], U[g], ALU.mult).then_inc(prod_ready, 1)
                dve.wait_ge(abs_ready, u + 1)
                a = mag[g]
                nc.vector.tensor_tensor(k.near[:, :, :], a[:, 0:3, :], a[:, 1:4, :], ALU.is_ge)
                nc.vector.tensor_tensor(k.over[:, :, :], a[:, 0:2, :], a[:, 2:4, :], ALU.is_ge)
                own(nc.vector.tensor_tensor(k.far[:, :, :], a[:, 0:1, :], a[:, 3:4, :], ALU.is_ge))
                nc.vector.tensor_tensor(k.outer[:, :, :], k.near[:, 0:3:2, :], k.over[:, :, :], ALU.add)
                own(nc.vector.tensor_tensor(k.inner[:, :, :], k.over[:, :, :], k.near[:, 1:2, :].broadcast_to([P, 2, P]), ALU.add))
                nc.vector.tensor_tensor(k.outer[:, :, :], k.outer[:, :, :], k.far[:, :, :].broadcast_to([P, 2, P]), ALU.add)
                nc.vector.tensor_tensor(k.inner[:, 0, :], k.inner[:, 0, :], k.near[:, 2, :], ALU.subtract)
                own(nc.vector.tensor_tensor(k.inner[:, 1, :], k.inner[:, 1, :], k.near[:, 0, :], ALU.subtract))
                own.end()
                h = hid[g]
                nc.vector.scalar_tensor_tensor(h[:, 0, :], k.outer[:, 0, :], 1.5, h[:, 0, :], ALU.is_gt, ALU.mult)
                nc.vector.scalar_tensor_tensor(h[:, 1, :], k.inner[:, 1, :], 0.5, h[:, 1, :], ALU.is_gt, ALU.mult)
                nc.vector.scalar_tensor_tensor(h[:, 2, :], k.inner[:, 0, :], 0.5, h[:, 2, :], ALU.is_lt, ALU.mult)
                nc.vector.scalar_tensor_tensor(h[:, 3, :], k.outer[:, 1, :], 1.5, h[:, 3, :], ALU.is_lt, ALU.mult).then_inc(kept_ready, 1)

            def add_out(t):
                dve.wait_ge(down_done, 2 * t + 2)
                nc.vector.tensor_tensor(k.x[:, t, :], k.x[:, t, :], Y, ALU.add).then_inc(x_done, 1)

            def tile(tf, sf, tb, sb):
                if tf is not None:
                    front = Steps(dve, front_steps, tf, 2)
                    norm_moments(k, nc, front, tf, sf, stats_ready)
                    dve.wait_ge(rstd_ready, tf + 1)
                    wait(dve, xT_turned, tf - 1)
                    nc.vector.tensor_scalar(k.xn[sf][:, :], k.x[:, tf, :], k.moments[:, sf, 0:1], k.rstd[:, sf, :],
                                            ALU.subtract, ALU.mult).then_inc(xn_ready, 1)
                if tb is not None:
                    unit(tb, 0)
                    if not (isinstance(tb, int) and tb == 0):
                        add_out(tb - 1)
                    unit(tb, 1)
            pipeline(dve, tile)
            add_out(TILES - 1)




def expert_weights(k):
    nc = k.nc
    groups = []
    for u in range(2):
        for kc in range(KC):
            cut = slice(kc * P, (kc + 1) * P)
            for c in range(0, MC, 4):
                groups.append(([k.raw_gu[:, u, c + j, cut] for j in range(4)],
                               k.wgu[:, kc, u, c * P:(c + 4) * P].rearrange("p (j n) -> p j n", n=P)))
            groups.append(([k.raw_gu[0:EI, u, MC, cut]], k.wgu[:, kc, u, MC * P:MC * P + EI].unsqueeze(1)))
    for c in range(0, MC, 2):
        groups.append(([k.raw_d[:, nb, (c + j) * P:(c + j + 1) * P] for j in range(2) for nb in range(2)],
                       k.wd[:, c:c + 2, :].rearrange("p c (b n) -> p (c b) n", n=P)))
    groups.append(([k.raw_d[:, nb, MC * P:MC * P + EI] for nb in range(2)], k.wd[0:EI, MC, :].rearrange("p (b n) -> p b n", n=P)))
    groups.append(([k.raw_r[:, kc * P:(kc + 1) * P] for kc in range(KC)], k.wr[:, :, :]))
    transpose_weights(k, "w3", groups, (k.moe_in, k.moe_loads * 16))


def experts(k, out):
    nc, sem = k.nc, k.sem
    names = ("stats_ready rstd_ready xn_ready xT_turned xnT_ready xall_ready logits_done front_steps").split()
    (stats_ready, rstd_ready, xn_ready, xT_turned, xnT_ready, xall_ready, logits_done, front_steps) = (sem("m0_" + n) for n in names)
    TB, LB = k.psum[:, 4, :], k.psum[:, 5, 0:TILES * E]

    with nc.Block() as block:
        @block.gpsimd
        def _(pool):
            def tile(tf, sf, tb, sb):
                if tf is not None:
                    norm_rstd(k, nc, pool, tf, sf, stats_ready, rstd_ready)
            pipeline(pool, tile)

        @block.tensor
        def _(pe):
            def tile(tf, sf, tb, sb):
                if tf is not None:
                    pe.wait_ge(xn_ready, tf + 1)
                    wait(pe, xnT_ready, tf)
                    for kc in range(KC):
                        last = nc.tensor.transpose(TB[:, kc * P:(kc + 1) * P], k.xn[sf][:, kc * P:(kc + 1) * P], k.ident[:, :])
                    last.then_inc(xT_turned, 1)
                if tb is not None:
                    pe.wait_ge(xnT_ready, tb + 1)
                    for kc in range(KC):
                        last = nc.tensor.matmul(LB[:, bass.ds(tb * E, E)], k.xnT[sb][:, kc, :], k.wr[:, kc, :],
                                                start=kc == 0, stop=kc == KC - 1)
                    last.then_inc(logits_done, 1)
            pipeline(pe, tile)

        @block.scalar
        def _(act):
            def tile(tf, sf, tb, sb):
                if tf is not None:
                    act.wait_ge(xT_turned, tf + 1)
                    wait(act, logits_done, tf - 1)
                    wait(act, xall_ready, tf - 1)
                    nc.scalar.activation(k.xnT[sf][:, :, :], TB[:, 0:D].rearrange("p (k n) -> p k n", n=P), ACT.Copy).then_inc(xnT_ready, 1)
            pipeline(act, tile)

        @block.vector
        def _(dve):
            def tile(tf, sf, tb, sb):
                if tf is not None:
                    front = Steps(dve, front_steps, tf, 2)
                    norm_moments(k, nc, front, tf, sf, stats_ready)
                    dve.wait_ge(rstd_ready, tf + 1)
                    wait(dve, xT_turned, tf - 1)
                    nc.vector.tensor_scalar(k.xn[sf][:, :], k.x[:, tf, :], k.moments[:, sf, 0:1], k.rstd[:, sf, :],
                                            ALU.subtract, ALU.mult).then_inc(xn_ready, 1)
                if tb is not None:
                    dve.wait_ge(xnT_ready, tb + 1)
                    nc.vector.tensor_scalar(k.xall[:, :, tb, :], k.xnT[sb][:, :, :], 1.0, None, ALU.mult).then_inc(xall_ready, 1)
            pipeline(dve, tile)

    route(k)

    names = "gate_done up_done comb_done silu_ready hid_ready down_done x_done prod_done stored".split()
    (gate_done, up_done, comb_done, silu_ready, hid_ready, down_done, x_done, prod_done, stored) = (sem("m2_" + n) for n in names)
    G = [k.psum[:, g, :] for g in range(2)]
    U = [k.psum[:, 2 + g, :] for g in range(2)]
    C = [k.psum[:, 4 + g, :] for g in range(2)]
    Y = [k.psum[:, 6 + g, 0:D] for g in range(2)]
    rows = [P] * MC + [EI]
    tok = HALF * P

    with nc.Block() as block:
        @block.tensor
        def _(pe):
            def half(v):
                for c in range(MCS):
                    n, g = rows[c], c % 2
                    units = v * MCS + c
                    cols = slice(c * P, c * P + n)
                    xs = k.xall[:, :, :, :].rearrange("p k t n -> p k (t n)")
                    wait(pe, silu_ready, units - 1)
                    for kc in range(KC):
                        last = nc.tensor.matmul(G[g][0:n, :], k.wgu[:, kc, 0, cols], xs[:, kc, bass.ds(v * tok, tok)], start=kc == 0, stop=kc == KC - 1)
                    last.then_inc(gate_done, 1)
                    wait(pe, hid_ready, units - 1)
                    for kc in range(KC):
                        last = nc.tensor.matmul(U[g][0:n, :], k.wgu[:, kc, 1, cols], xs[:, kc, bass.ds(v * tok, tok)], start=kc == 0, stop=kc == KC - 1)
                    last.then_inc(up_done, 1)
                    if c < MC:
                        nc.tensor.matmul(C[g], k.expert[:, cols], k.combT[:, bass.ds(v * tok, tok)], start=True, stop=True).then_inc(comb_done, 1)
                for j in range(HALF):
                    pe.wait_ge(hid_ready, v * MCS + MCS)
                    wait(pe, x_done, v * HALF + j - 1)
                    for c in range(MCS):
                        last = nc.tensor.matmul(Y[j % 2], k.hid[0:rows[c], c, j * P:(j + 1) * P], k.wd[0:rows[c], c, :], start=c == 0, stop=c == MCS - 1)
                    last.then_inc(down_done, 1)
            for v in range(TILES // HALF):
                half(v)

        @block.scalar
        def _(act):
            def half(v):
                for c in range(MCS):
                    n, g = rows[c], c % 2
                    units = v * MCS + c
                    act.wait_ge(gate_done, units + 1)
                    wait(act, prod_done, units - 1)
                    nc.scalar.activation(k.sg[g][0:n, :], G[g][0:n, :], ACT.Silu).then_inc(silu_ready, 1)
            for v in range(TILES // HALF):
                half(v)

        @block.vector
        def _(dve):
            def half(v):
                for c in range(MCS):
                    n, g = rows[c], c % 2
                    units = v * MCS + c
                    dve.wait_ge(silu_ready, units + 1)
                    dve.wait_ge(up_done, units + 1)
                    wait(dve, down_done, v * HALF)
                    ins = nc.vector.tensor_tensor(k.hid[0:n, c, :], k.sg[g][0:n, :], U[g][0:n, :], ALU.mult).then_inc(prod_done, 1)
                    dve.wait_ge(prod_done, units + 1)
                    if c < MC:
                        dve.wait_ge(comb_done, v * MC + c + 1)
                        nc.vector.tensor_tensor(k.hid[:, c, :], k.hid[:, c, :], C[g], ALU.mult).then_inc(hid_ready, 1)
                    else:
                        nc.vector.memset(k.pause[:, :], 0.0).then_inc(hid_ready, 1)
                for j in range(HALF):
                    t = v * HALF + j
                    dve.wait_ge(down_done, t + 1)
                    nc.vector.tensor_tensor(k.x[:, t, :], k.x[:, t, :], Y[j % 2], ALU.add).then_inc(x_done, 1)
            for v in range(TILES // HALF):
                half(v)

        @block.sync
        def _(sp):
            for t in range(TILES):
                sp.wait_ge(x_done, t + 1)
                sp.dma_start(tiles_of(out)[:, t, :], k.x[:, t, :]).then_inc(stored, 16)
            sp.wait_ge(stored, TILES * 16)


def route(k):
    nc, sem = k.nc, k.sem
    scored, parted, turned, own_steps, copied = (sem("r_" + n) for n in "scored parted turned own_steps copied".split())
    LB, CB = k.psum[:, 5, 0:TILES * E], k.psum[0:3 * E, 6, :].bitcast(BF16)
    with nc.Block() as block:
        @block.scalar
        def _(act):
            nc.scalar.activation(k.score[:, :], LB, ACT.Sigmoid).then_inc(scored, 1)

        @block.vector
        def _(dve):
            own = Steps(dve, own_steps, 0, 13)
            score = k.score[:, :].rearrange("p (t e) -> p t e", e=E)
            pick = k.pick[:, :].rearrange("p (t e) -> p t e", e=E)
            dve.wait_ge(scored, 1)
            own(nc.vector.tensor_tensor(pick, score, k.ebias[:, :].unsqueeze(1).broadcast_to([P, TILES, E]), ALU.add))
            for t in range(TILES):
                ins = nc.vector.max(k.best[:, t, :], pick[:, t, :])
            own(ins)
            for t in range(TILES):
                ins = nc.vector.max_index(k.besti[:, t, :], k.best[:, t, :], pick[:, t, :])
            own(ins)
            own(nc.vector.tensor_copy(k.bestf[:, :, :], k.besti[:, :, 0:TOPK]))
            own(nc.vector.tensor_tensor(k.hit[:, :, :, :], k.bestf[:, :, :].unsqueeze(3).broadcast_to([P, TILES, TOPK, E]),
                                        k.iota[:, :].unsqueeze(1).unsqueeze(1).broadcast_to([P, TILES, TOPK, E]), ALU.is_equal))
            own(nc.vector.tensor_reduce(pick, k.hit[:, :, :, :].rearrange("p t r e -> p t e r"), AX.X, ALU.add))
            own(nc.vector.tensor_tensor(k.pick[:, :], k.pick[:, :], k.score[:, :], ALU.mult))
            own(nc.vector.tensor_reduce(k.wsum[:, :, 0], pick, AX.X, ALU.add))
            own(nc.vector.tensor_scalar(k.wsum[:, :, 0], k.wsum[:, :, 0], 1e-20, None, ALU.add))
            own(nc.vector.reciprocal(k.wsum[:, :, 1], k.wsum[:, :, 0]))
            own(nc.vector.tensor_tensor(pick, pick, k.wsum[:, :, 1:2].broadcast_to([P, TILES, E]), ALU.mult))
            parts = k.parts[:, :, :, :]
            nc.vector.tensor_copy(parts[:, :, 0, :], pick).then_inc(own_steps, 1)
            own.n += 1
            dve.wait_ge(own_steps, own.n)
            own(nc.vector.tensor_tensor(pick, pick, parts[:, :, 0, :], ALU.subtract))
            own.end()
            nc.vector.tensor_copy(parts[:, :, 1, :], pick).then_inc(parted, 1)
            dve.wait_ge(parted, 1)
            nc.vector.tensor_tensor(parts[:, :, 2, :], pick, parts[:, :, 1, :], ALU.subtract).then_inc(parted, 1)

            dve.wait_ge(turned, 1)
            nc.vector.tensor_copy(k.combT[:, :], CB[:, :]).then_inc(copied, 1)

        @block.tensor
        def _(pe):
            pe.wait_ge(parted, 2)
            for t in range(TILES):
                last = nc.tensor.transpose(CB[:, t * P:(t + 1) * P], k.parts[:, t, :, :].rearrange("p s e -> p (s e)"), k.identb[:, :])
            last.then_inc(turned, 1)


def tiles_of(ap):
    return ap.rearrange("b s n -> (b s) n").rearrange("(t p) n -> p t n", p=P)


def rows_of(ap):
    return ap.rearrange("(j p) n -> p j n", p=P)


ATT_RAW = ("L0_attn_Wq", "L0_attn_Wk", "L0_attn_Wv", "L0_attn_Wo", "L1_attn_Wq", "L1_attn_Wk", "L1_attn_Wv", "L1_attn_Wo",
           "L1_xattn_wq", "L1_xattn_wk", "L1_xattn_wv", "L1_xattn_wo")


def load_experts(k, sp):
    d, loads = k.dram, 0
    for u in range(2):
        for f in range(4):
            i = 0
            while i < EI:
                row = EI * f + i
                n = min(EI - i, P - row % P)
                src = d["L1_ffn_gate_up_proj"][:, u * EI + i:u * EI + i + n, :].rearrange("(g f) i n -> f i g n", f=4)[f]
                sp.dma_start(k.raw_gu[row % P:row % P + n, u, row // P:MC:3, :], src).then_inc(k.moe_in, 16)
                loads += 1
                i += n
    for u, n in enumerate(("L1_ffn_shared_gate_w", "L1_ffn_shared_up_w")):
        sp.dma_start(k.raw_gu[0:EI, u, MC, :], d[n]).then_inc(k.moe_in, 16)
    for nb in range(KC):
        sp.dma_start(k.raw_d[:, nb, 0:MC * P].rearrange("p (e i) -> p e i", i=EI),
                     d["L1_ffn_down_proj"][:, nb * P:(nb + 1) * P, :].rearrange("e p i -> p e i")).then_inc(k.moe_in, 16)
    sp.dma_start(k.raw_d[:, :, MC * P:], rows_of(d["L1_ffn_shared_down_w"])).then_inc(k.moe_in, 16)
    sp.dma_start(k.raw_r[:, :], d["L1_ffn_router_w"]).then_inc(k.moe_in, 16)
    sp.dma_start(k.ebias[:, :], d["L1_ffn_e_bias"].partition_broadcast(P)).then_inc(k.moe_in, 16)
    sp.dma_start(k.iota[:, :], d["c_iota"]).then_inc(k.moe_in, 16)
    sp.dma_start(k.expert[:, :], d["c_expert"]).then_inc(k.moe_in, 16)
    k.moe_loads = loads + 2 + KC + 5


def setup(k):
    nc, d = k.nc, k.dram
    k.raw = {n: k.raw_first[:, i] for i, n in enumerate(ATT_RAW[0:4])}
    k.raw.update({n: k.raw_att[:, i] for i, n in enumerate(ATT_RAW[4:])})
    k.w1_bqk, k.w1_bv, k.w1_bo = k.sb("w1_bqk", [P, 4]), k.sb("w1_bv", [P, D]), k.sb("w1_bo", [P, D])
    k.w2_bq, k.w2_bk, k.w2_bv, k.w2_bo = k.sb("w2_bq", [P, D]), k.sb("w2_bk", [P, 2]), k.sb("w2_bv", [P, D]), k.sb("w2_bo", [P, D])
    k.bias_in, k.ffn_in, k.moe_in = k.sem("bias_in"), k.sem("ffn_in"), k.sem("moe_in")
    k.first_in, k.ctx_in, k.att_in, k.made = k.sem("first_in"), k.sem("ctx_in"), k.sem("att_in"), k.sem("made")
    with nc.Block() as block:
        @block.sync
        def _(sp):
            for n in ATT_RAW[0:4]:
                sp.dma_start(k.raw[n][:, :, :], rows_of(d[n])).then_inc(k.first_in, 16)
            sp.dma_start(k.ident[:, :], d["c_ident"]).then_inc(k.first_in, 16)
            sp.dma_start(k.x[:, :, :], tiles_of(d["x"])).then_inc(k.first_in, 16)
            sp.dma_start(k.rope[:, :, :], d["c_rope"].rearrange("p (a f) -> p a f", a=2)).then_inc(k.first_in, 16)
            sp.dma_start(k.causal[:, :], d["c_causal"]).then_inc(k.first_in, 16)
            sp.dma_start(k.parity[:, :], d["c_parity"]).then_inc(k.first_in, 16)
            sp.wait_ge(k.first_in, 9 * 16)

        @block.vector
        def _(dve):
            nc.vector.memset(k.halfpow[:, :], -0.5)
            nc.vector.memset(k.zero[:, :], 0.0)
            nc.vector.memset(k.ones[:, :], 1.0)
            nc.vector.memset(k.unround[:, :], -ROUND)
            for s in range(2):
                ins = nc.vector.memset(k.vblk[s][:, :, :, :], 0.0)
            ins.then_inc(k.made, 1)
            dve.wait_ge(k.made, 1)
            for s in range(2):
                nc.vector.memset(k.vblk[s][0:64, :, :, 32:33], 1.0)
                nc.vector.memset(k.vblk[s][64:128, :, :, 33:34], 1.0)
            dve.wait_ge(k.first_in, 9 * 16)
            nc.vector.tensor_copy(k.identb[:, :], k.ident[:, :])


def load_later_weights(k, sp):
    nc, d = k.nc, k.dram
    sp.dma_start(k.ctx[:, :, :], tiles_of(d["ctx_2048"])).then_inc(k.ctx_in, 16)
    sp.dma_start(k.place[:, :], d["c_place"]).then_inc(k.ctx_in, 16)
    sp.dma_start(k.mask[:, :, :], tiles_of(d["mask_BxSxS2_ff0"])).then_inc(k.ctx_in, 16)
    for n in ATT_RAW[4:]:
        sp.dma_start(k.raw[n][:, :, :], rows_of(d[n])).then_inc(k.att_in, 16)
    for buf, n in ((k.w1_bv, "L1_attn_bv"), (k.w1_bo, "L1_attn_bo"), (k.w2_bq, "L1_xattn_bq"), (k.w2_bv, "L1_xattn_bv"), (k.w2_bo, "L1_xattn_bo"), (k.gamma, "L0_xattn_gamma")):
        sp.dma_start(buf[:, :], d[n].partition_broadcast(P)).then_inc(k.bias_in, 16)
    with nc.allow_non_contiguous_dma(reason="256 biases, one to a partition"):
        for buf, n in ((k.w1_bqk[:, 0:2], "L1_attn_bq"), (k.w1_bqk[:, 2:4], "L1_attn_bk"), (k.w2_bk[:, :], "L1_xattn_bk")):
            sp.dma_start(buf, d[n].rearrange("(c p) -> p c", p=P)).then_inc(k.bias_in, 16)
    for n, i in (("L0_ffn_w_gate", "gate"), ("L0_ffn_w_up", "up")):
        sp.dma_start(k.w_ffn[i], rows_of(d[n])).then_inc(k.ffn_in, 16)
    sp.dma_start(k.w_ffn["down"].rearrange("p g i n -> p g (i n)"),
                 d["L0_ffn_w_down"].rearrange("(g p i) n -> p g (i n)", g=GB, i=PL)).then_inc(k.ffn_in, 16)
    sp.wait_ge(k.ctx_in, 3 * 16)
    sp.wait_ge(k.bias_in, 9 * 16)


def quantise_weights(k, raws, scales):
    nc = k.nc
    steps_done, diag_ready, spread_done = (k.sem("wq_" + n) for n in "steps_done diag_ready spread_done".split())
    with nc.Block() as block:
        @block.vector
        def _(dve):
            dve.wait_ge(k.att_in, 8 * 16)
            own = Steps(dve, steps_done, 0, 7)
            for i, raw in enumerate(raws):
                nc.vector.tensor_reduce(k.wabs[:, 2 * i:2 * i + 2], raw[:, :, :], AX.X, ALU.max, apply_absolute_value=True)
            for by, bk in ((k.w1_bkm, k.w1_bqk[:, 2:4]), (k.w2_bkm, k.w2_bk[:, :])):
                for par in range(2):
                    nc.vector.tensor_scalar(by[:, par, :], bk, k.parity[:, par:par + 1], None, ALU.mult)
            n = 2 * len(raws)
            own(nc.vector.memset(k.pause[:, :], 0.0))
            own(nc.vector.tensor_scalar(k.wscale[:, 0:n], k.wabs[:, 0:n], 1.0 / 127.0, Q_EPS, ALU.mult, ALU.max))
            own(nc.vector.reciprocal(k.wabs[:, 0:n], k.wscale[:, 0:n]))
            for first, last, op0, op1 in ((None, ROUND, ALU.mult, ALU.add), (ROUND, 127.0, ALU.subtract, ALU.min), (-127.0, None, ALU.max, None)):
                for i, raw in enumerate(raws):
                    for j in range(KC):
                        row = raw[:, j, :]
                        by = k.wabs[:, 2 * i + j:2 * i + j + 1] if first is None else first
                        ins = nc.vector.tensor_scalar(row, row, by, last, op0, *([op1] if op1 else []))
                own(ins)
            for i in range(n):
                ins = nc.vector.tensor_scalar(k.diag[:, i, :], k.ident[:, :], k.wscale[:, i:i + 1], None, ALU.mult)
            ins.then_inc(diag_ready, 1)
            dve.wait_ge(spread_done, 1)
            for i, scale in enumerate(scales):
                ins = nc.vector.tensor_copy(scale[:, :], k.psum[:, i, 0:D])
            own(ins)
            own.end()

        @block.tensor
        def _(pe):
            pe.wait_ge(diag_ready, 1)
            for i in range(2 * len(raws)):
                last = nc.tensor.matmul(k.psum[:, i // 2, (i % 2) * P:(i % 2 + 1) * P], k.ones[:, :], k.diag[:, i, :], start=True, stop=True)
            last.then_inc(spread_done, 1)


def attention_weights(k, w0):
    nc, d, raw, sb = k.nc, k.dram, k.raw, k.sb
    k.w1_bkm, k.w2_bkm = sb("w1_bkm", [P, 2, 2]), sb("w2_bkm", [P, 2, 2])
    w1 = {"qk": w0["qk"], "v": w0["v"], "o": w0["o"], "bq": k.w1_bqk[:, 0:2], "bkm": k.w1_bkm, "bv": k.w1_bv, "bo": k.w1_bo}
    w2 = {"q": sb("w2_q", [P, KC, D], BF16), "k": sb("w2_k", [P, KC, D]), "v": sb("w2_v", [P, KC, D]), "o": sb("w2_o", [P, KC, D], BF16),
          "swq": sb("w2_swq", [P, D]), "swo": sb("w2_swo", [P, D]), "bq": k.w2_bq, "bkm": k.w2_bkm, "bv": k.w2_bv, "bo": k.w2_bo}
    k.wabs, k.wscale, k.diag = sb("wabs", [P, 4]), sb("wscale", [P, 4]), sb("diag", [P, 4, P])
    quantise_weights(k, [raw["L1_xattn_wq"], raw["L1_xattn_wo"]], [w2["swq"], w2["swo"]])
    groups = []
    for n, dst in (("L1_attn_Wq", w1["qk"][:, :, 0:D]), ("L1_attn_Wk", w1["qk"][:, :, D:2 * D]), ("L1_attn_Wv", w1["v"]), ("L1_attn_Wo", w1["o"]),
                   ("L1_xattn_wq", w2["q"]), ("L1_xattn_wk", w2["k"]), ("L1_xattn_wv", w2["v"]), ("L1_xattn_wo", w2["o"])):
        groups += square_groups(raw[n], dst)
    transpose_weights(k, "w1", groups)
    return w1, w2


def decoder(nc, dram, out, layers="012345"):
    ctx = ExitStack()
    with ctx:
        k = allocate(nc, ctx, dram)
        setup(k)
        w0 = {"qk": k.sb("w0_qk", [P, KC, 2 * D]), "v": k.sb("w0_v", [P, KC, D]), "o": k.sb("w0_o", [P, KC, D])}
        raw = k.raw
        if "0" in layers:
            transpose_weights(k, "w0", square_groups(raw["L0_attn_Wq"], w0["qk"][:, :, 0:D]) + square_groups(raw["L0_attn_Wk"], w0["qk"][:, :, D:2 * D])
                              + square_groups(raw["L0_attn_Wv"], w0["v"]) + square_groups(raw["L0_attn_Wo"], w0["o"]))
            attention(k, "a0", ROPE, w0, lambda sp: load_later_weights(k, sp), lambda pool: set_ones(k, pool))
        if "1" in layers:
            channel_attention(k)
        if "2" in layers:
            sparse_ffn(k, k.w_ffn)
        if "3" in layers:
            release(k, "c0")
            w1, w2 = attention_weights(k, w0)
        if "3" in layers:
            attention(k, "a1", SELF, w1, lambda sp: load_experts(k, sp))
            attention(k, "a2", CROSS, w2)
        expert_weights(k)
        experts(k, out)



LAYERS = "012345"
_INS = ['x', 'ctx_2048', 'mask_BxSxS2_ff0', 'L0_attn_Wq', 'L0_attn_Wk', 'L0_attn_Wv', 'L0_attn_Wo', 'L0_xattn_gamma',
        'L0_ffn_w_gate', 'L0_ffn_w_up', 'L0_ffn_w_down', 'L1_attn_Wq', 'L1_attn_bq', 'L1_attn_Wk', 'L1_attn_bk',
        'L1_attn_Wv', 'L1_attn_bv', 'L1_attn_Wo', 'L1_attn_bo', 'L1_xattn_wq', 'L1_xattn_bq', 'L1_xattn_wk',
        'L1_xattn_bk', 'L1_xattn_wv', 'L1_xattn_bv', 'L1_xattn_wo', 'L1_xattn_bo', 'L1_ffn_router_w', 'L1_ffn_e_bias',
        'L1_ffn_gate_up_proj', 'L1_ffn_down_proj', 'L1_ffn_shared_gate_w', 'L1_ffn_shared_up_w', 'L1_ffn_shared_down_w']


def kernel(**inputs):
    import concourse.bacc as bacc
    from concourse.bass_utils import run_bass_kernel_spmd as run

    nc = bacc.Bacc("TRN2", target_bir_lowering=False, num_devices=1)
    arrays, dram = {}, {}
    for name, a in {**{n: inputs[n] for n in _INS}, **constants()}.items():
        a = np.ascontiguousarray(a)
        arrays[name + "_dram"] = a
        dram[name] = nc.dram_tensor(name + "_dram", a.shape, mybir.dt.from_np(a.dtype), kind="ExternalInput").ap()
    out = nc.dram_tensor("out_dram", (B, S, D), F32, kind="ExternalOutput").ap()
    decoder(nc, dram, out, LAYERS)
    return run(nc, [arrays], core_ids=[0]).results[0]["out_dram"]
```

```python
import numpy as np
import concourse.bass as bass
from concourse import mybir
from contextlib import ExitStack

F32 = mybir.dt.float32
BF16 = mybir.dt.bfloat16
U32 = mybir.dt.uint32
ALU = mybir.AluOpType
ACT = mybir.ActivationFunctionType
AX = mybir.AxisListType

P = 128
B, S, D = 16, 64, 256
TILES = B * S // P
KC = D // P
H, HD = 16, 16
PAIRS = H // 2
NEG = -1e30
LN_EPS = 1e-5
Q_EPS = 1e-8
ROUND = 1.5 * 2.0 ** 23
XH, XD = 8, 8
XP = P // XD
XG = 2
XV = 32
XC = 4 * XD + 4
XR = 9 * XD
I0 = 1024
E, EI, TOPK = 16, 96, 4
PL = 4
GB = I0 // (PL * P)
HALF = 4
MC = E * EI // P
MCS = MC + 1


def constants():
    pos = np.arange(S, dtype=np.float32)
    inv = (1.0 / np.float32(10000.0) ** (np.arange(0, HD, 2, dtype=np.float32) / np.float32(HD))).astype(np.float32)
    ang = np.outer(pos, inv).astype(np.float32)
    cos, sin = np.cos(ang).astype(np.float32), np.sin(ang).astype(np.float32)
    cs = np.stack([cos, cos], -1).reshape(S, HD)
    sn = np.stack([-sin, sin], -1).reshape(S, HD)
    causal = np.where(np.tril(np.ones((S, S), bool)), 0.0, NEG).astype(np.float32)
    head = np.arange(P) // HD
    unit = np.arange(MC * P) // EI
    row, token, pair = np.arange(P)[:, None], np.arange(4 * XD)[None, :], np.arange(4)[None, :]
    place = (row // XV == token // XD) & (row % XV == token % XD)
    total = (row // XV == pair) & (row % XV == XD)
    return {
        "c_ident": np.eye(P, dtype=np.float32),
        "c_rope": np.tile(np.concatenate([cs, sn], 1), (2, 1)).astype(np.float32),
        "c_causal": np.tile(causal, (2, 1)),
        "c_parity": np.stack([head % 2 == 0, head % 2 == 1], 1).astype(np.float32),
        "c_place": np.concatenate([place, total], 1).astype(np.float32),
        "c_iota": np.tile(np.arange(E, dtype=np.float32), (P, 1)),
        "c_expert": np.tile(unit[None, :] == np.arange(E)[:, None], (3, 1)).astype("bfloat16"),
    }


class Kit:
    pass


def allocate(nc, ctx, dram):
    k = Kit()
    k.nc, k.dram = nc, dram

    def sb(name, shape, dt=F32):
        return ctx.enter_context(nc.sbuf_tensor(name, shape, dt))

    k.layer_sems = {}

    def sem(name):
        handle = nc.alloc_semaphore(name=name)
        k.layer_sems.setdefault(name.split("_")[0], []).append(handle)
        return handle

    k.sb, k.sem = sb, sem
    k.x = sb("x", [P, TILES, D])
    k.ctx = sb("ctx", [P, TILES, D])
    k.ident = sb("ident", [P, P])
    k.identb = sb("identb", [P, P], BF16)
    k.rope = sb("rope", [P, 2, HD])
    k.causal = sb("causal", [P, S])
    k.parity = sb("parity", [P, 2])
    k.halfpow = sb("halfpow", [P, 1])
    k.zero = sb("zero", [P, 1])
    k.ones = sb("ones", [P, P])
    k.psum = ctx.enter_context(nc.psum_tensor("psum", [P, 8, 512], F32))
    k.stats = sb("stats", [P, 2, 6])
    k.moments = sb("moments", [P, 2, 2])
    k.varplus = sb("varplus", [P, 2, 1])
    k.pause = sb("pause", [P, 1])
    k.unround = sb("unround", [P, 1])
    k.rstd = sb("rstd", [P, 2, 1])
    k.xn = [sb(f"xn{s}", [P, D]) for s in range(2)]
    k.xnT = [sb(f"xnT{s}", [P, KC, P]) for s in range(2)]
    k.xqT = [sb(f"xqT{s}", [P, KC, P], BF16) for s in range(2)]
    k.ctxs = [sb(f"ctxs{s}", [P, D]) for s in range(2)]
    k.ctxT = [sb(f"ctxT{s}", [P, KC, P]) for s in range(2)]
    k.qk = [sb(f"qk{s}", [P, 2 * D]) for s in range(2)]
    k.qkT = [sb(f"qkT{s}", [P, 4, P]) for s in range(2)]
    k.kTm = [sb(f"kTm{s}", [P, 2, 2, P]) for s in range(2)]
    k.probs = [sb(f"probs{s}", [P, H * S]) for s in range(2)]
    k.pT = [sb(f"pT{s}", [P, PAIRS, P]) for s in range(2)]
    k.vblk = [sb(f"vblk{s}", [P, 2, PAIRS, 34]) for s in range(2)]
    k.on = [sb(f"on{s}", [P, D]) for s in range(2)]
    k.oT = [sb(f"oT{s}", [P, KC, P]) for s in range(2)]
    k.oTb = [sb(f"oTb{s}", [P, KC, P], BF16) for s in range(2)]
    k.rot = sb("rot", [P, 2 * D])
    k.ytmp = sb("ytmp", [P, D])
    k.rowmax = sb("rowmax", [P, 2, H])
    k.rsum = sb("rsum", [P, 2, PAIRS, 2])
    k.qscr = sb("qscr", [P, 2])
    k.sx = sb("sx", [P, 2, 1])
    k.so = sb("so", [P, 2, 1])
    k.mask = sb("mask", [P, TILES, S])
    k.gamma = sb("gamma", [P, 1])
    k.xsrc = [k.qkT[s][:, :, :].rearrange("p (a b) n -> p a (b n)", a=2) for s in range(2)]
    k.xpart = [sb(f"xpart{s}", [P, 3, 2, D], BF16) for s in range(2)]
    k.rest = k.rot[:, :].rearrange("p (a n) -> p a n", a=2)
    k.vT = [k.pT[s][:, :, :].rearrange("p a n -> p (a n)").rearrange("p (c a d) -> p c a d", c=KC, d=XV) for s in range(2)]
    k.xout = [k.qk[s][:, :] for s in range(2)]
    k.place = sb("place", [P, XC])
    k.xrs = sb("xrs", [P, KC, 4, 4, 1])
    k.negmax = sb("negmax", [P, 2 * XP])
    k.mpart = [sb(f"mpart{s}", [P, P // XP, XP], BF16) for s in range(2)]
    k.mrow = [sb(f"mrow{s}", [3 * XP, P], BF16) for s in range(2)]
    k.ffn_s = [k.probs[s][:, 0:PL * P] for s in range(2)]
    k.ffn_h = [k.probs[s][:, PL * P:2 * PL * P].rearrange("p (i n) -> p i n", i=PL) for s in range(2)]
    k.ffn_a = [k.pT[s][:, 0:PL, :] for s in range(2)]
    k.near, k.over, k.far = sb("near", [P, 3, P], BF16), sb("over", [P, 2, P], BF16), sb("far", [P, 1, P], BF16)
    k.outer, k.inner = sb("outer", [P, 2, P], BF16), sb("inner", [P, 2, P], BF16)
    region_a = sb("region_a", [P, 2 * MCS * D])
    k.raw_att = region_a[:, 0:8 * KC * D].rearrange("p (w k n) -> p w k n", w=8, k=KC)
    k.raw_gu = region_a[:, :].rearrange("p (u c n) -> p u c n", u=2, n=D)
    k.hid = region_a[:, :].rearrange("p (c n) -> p c n", n=HALF * P)
    operands = 2 * 2 * XP * D // 2
    region_b = sb("region_b", [P, max(operands + 2 * XG * KC * D, 2 * KC * MCS * P + MCS * D)])
    k.raw_first = region_b[:, 0:4 * KC * D].rearrange("p (w k n) -> p w k n", w=4, k=KC)
    both = region_b[:, 0:operands].bitcast(BF16).rearrange("p (o s a n) -> p o s a n", o=2, s=2, a=XP)
    k.qop, k.kop = [both[:, 0, s] for s in range(2)], [both[:, 1, s] for s in range(2)]
    k.xprob = [region_b[:, operands + s * XG * KC * D:operands + (s + 1) * XG * KC * D].rearrange("p (a c n) -> p a c n", a=XG, c=KC) for s in range(2)]
    k.wgu = region_b[:, 0:2 * KC * MCS * P].rearrange("p (k u n) -> p k u n", k=KC, u=2)
    k.wd = region_b[:, 2 * KC * MCS * P:].rearrange("p (c n) -> p c n", n=D)
    region_c = sb("region_c", [P, KC * TILES * P + 1024 + KC * (MC * P + EI)])
    assert 3 * KC * I0 <= KC * TILES * P + 1024 + KC * (MC * P + EI)
    k.w_ffn = {"gate": region_c[:, 0:KC * I0].rearrange("p (k n) -> p k n", k=KC),
               "up": region_c[:, KC * I0:2 * KC * I0].rearrange("p (k n) -> p k n", k=KC),
               "down": region_c[:, 2 * KC * I0:3 * KC * I0].rearrange("p (g i n) -> p g i n", g=GB, i=PL)}
    k.xall = region_c[:, 0:KC * TILES * P].rearrange("p (k t n) -> p k t n", k=KC, t=TILES)
    k.sg = [region_c[:, 2048 + g * 512:2560 + g * 512] for g in range(2)]
    k.m_stats, k.m_moments, k.m_rstd = sb("m_stats", [P, TILES, 6]), sb("m_moments", [P, TILES, 2]), sb("m_rstd", [P, TILES, 1])
    k.raw_d = region_c[:, KC * TILES * P + 1024:].rearrange("p (k n) -> p k n", k=KC)
    k.raw_r, k.wr = sb("raw_r", [E, D]), sb("wr", [P, KC, E])
    k.score, k.pick = sb("score", [P, TILES * E]), sb("pick", [P, TILES * E])
    k.ebias, k.iota = sb("ebias", [P, E]), sb("iota", [P, E])
    k.best, k.besti, k.bestf = sb("best", [P, TILES, 8]), sb("besti", [P, TILES, 8], U32), sb("bestf", [P, TILES, TOPK])
    k.hit, k.wsum = sb("hit", [P, TILES, TOPK, E]), sb("wsum", [P, TILES, 2])
    k.parts = sb("parts", [P, TILES, 3, E], BF16)
    k.combT, k.expert = sb("combT", [3 * E, TILES * P], BF16), sb("expert", [3 * E, MC * P], BF16)
    return k


def wait(eng, sem, value):
    if isinstance(value, int) and value <= 0:
        return
    eng.wait_ge(sem, value)


def release(k, layer):
    k.nc.clear_and_free_semaphores(k.layer_sems.pop(layer))
    k.nc.all_engine_barrier()


class Steps:

    def __init__(self, eng, sem, t, per):
        self.eng, self.sem, self.t, self.per, self.n = eng, sem, t, per, 0

    def __call__(self, ins):
        self.n += 1
        ins.then_inc(self.sem, 1)
        self.eng.wait_ge(self.sem, self.t * self.per + self.n)

    def end(self):
        assert self.n == self.per, (self.n, self.per)


def pipeline(eng, tile):
    tile(0, 0, None, None)
    tile(1, 1, 0, 0)
    with eng.Fori(0, TILES // 2 - 1) as i:
        tile(2 * i + 2, 0, 2 * i + 1, 1)
        tile(2 * i + 3, 1, 2 * i + 2, 0)
    tile(None, None, TILES - 1, 1)



def norm_moments(k, nc, steps, t, s, stats_ready):
    steps(nc.vector.bn_stats(k.stats[:, s, :], k.x[:, t, :]))
    nc.vector.memset(k.pause[:, :], 0.0)
    steps(nc.vector.bn_aggr(k.moments[:, s, :], k.stats[:, s, :]))
    nc.vector.tensor_scalar(k.varplus[:, s, :], k.moments[:, s, 1:2], LN_EPS, None, ALU.add).then_inc(stats_ready, 1)


def norm_rstd(k, nc, pool, t, s, stats_ready, rstd_ready):
    pool.wait_ge(stats_ready, t + 1)
    nc.gpsimd.tensor_tensor(k.rstd[:, s, :], k.varplus[:, s, :], k.halfpow[:, :], ALU.pow).then_inc(rstd_ready, 1)



class WeightTurning:

    def __init__(self, k, name, groups, by_dve=()):
        self.nc, self.psum, self.ident, self.groups = k.nc, k.psum, k.ident, groups
        self.turned = k.sem(name + "_turned")
        self.by_act, self.by_dve = k.sem(name + "_by_act"), k.sem(name + "_by_dve")
        self.copied, counts = [], {"act": 0, "dve": 0}
        for g in range(len(groups)):
            who = "dve" if g in by_dve else "act"
            counts[who] += 1
            self.copied.append((who, counts[who]))

    def groups_of(self, engine):
        return sum(who == engine for who, _ in self.copied)

    def out_of(self, g):
        blocks, dst = self.groups[g]
        rows, cols = blocks[0].shape
        src = self.psum[0:cols, g % 4, 0:len(blocks) * P].rearrange("p (j r) -> p j r", r=P)[:, :, 0:rows]
        return dst, src

    def tensor(self, pe, first=0, last=None):
        for g in range(first, len(self.groups) if last is None else last):
            if g >= 4:
                who, count = self.copied[g - 4]
                pe.wait_ge(self.by_act if who == "act" else self.by_dve, count)
            for j, b in enumerate(self.groups[g][0]):
                rows, cols = b.shape
                ins = self.nc.tensor.transpose(self.psum[0:cols, g % 4, j * P:j * P + rows], b, self.ident[0:rows, 0:rows])
            ins.then_inc(self.turned, 1)

    def scalar(self, act, first=0, last=None):
        for g, (who, _) in enumerate(self.copied):
            if who == "act" and first <= g < (len(self.groups) if last is None else last):
                act.wait_ge(self.turned, g + 1)
                dst, src = self.out_of(g)
                self.nc.scalar.activation(dst, src, ACT.Copy).then_inc(self.by_act, 1)

    def vector(self, dve):
        for g, (who, _) in enumerate(self.copied):
            if who == "dve":
                dve.wait_ge(self.turned, g + 1)
                dst, src = self.out_of(g)
                self.nc.vector.tensor_copy(dst, src).then_inc(self.by_dve, 1)


def transpose_weights(k, name, groups):
    turning = WeightTurning(k, name, groups, by_dve=range(1, len(groups), 2))
    with k.nc.Block() as block:
        @block.tensor
        def _(pe):
            turning.tensor(pe)

        @block.scalar
        def _(act):
            turning.scalar(act)

        @block.vector
        def _(dve):
            turning.vector(dve)


def square_groups(raw, dst):
    return [([raw[:, j, kc * P:(kc + 1) * P] for j in range(KC)],
             dst[:, kc, :].rearrange("p (j n) -> p j n", n=P)) for kc in range(KC)]



ROPE, SELF, CROSS = "rope", "self", "cross"


def pipeline5(eng, iteration):
    def stages(i):
        return [i - d if 0 <= i - d < TILES else None for d in range(5)]
    for i in range(4):
        iteration(*stages(i), i % 2)
    with eng.Fori(0, TILES // 2 - 2) as i:
        for j in range(2):
            iteration(*(2 * i + (4 + j - d) for d in range(5)), j)
    for i in range(TILES, TILES + 4):
        iteration(*stages(i), i % 2)


def attention(k, name, kind, w, load=None, fill=None):
    nc, sem = k.nc, k.sem
    bf = kind == CROSS
    names = ("stats_ready rstd_ready xn_ready xT_turned xnT_ready qk_done v_done q_ready qkT_turned qT_ready kTm_ready "
             "scores_done softmax_in exp_done pT_turned pT_ready v_ready pv_done on_ready oT_turned oT_ready y_done "
             "x_done norm_steps q_steps masked max_ready last_steps ctx_ready ctx_turned ctxT_ready bias_added").split()
    m = {n: sem(f"{name}_{n}") for n in names}
    (stats_ready, rstd_ready, xn_ready, xT_turned, xnT_ready, qk_done, v_done, q_ready, qkT_turned, qT_ready, kTm_ready,
     scores_done, softmax_in, exp_done, pT_turned, pT_ready, v_ready, pv_done, on_ready, oT_turned, oT_ready, y_done,
     x_done, norm_steps, q_steps, masked, max_ready, last_steps, ctx_ready, ctx_turned, ctxT_ready, bias_added) = (m[n] for n in names)
    SC = k.psum[:, 0:4, :]
    TB, QK, VB, OB = (k.psum[:, b, :] for b in range(4, 8))
    xnT = k.xqT if bf else k.xnT
    scale = 1.0 if bf else 0.25
    norm_per = {ROPE: 2, SELF: 2, CROSS: 7}[kind]
    last_per = {ROPE: 1, SELF: 2, CROSS: 8}[kind]

    with nc.Block() as block:
        @block.sync
        def _(sp):
            if load is not None:
                load(sp)

        @block.gpsimd
        def _(pool):
            def less_maximum(t, s):
                pool.wait_ge(max_ready, t + 1)
                flat = k.probs[s][:, :].rearrange("p (h n) -> p h n", n=S)
                nc.gpsimd.tensor_tensor(flat, flat, k.rowmax[:, s, :].unsqueeze(2).broadcast_to([P, H, S]), ALU.subtract).then_inc(softmax_in, 1)
                pool.wait_ge(softmax_in, t + 1)

            def add_bias(t):
                pool.wait_ge(xn_ready, t + 1)
                nc.gpsimd.tensor_tensor(k.x[:, t, :], k.x[:, t, :], w["bo"][:, :], ALU.add).then_inc(bias_added, 1)
                pool.wait_ge(bias_added, t + 1)

            def iteration(tn, tf, ts, tb, tl, s):
                if tn is not None:
                    norm_rstd(k, nc, pool, tn, s, stats_ready, rstd_ready)
                    pool.wait_ge(rstd_ready, tn + 1)
                if ts is not None and kind == CROSS:
                    less_maximum(ts, s)
                if tn is not None and kind != ROPE:
                    add_bias(tn)
            pipeline5(pool, iteration)
            if fill is not None:
                pool.wait_ge(rstd_ready, TILES)
                fill(pool)

        @block.tensor
        def _(pe):
            def products(t, s):
                if kind == CROSS:
                    pe.wait_ge(ctxT_ready, t + 1)
                    wait(pe, kTm_ready, t)
                    for c in range(2):
                        for kc in range(KC):
                            last = nc.tensor.matmul(QK[:, c * P:(c + 1) * P], w["k"][:, kc, c * P:(c + 1) * P],
                                                    k.ctxT[s][:, kc, :], start=kc == 0, stop=kc == KC - 1)
                    last.then_inc(qk_done, 1)
                    pe.wait_ge(xnT_ready, t + 1)
                    wait(pe, q_ready, t)
                    wait(pe, v_ready, t)
                    for kc in range(KC):
                        nc.tensor.matmul(VB[:, D:2 * D], xnT[s][:, kc, :], w["q"][:, kc, :], start=kc == 0, stop=kc == KC - 1)
                else:
                    pe.wait_ge(xnT_ready, t + 1)
                    wait(pe, q_ready if kind == ROPE else kTm_ready, t)
                    if kind == ROPE:
                        for kc in range(KC):
                            last = nc.tensor.matmul(QK, xnT[s][:, kc, :], w["qk"][:, kc, :], start=kc == 0, stop=kc == KC - 1)
                    else:
                        for c in range(4):
                            for kc in range(KC):
                                last = nc.tensor.matmul(QK[:, c * P:(c + 1) * P], w["qk"][:, kc, c * P:(c + 1) * P],
                                                        xnT[s][:, kc, :], start=kc == 0, stop=kc == KC - 1)
                    last.then_inc(qk_done, 1)
                    wait(pe, v_ready, t)
                src = k.ctxT[s] if kind == CROSS else xnT[s]
                for kc in range(KC):
                    last = nc.tensor.matmul(VB[:, 0:D], src[:, kc, :], w["v"][:, kc, :], start=kc == 0, stop=kc == KC - 1)
                last.then_inc(v_done, 1)

            def turn_out(t, s):
                pe.wait_ge(on_ready, t + 1)
                for kc in range(KC):
                    last = nc.tensor.transpose(OB[:, kc * P:(kc + 1) * P], k.on[s][:, kc * P:(kc + 1) * P], k.ident[:, :])
                last.then_inc(oT_turned, 1)

            def turn_probs(t, s):
                pe.wait_ge(exp_done, t + 1)
                for r in range(4):
                    for hh in range(2):
                        c = s * 256 + hh * P
                        last = nc.tensor.transpose(SC[:, r, c:c + P], k.probs[s][:, (r * 2 + hh) * P:(r * 2 + hh + 1) * P], k.ident[:, :])
                    if r % 2 == 1:
                        last.then_inc(pT_turned, 1)

            def project(t, s):
                pe.wait_ge(oT_ready, t + 1)
                for kc in range(KC):
                    last = nc.tensor.matmul(OB[:, D:2 * D], (k.oTb if bf else k.oT)[s][:, kc, :], w["o"][:, kc, :],
                                            start=kc == 0, stop=kc == KC - 1)
                last.then_inc(y_done, 1)

            def turn_qk(t, s):
                pe.wait_ge(q_ready, t + 1)
                for c in range(4 if kind == ROPE else 2):
                    last = nc.tensor.transpose(TB[:, c * P:(c + 1) * P], k.qk[s][:, c * P:(c + 1) * P], k.ident[:, :])
                last.then_inc(qkT_turned, 1)

            def turn_x(t, s):
                pe.wait_ge(xn_ready, t + 1)
                if kind == SELF:
                    wait(pe, xnT_ready, t)
                elif kind == ROPE:
                    wait(pe, kTm_ready, t)
                else:
                    pe.wait_ge(ctxT_ready, t + 1)
                for kc in range(KC):
                    last = nc.tensor.transpose(TB[:, kc * P:(kc + 1) * P], k.xn[s][:, kc * P:(kc + 1) * P], k.ident[:, :])
                last.then_inc(xT_turned, 1)

            def turn_context(t, s):
                pe.wait_ge(ctx_ready, t + 1)
                wait(pe, qT_ready, t)
                for kc in range(KC):
                    last = nc.tensor.transpose(TB[:, (2 + kc) * P:(3 + kc) * P], k.ctxs[s][:, kc * P:(kc + 1) * P], k.ident[:, :])
                last.then_inc(ctx_turned, 1)

            def attend(t, s):
                pe.wait_ge(pT_ready, 2 * t + 2)
                pe.wait_ge(v_ready, t + 1)
                wait(pe, x_done, t)
                for p in range(PAIRS):
                    for b in range(2):
                        last = nc.tensor.matmul(OB[64 * b:64 * b + 64, 34 * p:34 * p + 34], k.pT[s][:, p, 64 * b:64 * b + 64],
                                                k.vblk[s][:, b, p, :], start=True, stop=True)
                last.then_inc(pv_done, 1)

            def scores(t, s):
                pe.wait_ge(qT_ready, t + 1)
                pe.wait_ge(kTm_ready, t + 1)
                wait(pe, masked, t)
                wait(pe, pT_ready, 2 * t - 2)
                for hh in range(2):
                    for r in range(4):
                        for b in range(2):
                            c = s * 256 + hh * P
                            last = nc.tensor.matmul(
                                SC[64 * b:64 * b + 64, r, c:c + P],
                                k.qkT[s][32 * r:32 * r + 32, hh, 64 * b:64 * b + 64],
                                k.kTm[s][32 * r:32 * r + 32, hh, :, 64 * b:64 * b + 64],
                                start=True, stop=True)
                last.then_inc(scores_done, 1)

            def iteration(tn, tf, ts, tb, tl, s):
                if tf is not None:
                    products(tf, 1 - s)
                if ts is not None:
                    pe.wait_ge(masked, ts + 1)
                if tb is not None:
                    turn_probs(tb, 1 - s)
                if tf is not None and kind == ROPE:
                    turn_qk(tf, 1 - s)
                if tl is not None:
                    turn_out(tl, s)
                if tf is not None and kind == CROSS:
                    turn_qk(tf, 1 - s)
                if tl is not None:
                    project(tl, s)
                if tn is not None and kind == CROSS:
                    turn_context(tn, s)
                if tf is not None:
                    scores(tf, 1 - s)
                if tn is not None and kind != CROSS:
                    turn_x(tn, s)
                if tb is not None:
                    attend(tb, 1 - s)
                if tn is not None and kind == CROSS:
                    turn_x(tn, s)
            pipeline5(pe, iteration)

        @block.scalar
        def _(act):
            def masked_k(t, s, srcs):
                for c, src in enumerate(srcs):
                    for par in range(2):
                        ins = nc.scalar.activation(k.kTm[s][:, c, par, :], src, ACT.Identity, bias=w["bkm"][:, par, c:c + 1], scale=k.parity[:, par:par + 1])
                ins.then_inc(kTm_ready, 1)

            def values(t, s):
                act.wait_ge(v_done, t + 1)
                if kind == CROSS:
                    act.wait_ge(q_ready, t + 1)
                wait(act, pv_done, t - 1)
                for par in range(2):
                    for b in range(2):
                        ins = nc.scalar.activation(k.vblk[s][64 * par:64 * par + 64, b, :, 16 * par:16 * par + 16],
                                                   VB[64 * b:64 * b + 64, 0:D].rearrange("k (p c d) -> k p c d", c=2, d=HD)[:, :, par, :],
                                                   ACT.Copy)
                ins.then_inc(v_ready, 1)

            def turned_q(t, s):
                act.wait_ge(qkT_turned, t + 1)
                wait(act, scores_done, t - 1)
                turned = TB.rearrange("p (c n) -> p c n", n=P)
                nc.scalar.activation(k.qkT[s][:, 0:2, :], turned[:, 0:2, :], ACT.Copy, scale=1.0 if kind == ROPE else 0.25).then_inc(qT_ready, 1)

            def turned_k(t, s):
                turned = TB.rearrange("p (c n) -> p c n", n=P)
                for par in range(2):
                    ins = nc.scalar.activation(k.kTm[s][:, :, par, :], turned[:, 2:4, :], ACT.Copy, scale=k.parity[:, par:par + 1])
                ins.then_inc(kTm_ready, 1)

            def products(t, s):
                if kind == SELF:
                    act.wait_ge(qk_done, t + 1)
                    wait(act, scores_done, t - 1)
                    for c in range(2):
                        ins = nc.scalar.activation(k.qkT[s][:, c, :], QK[:, c * P:(c + 1) * P], ACT.Identity, bias=w["bq"][:, c:c + 1])
                    ins.then_inc(qT_ready, 1)
                if kind == CROSS:
                    act.wait_ge(qk_done, t + 1)
                    wait(act, scores_done, t - 1)
                    masked_k(t, s, [QK[:, c * P:(c + 1) * P] for c in range(2)])

            def turned_out(t, s):
                act.wait_ge(oT_turned, t + 1)
                src = OB[:, 0:D].rearrange("p (k n) -> p k n", n=P)
                if bf:
                    nc.scalar.activation(k.oTb[s][:, :, :], src, ACT.Identity, bias=k.unround[:, :]).then_inc(oT_ready, 1)
                else:
                    nc.scalar.activation(k.oT[s][:, :, :], src, ACT.Copy).then_inc(oT_ready, 1)

            def turned_probs(t, s):
                wait(act, pv_done, t)
                for half in range(2):
                    act.wait_ge(pT_turned, 2 * t + half + 1)
                    banks = slice(2 * half, 2 * half + 2)
                    dst = k.pT[s][:, :, :].rearrange("p (h r) n -> p r h n", h=2)[:, banks, :, :]
                    src = SC[:, banks, s * 256:s * 256 + 256].rearrange("p r (h n) -> p r h n", h=2)
                    nc.scalar.activation(dst, src, ACT.Copy).then_inc(pT_ready, 1)

            def turned_context(t, s):
                act.wait_ge(ctx_turned, t + 1)
                wait(act, v_done, t - 1)
                nc.scalar.activation(k.ctxT[s][:, :, :], TB.rearrange("p (k n) -> p k n", n=P)[:, 2:4, :], ACT.Copy).then_inc(ctxT_ready, 1)

            def turned_x(t, s):
                act.wait_ge(xT_turned, t + 1)
                wait(act, v_done, t - 1)
                src = TB.rearrange("p (k n) -> p k n", n=P)
                if kind == CROSS:
                    nc.scalar.activation(xnT[s][:, :, :], src[:, 0:2, :], ACT.Identity, bias=k.unround[:, :]).then_inc(xnT_ready, 1)
                else:
                    nc.scalar.activation(xnT[s][:, :, :], src[:, 0:2, :], ACT.Copy).then_inc(xnT_ready, 1)

            def iteration(tn, tf, ts, tb, tl, s):
                if tn is not None and kind == CROSS:
                    wait(act, ctx_turned, tn - 1)
                    nc.scalar.activation(k.ctxs[s][:, :], k.ctx[:, tn, :], ACT.Copy).then_inc(ctx_ready, 1)
                if tf is not None:
                    products(tf, 1 - s)
                if tb is not None:
                    turned_probs(tb, 1 - s)
                if tf is not None and kind == ROPE:
                    turned_q(tf, 1 - s)
                if tl is not None:
                    turned_out(tl, s)
                if tf is not None and kind == CROSS:
                    turned_q(tf, 1 - s)
                if tf is not None and kind == ROPE:
                    turned_k(tf, 1 - s)
                if tn is not None and kind == CROSS:
                    turned_context(tn, s)
                if ts is not None:
                    act.wait_ge(softmax_in, ts + 1)
                    nc.scalar.activation(k.probs[s][:, :], k.probs[s][:, :], ACT.Exp, scale=scale).then_inc(exp_done, 1)
                if tn is not None:
                    turned_x(tn, s)
                if tf is not None:
                    values(tf, 1 - s)
            pipeline5(act, iteration)

        @block.vector
        def _(dve):
            def quantise(step, row, sx, scratch):
                step(nc.vector.tensor_reduce(scratch[:, 0:1], row, AX.X, ALU.max, apply_absolute_value=True))
                step(nc.vector.tensor_scalar(sx, scratch[:, 0:1], 1.0 / 127.0, Q_EPS, ALU.mult, ALU.max))
                step(nc.vector.reciprocal(scratch[:, 1:2], sx))
                step(nc.vector.tensor_scalar(row, row, scratch[:, 1:2], ROUND, ALU.mult, ALU.add))
                return nc.vector.tensor_scalar(row, row, ROUND + 127.0, ROUND - 127.0, ALU.min, ALU.max)

            def mask_scores(t, s):
                dve.wait_ge(scores_done, t + 1)
                sc = SC[:, :, s * 256:s * 256 + 256].rearrange("p r (g n) -> p r g n", n=S)
                pr = k.probs[s][:, :].rearrange("p (r g n) -> p r g n", r=4, n=S)
                msk = (k.mask[:, t, :] if kind == CROSS else k.causal[:, :]).unsqueeze(1).unsqueeze(1).broadcast_to([P, 4, 4, S])
                nc.vector.tensor_tensor(pr, sc, msk, ALU.add).then_inc(masked, 1)

            def maximum(t, s):
                dve.wait_ge(masked, t + 1)
                flat = k.probs[s][:, :].rearrange("p (h n) -> p h n", n=S)
                nc.vector.tensor_reduce(k.rowmax[:, s, :], flat, AX.X, ALU.max).then_inc(max_ready, 1)

            def less_maximum(t, s):
                dve.wait_ge(max_ready, t + 1)
                flat = k.probs[s][:, :].rearrange("p (h n) -> p h n", n=S)
                nc.vector.tensor_tensor(flat, flat, k.rowmax[:, s, :].unsqueeze(2).broadcast_to([P, H, S]), ALU.subtract).then_inc(softmax_in, 1)

            def normalise(t, s, own):
                dve.wait_ge(rstd_ready, t + 1)
                wait(dve, xT_turned, t - 1)
                ins = nc.vector.tensor_scalar(k.xn[s][:, :], k.x[:, t, :], k.moments[:, s, 0:1], k.rstd[:, s, :],
                                              ALU.subtract, ALU.mult)
                if kind == CROSS:
                    own(ins)
                    ins = quantise(own, k.xn[s][:, :], k.sx[:, s, :], k.qscr)
                ins.then_inc(xn_ready, 1)
                own.end()

            def finish_q(t, s):
                own = Steps(dve, q_steps, t, 1)
                dve.wait_ge(qk_done if kind == ROPE else v_done, t + 1)
                wait(dve, qkT_turned, t - 1)
                if kind == ROPE:
                    src = QK.rearrange("p (h f c) -> p h f c", f=HD // 2, c=2)
                    dst = k.rot[:, :].rearrange("p (h f c) -> p h f c", f=HD // 2, c=2)
                    cosv = k.rope[:, 0, :].unsqueeze(1).broadcast_to([P, 2 * H, HD])
                    sinv = k.rope[:, 1, :].rearrange("p (f c) -> p f c", c=2).unsqueeze(1).broadcast_to([P, 2 * H, HD // 2, 2])
                    nc.vector.tensor_tensor(k.qk[s][:, :].rearrange("p (h f) -> p h f", f=HD),
                                            QK.rearrange("p (h f) -> p h f", f=HD), cosv, ALU.mult)
                    nc.vector.tensor_tensor(dst[:, :, :, 0], src[:, :, :, 1], sinv[:, :, :, 0], ALU.mult)
                    own(nc.vector.tensor_tensor(dst[:, :, :, 1], src[:, :, :, 0], sinv[:, :, :, 1], ALU.mult))
                    nc.vector.tensor_tensor(k.qk[s][:, :], k.qk[s][:, :], k.rot[:, :], ALU.add).then_inc(q_ready, 1)
                else:
                    q = k.qk[s][:, 0:D]
                    own(nc.vector.scalar_tensor_tensor(q, VB[:, D:2 * D], k.sx[:, s, :], w["swq"][:, :], ALU.mult, ALU.mult))
                    nc.vector.tensor_tensor(q, q, w["bq"][:, :], ALU.add).then_inc(q_ready, 1)
                own.end()

            def finish_k(t, s):
                dve.wait_ge(qT_ready, t + 1)
                wait(dve, scores_done, t - 1)
                for c in range(2):
                    for par in range(2):
                        ins = nc.vector.tensor_scalar(k.kTm[s][:, c, par, :], QK[:, (2 + c) * P:(3 + c) * P], k.parity[:, par:par + 1],
                                                      w["bkm"][:, par, c:c + 1], ALU.mult, ALU.add)
                ins.then_inc(kTm_ready, 1)

            def divide(t, s, last):
                dve.wait_ge(pv_done, t + 1)
                ov = OB[:, 0:34 * PAIRS].rearrange("p (a c) -> p a c", c=34)
                last(nc.vector.reciprocal(k.rsum[:, s, :, :], ov[:, :, 32:34]))
                ins = nc.vector.tensor_tensor(k.on[s][:, :].rearrange("p (a c d) -> p a c d", c=2, d=HD),
                                              ov[:, :, 0:32].rearrange("p a (c d) -> p a c d", d=HD),
                                              k.rsum[:, s, :, :].unsqueeze(3).broadcast_to([P, PAIRS, 2, HD]), ALU.mult)
                if kind != ROPE:
                    last(ins)
                    ins = nc.vector.tensor_tensor(k.on[s][:, :], k.on[s][:, :], w["bv"][:, :], ALU.add)
                if kind == CROSS:
                    last(ins)
                    ins = quantise(last, k.on[s][:, :], k.so[:, s, :], k.qscr)
                ins.then_inc(on_ready, 1)

            def add_out(t, s, last):
                dve.wait_ge(y_done, t + 1)
                y = OB[:, D:2 * D]
                if kind == CROSS:
                    last(nc.vector.scalar_tensor_tensor(k.ytmp[:, :], y, k.so[:, s, :], w["swo"][:, :], ALU.mult, ALU.mult))
                    y = k.ytmp[:, :]
                if kind != ROPE:
                    dve.wait_ge(bias_added, t + 1)
                nc.vector.tensor_tensor(k.x[:, t, :], k.x[:, t, :], y, ALU.add).then_inc(x_done, 1)
                last.end()

            def iteration(tn, tf, ts, tb, tl, s):
                if ts is not None:
                    mask_scores(ts, s)
                if tf is not None and kind == ROPE:
                    finish_q(tf, 1 - s)
                if tl is not None:
                    last = Steps(dve, last_steps, tl, last_per)
                    divide(tl, s, last)
                if tf is not None and kind == CROSS:
                    finish_q(tf, 1 - s)
                if tn is not None:
                    norm = Steps(dve, norm_steps, tn, norm_per)
                    norm_moments(k, nc, norm, tn, s, stats_ready)
                if ts is not None:
                    maximum(ts, s)
                if tl is not None and kind == CROSS:
                    add_out(tl, s, last)
                if tn is not None:
                    normalise(tn, s, norm)
                if ts is not None and kind != CROSS:
                    less_maximum(ts, s)
                if tf is not None and kind == SELF:
                    finish_k(tf, 1 - s)
                if tl is not None and kind != CROSS:
                    add_out(tl, s, last)
            pipeline5(dve, iteration)



def pipeline3(eng, step, after_first=None):
    step(0, None, None, 0)
    if after_first is not None:
        after_first()
    step(1, 0, None, 1)
    step(2, 1, 0, 0)
    with eng.Fori(0, 2) as i:
        step(2 * i + 3, 2 * i + 2, 2 * i + 1, 1)
        step(2 * i + 4, 2 * i + 3, 2 * i + 2, 0)
    step(7, 6, 5, 1)
    step(None, 7, 6, 0)
    step(None, None, 7, 1)


def set_ones(k, pool):
    k.nc.gpsimd.memset(k.kop[0][64:96, :, :], 1.0).then_inc(k.made, 1)
    pool.wait_ge(k.made, 2)
    k.nc.gpsimd.memset(k.kop[1][64:96, :, :], 1.0)


def channel_attention(k, quantising, turning):
    assert TILES == 8
    nc, sem = k.nc, k.sem
    names = ("stats_ready rstd_ready src_ready highs_ready rests_ready mids_ready lows_ready "
             "written0 written1 first_loaded0 first_loaded1 last_loaded0 last_loaded1 ctx_turned v_ready "
             "s_done max_ready negmax_parts mt_turned mrow_ready first_rows_in last_rows_in st_done exp_done pv_done xout_ready placed on_ready oT_turned x_done "
             "front_steps part_steps back_steps context_ready ones_set sync_waits").split()
    (stats_ready, rstd_ready, src_ready, highs_ready, rests_ready, mids_ready, lows_ready,
     written0, written1, first_loaded0, first_loaded1, last_loaded0, last_loaded1, ctx_turned, v_ready,
     s_done, max_ready, negmax_parts, mt_turned, mrow_ready, first_rows_in, last_rows_in, st_done, exp_done, pv_done, xout_ready, placed, on_ready, oT_turned, x_done,
     front_steps, part_steps, back_steps, context_ready, ones_set, sync_waits) = (sem("c0_" + n) for n in names)
    written = [written0, written1]
    loaded = [[first_loaded0, first_loaded1], [last_loaded0, last_loaded1]]
    rows_in = [first_rows_in, last_rows_in]

    def nth(t, s, each):
        return (t - s) // 2 * each + each if isinstance(t, int) else t * (each // 2) + (each - s * (each // 2))
    SB = [k.psum[:, g, :].rearrange("p (c n) -> p c n", c=KC) for g in range(2)]
    ST = [k.psum[:, 2 + 2 * g:4 + 2 * g, :] for g in range(2)]
    OB, TB = k.psum[:, 6, :], k.psum[:, 7, :]
    MT = TB[:, 0:64].bitcast(BF16)
    GR = XP // XG
    HP = XP // 2
    SCALE = float(1.0 / np.sqrt(np.float32(XD)))
    scratch = [[nc.dram_tensor(f"scratch_{o}{s}", (3 * XD, XP, D), BF16).ap() for s in range(2)] for o in "qk"]
    operand = [k.qop, k.kop]

    with nc.Block() as block:
        @block.sync
        def _(sp):
            def hold(sem, value):
                sp.wait_ge(sem, value)
                sp.sem_inc(sync_waits, 1)

            def write(t, s):
                for j, part_ready in enumerate((highs_ready, mids_ready, lows_ready)):
                    hold(part_ready, t + 1)
                    for o in range(2):
                        rows = slice(j * XD, (j + 1) * XD) if o == 0 else slice(j, 3 * XD, 3)
                        sp.dma_start(scratch[o][s][rows, :, :].rearrange("d a n -> a d n"), k.xpart[s][:, j, o, :]).then_inc(written[s], 16)

            def read(t, s, half):
                hold(written[s], nth(t, s, 96))
                cut = slice(half * HP, (half + 1) * HP)
                for o in range(2):
                    src = scratch[o][s].rearrange("r a n -> r (a n)")[:, half * HP * D:(half + 1) * HP * D].unsqueeze(1 - o)
                    src = src.broadcast_to([3 * XD, 3, HP * D] if o == 0 else [3, 3 * XD, HP * D])
                    sp.dma_start(operand[o][s][0:XR, cut, :], src).then_inc(loaded[half][s], 16)

            def rows(t, s, half):
                hold(mrow_ready, 2 * t + half + 1)
                dst = k.qop[s][XR:XR + 3, half * HP:(half + 1) * HP, :].rearrange("r a (c n) -> r (a c) n", c=KC)
                sp.dma_start(dst, k.mrow[half][:, :]).then_inc(rows_in[half], 16)

            def step(tp, tf, tb, a):
                if tb is not None:
                    rows(tb, a, 1)
                if tp is not None:
                    write(tp, a)
                    if tb is not None:
                        hold(st_done, GR * tb + GR // 2)
                    read(tp, a, 0)
                if tf is not None:
                    rows(tf, 1 - a, 0)
                if tp is not None:
                    if tb is not None:
                        hold(st_done, GR * tb + GR)
                    read(tp, a, 1)
            pipeline3(sp, step)

        @block.gpsimd
        def _(pool):
            def split_max(t, half):
                own = Steps(pool, part_steps, 2 * t + half, 3)
                zero = k.zero[:, :].broadcast_to([P, 2 * HP])
                src = k.negmax[:, half * 2 * HP:(half + 1) * 2 * HP]
                pool.wait_ge(max_ready, XP * t + HP * (half + 1))
                wait(pool, mt_turned, 2 * t + half - 1)
                own(nc.gpsimd.tensor_tensor(k.mpart[half][:, 0, :], src, zero, ALU.add))
                own(nc.gpsimd.tensor_tensor(src, src, k.mpart[half][:, 0, :], ALU.subtract))
                own(nc.gpsimd.tensor_tensor(k.mpart[half][:, 1, :], src, zero, ALU.add))
                nc.gpsimd.tensor_tensor(k.mpart[half][:, 2, :], src, k.mpart[half][:, 1, :], ALU.subtract).then_inc(negmax_parts, 1)
                own.end()

            def context(t, s):
                wait(pool, lows_ready, t - 1)
                wait(pool, ctx_turned, t - 1)
                nc.gpsimd.tensor_tensor(k.xsrc[s][:, 1, :], k.ctx[:, t, :], k.zero[:, :].broadcast_to([P, D]), ALU.add).then_inc(context_ready, 1)

            def step(tp, tf, tb, a):
                if tp is not None:
                    norm_rstd(k, nc, pool, tp, a, stats_ready, rstd_ready)
                    context(tp, a)
                    pool.wait_ge(highs_ready, tp + 1)
                    pool.wait_ge(context_ready, tp + 1)
                    nc.gpsimd.tensor_tensor(k.rest[:, :, :], k.xsrc[a][:, :, :], k.xpart[a][:, 0, :, :], ALU.subtract).then_inc(rests_ready, 1)
                    pool.wait_ge(mids_ready, tp + 1)
                    nc.gpsimd.tensor_tensor(k.xpart[a][:, 2, :, :], k.rest[:, :, :], k.xpart[a][:, 1, :, :], ALU.subtract).then_inc(lows_ready, 1)
                if tf is not None:
                    split_max(tf, 0)
                    split_max(tf, 1)
            pipeline3(pool, step)

        @block.tensor
        def _(pe):
            def turn_max(t, half):
                pe.wait_ge(negmax_parts, 2 * t + half + 1)
                if half == 0:
                    wait(pe, mrow_ready, 2 * t)
                    wait(pe, x_done, t - 1)
                else:
                    pe.wait_ge(v_ready, t + 1)
                nc.tensor.transpose(MT[:, :], k.mpart[half][:, :, :].rearrange("p j m -> p (j m)"), k.identb[:, :]).then_inc(mt_turned, 1)

            def values(t, s, g):
                u = GR * t + g
                pe.wait_ge(exp_done, u + 1)
                if g == 0:
                    pe.wait_ge(v_ready, t + 1)
                if g % (GR // 2) == 0:
                    wait(pe, xout_ready, 2 * t + g // (GR // 2))
                for a in range(XG):
                    p = XG * g + a
                    b, c = p // 4 % 2, p % 4
                    for lc in range(KC):
                        last = nc.tensor.matmul(OB[XV * c:XV * (c + 1), b * D:(b + 1) * D], k.vT[s][:, lc, p, :],
                                                k.xprob[g % 2][:, a, lc, :], start=lc == 0, stop=lc == KC - 1)
                last.then_inc(pv_done, 1)

            def turn_values(t):
                pe.wait_ge(xout_ready, 2 * t + 2)
                for b in range(4):
                    for qc in range(KC):
                        c = (qc * 4 + b) * XC
                        last = nc.tensor.matmul(TB[:, c:c + XC], k.xout[b // 2][:, (b % 2) * D + qc * P:(b % 2) * D + (qc + 1) * P],
                                                k.place[:, :], start=True, stop=True)
                last.then_inc(placed, 1)

            def turn_out(t):
                pe.wait_ge(on_ready, t + 1)
                for qc in range(KC):
                    last = nc.tensor.transpose(TB[:, qc * P:(qc + 1) * P], k.on[0][:, qc * P:(qc + 1) * P], k.ident[:, :])
                last.then_inc(oT_turned, 1)

            def turn_context(t, s):
                pe.wait_ge(context_ready, t + 1)
                pe.wait_ge(mrow_ready, 2 * t + 1)
                for lc in range(KC):
                    last = nc.tensor.transpose(TB[:, (2 + lc) * P:(3 + lc) * P], k.xsrc[s][:, 1, lc * P:(lc + 1) * P], k.ident[:, :])
                last.then_inc(ctx_turned, 1)

            def step(tp, tf, tb, a):
                before = tb - 1 if tb is not None and not (isinstance(tb, int) and tb == 0) else None
                for g in range(GR):
                    if tb is not None:
                        if g == 1:
                            turn_max(tb, 1)
                        u = GR * tb + g
                        if g % (GR // 2) == 0:
                            pe.wait_ge(rows_in[g // (GR // 2)], 16 * tb + 16)
                        wait(pe, exp_done, u - 1)
                        for j in range(XG):
                            for lc in range(KC):
                                last = nc.tensor.matmul(ST[g % 2][:, j, lc * D:(lc + 1) * D], k.kop[a][0:XR + 3, XG * g + j, lc * P:(lc + 1) * P],
                                                        k.qop[a][0:XR + 3, XG * g + j, :], start=True, stop=True)
                        last.then_inc(st_done, 1)
                    if tf is not None:
                        if g % (GR // 2) == 0:
                            pe.wait_ge(loaded[g // (GR // 2)][1 - a], nth(tf, 1 - a, 32))
                        for j in range(XG):
                            p = XG * g + j
                            wait(pe, max_ready, XP * tf + p - 1)
                            for qc in range(KC):
                                last = nc.tensor.matmul(SB[p % 2][:, qc, :], k.qop[1 - a][0:XR, p, qc * P:(qc + 1) * P],
                                                        k.kop[1 - a][0:XR, p, :], start=True, stop=True)
                            last.then_inc(s_done, 1)
                        if g == 5:
                            turn_max(tf, 0)
                        if g == 6:
                            turn_context(tf, 1 - a)
                    if before is not None and g == 2:
                        pe.wait_ge(mrow_ready, 2 * tb + 2)
                        turn_values(before)
                    if before is not None and g == 3:
                        turn_out(before)
                    if tb is not None and g >= 1:
                        values(tb, a, g - 1)
                if tb is not None:
                    values(tb, a, GR - 1)
            early = len(turning.groups) - 4
            turning.tensor(pe, 0, early)
            quantising.tensor(pe)
            turning.tensor(pe, early)
            pe.wait_ge(turning.by_act, turning.groups_of("act"))
            pe.wait_ge(turning.by_dve, turning.groups_of("dve"))
            pe.wait_ge(quantising.done, 1)
            pe.wait_ge(ones_set, 1)
            pipeline3(pe, step)
            pe.wait_ge(x_done, TILES - 1)
            turn_values(TILES - 1)
            turn_out(TILES - 1)

        @block.scalar
        def _(act):
            def max_rows(t, half):
                act.wait_ge(mt_turned, 2 * t + half + 1)
                wait(act, rows_in[half], 16 * t)
                nc.scalar.activation(k.mrow[half][:, :], MT[0:6 * HP, :], ACT.Copy).then_inc(mrow_ready, 1)

            def turned_values(t, s):
                act.wait_ge(ctx_turned, t + 1)
                wait(act, pv_done, GR * (t - 1))
                nc.scalar.activation(k.vT[s][:, :, :, 0:XD], TB[:, D:2 * D].rearrange("p (c a d) -> p c a d", c=KC, d=XD), ACT.Copy).then_inc(v_ready, 1)

            def half_out(t, half):
                act.wait_ge(pv_done, GR * t + (half + 1) * GR // 2)
                wait(act, placed, t)
                nc.scalar.activation(k.xout[half], OB, ACT.Copy).then_inc(xout_ready, 1)

            def step(tp, tf, tb, a):
                for g in range(GR):
                    if tb is not None:
                        u = GR * tb + g
                        act.wait_ge(st_done, u + 1)
                        wait(act, pv_done, u - 1)
                        nc.scalar.activation(k.xprob[g % 2][:, :, :, :], ST[g % 2], ACT.Exp, scale=SCALE).then_inc(exp_done, 1)
                        if g == 1:
                            max_rows(tb, 1)
                        if g == GR // 2:
                            half_out(tb, 0)
                    if tp is not None and g == 1:
                        act.wait_ge(src_ready, tp + 1)
                        act.wait_ge(context_ready, tp + 1)
                        wait(act, written[a], nth(tp, a, 96) - 96)
                        nc.scalar.activation(k.xpart[a][:, 0, :, :], k.xsrc[a][:, :, :], ACT.Copy).then_inc(highs_ready, 1)
                    if tp is not None and g == 2:
                        act.wait_ge(rests_ready, tp + 1)
                        nc.scalar.activation(k.xpart[a][:, 1, :, :], k.rest[:, :, :], ACT.Copy).then_inc(mids_ready, 1)
                    if tf is not None and g == 5:
                        max_rows(tf, 0)
                    if tf is not None and g == 6:
                        turned_values(tf, 1 - a)
                if tb is not None:
                    half_out(tb, 1)
            pipeline3(act, step, lambda: turning.scalar(act))

        @block.vector
        def _(dve):
            nc.vector.tensor_scalar(k.place[:, 0:4 * XD], k.place[:, 0:4 * XD], k.gamma[:, :], None, ALU.mult)

            def constants():
                for s in range(2):
                    nc.vector.memset(k.vT[s][:, :, :, XD:XD + 1], 1.0)
                    nc.vector.memset(k.vT[s][:, :, :, XD + 1:], 0.0)
                    ins = nc.vector.memset(k.mpart[s][:, 3:, :], 0.0)
                ins.then_inc(ones_set, 1)
                quantising.vector(dve)
                turning.vector(dve)

            def normalise(t, s):
                wait(dve, lows_ready, t - 1)
                dve.wait_ge(rstd_ready, t + 1)
                nc.vector.tensor_scalar(k.xsrc[s][:, 0, :], k.x[:, t, :], k.moments[:, s, 0:1], k.rstd[:, s, :],
                                        ALU.subtract, ALU.mult).then_inc(src_ready, 1)

            def add_out(t):
                dve.wait_ge(oT_turned, t + 1)
                nc.vector.tensor_tensor(k.x[:, t, :], k.x[:, t, :], TB[:, 0:D], ALU.add).then_inc(x_done, 1)

            def divide(t):
                dve.wait_ge(placed, t + 1)
                tv = TB[:, 0:KC * 4 * XC].rearrange("p (q b c) -> p q b c", q=KC, b=4)
                nc.vector.reciprocal(k.xrs[:, :, :, :, 0], tv[:, :, :, 4 * XD:]).then_inc(back_steps, 1)
                dve.wait_ge(back_steps, t + 1)
                for qc in range(KC):
                    ins = nc.vector.tensor_tensor(k.on[0][:, qc * P:(qc + 1) * P].rearrange("p (b a d) -> p b a d", b=4, d=XD),
                                                  tv[:, qc, :, 0:4 * XD].rearrange("p b (a d) -> p b a d", d=XD),
                                                  k.xrs[:, qc, :, :, :].broadcast_to([P, 4, 4, XD]), ALU.mult)
                ins.then_inc(on_ready, 1)

            def step(tp, tf, tb, a):
                before = tb - 1 if tb is not None and not (isinstance(tb, int) and tb == 0) else None
                if tp is not None:
                    norm_moments(k, nc, Steps(dve, front_steps, tp, 2), tp, a, stats_ready)
                    if tf is None:
                        normalise(tp, a)
                if tf is not None:
                    for p in range(XP):
                        dve.wait_ge(s_done, XP * tf + p + 1)
                        if p % HP == 0:
                            wait(dve, negmax_parts, 2 * tf + p // HP - 1)
                        nc.vector.tensor_reduce(k.negmax[:, 2 * p:2 * p + 2], SB[p % 2], AX.X, ALU.max, negate=True).then_inc(max_ready, 1)
                        if tp is not None and p == XG:
                            normalise(tp, a)
                        if before is not None and p == 3 * XG - 1:
                            divide(before)
                        if before is not None and p == 4 * XG - 1:
                            add_out(before)
                elif before is not None:
                    divide(before)
                    add_out(before)
            pipeline3(dve, step, constants)
            divide(TILES - 1)
            add_out(TILES - 1)




def sparse_ffn(k, w):
    nc, sem = k.nc, k.sem
    names = ("stats_ready rstd_ready xn_ready xT_turned xnT_ready gate_done up_done silu_ready prod_ready abs_ready kept_ready "
             "down_done x_done front_steps unit_steps").split()
    (stats_ready, rstd_ready, xn_ready, xT_turned, xnT_ready, gate_done, up_done, silu_ready, prod_ready, abs_ready, kept_ready,
     down_done, x_done, front_steps, unit_steps) = (sem("f0_" + n) for n in names)
    G = [k.psum[:, g, :] for g in range(GB)]
    U = [k.psum[:, 2 + g, :] for g in range(GB)]
    TB, Y = k.psum[:, 4, :], k.psum[:, 5, 0:D]
    hid = [k.ffn_h[g][:, :, :] for g in range(GB)]
    mag = [k.ffn_a[g][:, :, :] for g in range(GB)]
    flat = [k.ffn_h[g][:, :, :].rearrange("p i n -> p (i n)") for g in range(GB)]

    with nc.Block() as block:
        @block.gpsimd
        def _(pool):
            def tile(tf, sf, tb, sb):
                if tf is not None:
                    norm_rstd(k, nc, pool, tf, sf, stats_ready, rstd_ready)
            pipeline(pool, tile)

        @block.tensor
        def _(pe):
            def gate_up(t, s, g):
                wait(pe, silu_ready, 2 * t + g - 1)
                for bank, wt, done in ((G[g], w["gate"], gate_done), (U[g], w["up"], up_done)):
                    if wt is w["up"]:
                        wait(pe, prod_ready, 2 * t + g - 1)
                    for i in range(PL):
                        for kc in range(KC):
                            last = nc.tensor.matmul(bank[:, i * P:(i + 1) * P], wt[:, kc, g * PL * P + i:(g + 1) * PL * P:PL],
                                                    k.xnT[s][:, kc, :], start=kc == 0, stop=kc == KC - 1)
                    last.then_inc(done, 1)

            def down(t, g):
                pe.wait_ge(kept_ready, 2 * t + g + 1)
                if g == 0:
                    wait(pe, x_done, t)
                for i in range(PL):
                    last = nc.tensor.matmul(Y, k.ffn_h[g][:, i, :], w["down"][:, g, i, :], start=g == 0 and i == 0, stop=g == GB - 1 and i == PL - 1)
                last.then_inc(down_done, 1)

            def tile(tf, sf, tb, sb):
                if tb is not None:
                    if isinstance(tb, int) and tb == 0:
                        pe.wait_ge(k.ffn_in, 3 * 16)
                    pe.wait_ge(xnT_ready, tb + 1)
                    gate_up(tb, sb, 0)
                    if not (isinstance(tb, int) and tb == 0):
                        down(tb - 1, 1)
                if tf is not None:
                    pe.wait_ge(xn_ready, tf + 1)
                    wait(pe, xnT_ready, tf)
                    for kc in range(KC):
                        last = nc.tensor.transpose(TB[:, kc * P:(kc + 1) * P], k.xn[sf][:, kc * P:(kc + 1) * P], k.ident[:, :])
                    last.then_inc(xT_turned, 1)
                if tb is not None:
                    gate_up(tb, sb, 1)
                    down(tb, 0)
            pipeline(pe, tile)
            down(TILES - 1, 1)

        @block.scalar
        def _(act):
            def unit(t, g):
                u = 2 * t + g
                act.wait_ge(gate_done, u + 1)
                wait(act, prod_ready, u - 1)
                nc.scalar.activation(k.ffn_s[g][:, :], G[g], ACT.Silu).then_inc(silu_ready, 1)

            def magnitude(t, g):
                u = 2 * t + g
                act.wait_ge(prod_ready, u + 1)
                wait(act, kept_ready, u - 1)
                nc.scalar.activation(mag[g], hid[g], ACT.Abs).then_inc(abs_ready, 1)

            def tile(tf, sf, tb, sb):
                if tf is not None:
                    act.wait_ge(xT_turned, tf + 1)
                    wait(act, up_done, 2 * tf - 2)
                    nc.scalar.activation(k.xnT[sf][:, :, :], TB[:, 0:D].rearrange("p (k n) -> p k n", n=P), ACT.Copy).then_inc(xnT_ready, 1)

            def whole(tf, sf, tb, sb):
                if tb is not None:
                    unit(tb, 0)
                    magnitude(tb, 0)
                tile(tf, sf, tb, sb)
                if tb is not None:
                    unit(tb, 1)
                    magnitude(tb, 1)
            pipeline(act, whole)

        @block.vector
        def _(dve):
            def unit(t, g):
                u = 2 * t + g
                own = Steps(dve, unit_steps, u, 3)
                dve.wait_ge(silu_ready, u + 1)
                dve.wait_ge(up_done, u + 1)
                wait(dve, down_done, u - 1)
                nc.vector.tensor_tensor(flat[g], k.ffn_s[g][:, :], U[g], ALU.mult).then_inc(prod_ready, 1)
                dve.wait_ge(abs_ready, u + 1)
                a = mag[g]
                nc.vector.tensor_tensor(k.near[:, :, :], a[:, 0:3, :], a[:, 1:4, :], ALU.is_ge)
                nc.vector.tensor_tensor(k.over[:, :, :], a[:, 0:2, :], a[:, 2:4, :], ALU.is_ge)
                own(nc.vector.tensor_tensor(k.far[:, :, :], a[:, 0:1, :], a[:, 3:4, :], ALU.is_ge))
                nc.vector.tensor_tensor(k.outer[:, :, :], k.near[:, 0:3:2, :], k.over[:, :, :], ALU.add)
                own(nc.vector.tensor_tensor(k.inner[:, :, :], k.over[:, :, :], k.near[:, 1:2, :].broadcast_to([P, 2, P]), ALU.add))
                nc.vector.tensor_tensor(k.outer[:, :, :], k.outer[:, :, :], k.far[:, :, :].broadcast_to([P, 2, P]), ALU.add)
                nc.vector.tensor_tensor(k.inner[:, 0, :], k.inner[:, 0, :], k.near[:, 2, :], ALU.subtract)
                own(nc.vector.tensor_tensor(k.inner[:, 1, :], k.inner[:, 1, :], k.near[:, 0, :], ALU.subtract))
                own.end()
                h = hid[g]
                nc.vector.scalar_tensor_tensor(h[:, 0, :], k.outer[:, 0, :], 1.5, h[:, 0, :], ALU.is_gt, ALU.mult)
                nc.vector.scalar_tensor_tensor(h[:, 1, :], k.inner[:, 1, :], 0.5, h[:, 1, :], ALU.is_gt, ALU.mult)
                nc.vector.scalar_tensor_tensor(h[:, 2, :], k.inner[:, 0, :], 0.5, h[:, 2, :], ALU.is_lt, ALU.mult)
                nc.vector.scalar_tensor_tensor(h[:, 3, :], k.outer[:, 1, :], 1.5, h[:, 3, :], ALU.is_lt, ALU.mult).then_inc(kept_ready, 1)

            def add_out(t):
                dve.wait_ge(down_done, 2 * t + 2)
                nc.vector.tensor_tensor(k.x[:, t, :], k.x[:, t, :], Y, ALU.add).then_inc(x_done, 1)

            def tile(tf, sf, tb, sb):
                if tf is not None:
                    front = Steps(dve, front_steps, tf, 2)
                    norm_moments(k, nc, front, tf, sf, stats_ready)
                    dve.wait_ge(rstd_ready, tf + 1)
                    wait(dve, xT_turned, tf - 1)
                    nc.vector.tensor_scalar(k.xn[sf][:, :], k.x[:, tf, :], k.moments[:, sf, 0:1], k.rstd[:, sf, :],
                                            ALU.subtract, ALU.mult).then_inc(xn_ready, 1)
                if tb is not None:
                    unit(tb, 0)
                    if not (isinstance(tb, int) and tb == 0):
                        add_out(tb - 1)
                    unit(tb, 1)
            pipeline(dve, tile)
            add_out(TILES - 1)




def expert_groups(k):
    groups = []
    for u in range(2):
        for kc in range(KC):
            cut = slice(kc * P, (kc + 1) * P)
            for c in range(0, MC, 4):
                groups.append(([k.raw_gu[:, u, c + j, cut] for j in range(4)],
                               k.wgu[:, kc, u, c * P:(c + 4) * P].rearrange("p (j n) -> p j n", n=P)))
            groups.append(([k.raw_gu[0:EI, u, MC, cut]], k.wgu[:, kc, u, MC * P:MC * P + EI].unsqueeze(1)))
    for c in range(0, MC, 2):
        groups.append(([k.raw_d[:, nb, (c + j) * P:(c + j + 1) * P] for j in range(2) for nb in range(2)],
                       k.wd[:, c:c + 2, :].rearrange("p c (b n) -> p (c b) n", n=P)))
    groups.append(([k.raw_d[:, nb, MC * P:MC * P + EI] for nb in range(2)], k.wd[0:EI, MC, :].rearrange("p (b n) -> p b n", n=P)))
    return groups


def experts(k, out):
    nc, sem = k.nc, k.sem
    names = "stats_done moments_done stats_ready rstd_ready xn_ready xT_turned xall_ready logits_done router_turned router_ready".split()
    (stats_done, moments_done, stats_ready, rstd_ready, xn_ready, xT_turned, xall_ready, logits_done, router_turned, router_ready) = (sem("m0_" + n) for n in names)
    T = [k.psum[:, 4 + 2 * s, 0:KC * P].rearrange("p (k n) -> p k n", n=P) for s in range(2)]
    LB, RB = k.psum[:, 5, 0:TILES * E], k.psum[:, 7, 0:KC * P].rearrange("p (k n) -> p k n", n=P)[:, :, 0:E]

    groups = expert_groups(k)
    early = 10
    turning = WeightTurning(k, "w3", groups, by_dve=range(len(groups) - 4, len(groups)))

    with nc.Block() as block:
        @block.gpsimd
        def _(pool):
            pool.wait_ge(stats_ready, 1)
            nc.gpsimd.tensor_tensor(k.m_rstd[:, :, :], k.m_moments[:, :, 1:2], k.halfpow[:, :].unsqueeze(1).broadcast_to([P, TILES, 1]), ALU.pow).then_inc(rstd_ready, 1)

        @block.tensor
        def _(pe):
            def logits(t):
                pe.wait_ge(xall_ready, t + 1)
                for kc in range(KC):
                    last = nc.tensor.matmul(LB[:, t * E:(t + 1) * E], k.xall[:, kc, t, :], k.wr[:, kc, :], start=kc == 0, stop=kc == KC - 1)
                last.then_inc(logits_done, 1)

            pe.wait_ge(k.moe_in, k.moe_loads * 16)
            for kc in range(KC):
                last = nc.tensor.transpose(RB[:, kc, :], k.raw_r[:, kc * P:(kc + 1) * P], k.ident[0:E, 0:E])
            last.then_inc(router_turned, 1)
            turning.tensor(pe, 0, early)
            for t in range(TILES):
                pe.wait_ge(xn_ready, t + 1)
                if t >= 2:
                    pe.wait_ge(xall_ready, t - 1)
                for kc in range(KC):
                    last = nc.tensor.transpose(T[t % 2][:, kc, :], k.xn[t % 2][:, kc * P:(kc + 1) * P], k.ident[:, :])
                last.then_inc(xT_turned, 1)
                if t == 1:
                    pe.wait_ge(router_ready, 1)
                if t >= 1:
                    logits(t - 1)
            logits(TILES - 1)

        @block.scalar
        def _(act):
            act.wait_ge(router_turned, 1)
            nc.scalar.activation(k.wr[:, :, :], RB, ACT.Copy).then_inc(router_ready, 1)
            turning.scalar(act, 0, early)
            for t in range(TILES):
                act.wait_ge(xT_turned, t + 1)
                nc.scalar.activation(k.xall[:, :, t, :], T[t % 2], ACT.Copy).then_inc(xall_ready, 1)

        @block.vector
        def _(dve):
            for t in range(TILES):
                nc.vector.bn_stats(k.m_stats[:, t, :], k.x[:, t, :]).then_inc(stats_done, 1)
            for t in range(TILES):
                dve.wait_ge(stats_done, t + 1)
                nc.vector.bn_aggr(k.m_moments[:, t, :], k.m_stats[:, t, :]).then_inc(moments_done, 1)
            dve.wait_ge(moments_done, TILES)
            nc.vector.tensor_scalar(k.m_moments[:, :, 1:2], k.m_moments[:, :, 1:2], LN_EPS, None, ALU.add).then_inc(stats_ready, 1)
            dve.wait_ge(rstd_ready, 1)
            for t in range(TILES):
                if t >= 2:
                    dve.wait_ge(xT_turned, t - 1)
                nc.vector.tensor_scalar(k.xn[t % 2][:, :], k.x[:, t, :], k.m_moments[:, t, 0:1], k.m_rstd[:, t, :],
                                        ALU.subtract, ALU.mult).then_inc(xn_ready, 1)

    route(k, turning, early)

    names = "gate_done up_done comb_done silu_ready hid_ready down_done x_done prod_done stored".split()
    (gate_done, up_done, comb_done, silu_ready, hid_ready, down_done, x_done, prod_done, stored) = (sem("m2_" + n) for n in names)
    G = [k.psum[:, g, :] for g in range(2)]
    U = [k.psum[:, 2 + g, :] for g in range(2)]
    C = [k.psum[:, 4 + g, :] for g in range(2)]
    Y = [k.psum[:, 6 + g, 0:D] for g in range(2)]
    rows = [P] * MC + [EI]
    tok = HALF * P

    with nc.Block() as block:
        @block.tensor
        def _(pe):
            def half(v):
                for c in range(MCS):
                    n, g = rows[c], c % 2
                    units = v * MCS + c
                    cols = slice(c * P, c * P + n)
                    xs = k.xall[:, :, :, :].rearrange("p k t n -> p k (t n)")
                    wait(pe, silu_ready, units - 1)
                    for kc in range(KC):
                        last = nc.tensor.matmul(G[g][0:n, :], k.wgu[:, kc, 0, cols], xs[:, kc, bass.ds(v * tok, tok)], start=kc == 0, stop=kc == KC - 1)
                    last.then_inc(gate_done, 1)
                    wait(pe, hid_ready, units - 1)
                    for kc in range(KC):
                        last = nc.tensor.matmul(U[g][0:n, :], k.wgu[:, kc, 1, cols], xs[:, kc, bass.ds(v * tok, tok)], start=kc == 0, stop=kc == KC - 1)
                    last.then_inc(up_done, 1)
                    if c < MC:
                        nc.tensor.matmul(C[g], k.expert[:, cols], k.combT[:, bass.ds(v * tok, tok)], start=True, stop=True).then_inc(comb_done, 1)
                for j in range(HALF):
                    wait(pe, x_done, v * HALF + j - 1)
                    for c in range(MCS):
                        if j == 0:
                            pe.wait_ge(hid_ready, v * MCS + c + 1)
                        last = nc.tensor.matmul(Y[j % 2], k.hid[0:rows[c], c, j * P:(j + 1) * P], k.wd[0:rows[c], c, :], start=c == 0, stop=c == MCS - 1)
                    last.then_inc(down_done, 1)
            for v in range(TILES // HALF):
                half(v)

        @block.scalar
        def _(act):
            def half(v):
                for c in range(MCS):
                    n, g = rows[c], c % 2
                    units = v * MCS + c
                    act.wait_ge(gate_done, units + 1)
                    wait(act, prod_done, units - 1)
                    nc.scalar.activation(k.sg[g][0:n, :], G[g][0:n, :], ACT.Silu).then_inc(silu_ready, 1)
            for v in range(TILES // HALF):
                half(v)

        @block.vector
        def _(dve):
            def half(v):
                for c in range(MCS):
                    n, g = rows[c], c % 2
                    units = v * MCS + c
                    dve.wait_ge(silu_ready, units + 1)
                    dve.wait_ge(up_done, units + 1)
                    wait(dve, down_done, v * HALF)
                    nc.vector.tensor_tensor(k.hid[0:n, c, :], k.sg[g][0:n, :], U[g][0:n, :], ALU.mult).then_inc(prod_done, 1)
                    dve.wait_ge(prod_done, units + 1)
                    if c < MC:
                        dve.wait_ge(comb_done, v * MC + c + 1)
                        nc.vector.tensor_tensor(k.hid[:, c, :], k.hid[:, c, :], C[g], ALU.mult).then_inc(hid_ready, 1)
                    else:
                        nc.vector.memset(k.pause[:, :], 0.0).then_inc(hid_ready, 1)
                for j in range(HALF):
                    t = v * HALF + j
                    dve.wait_ge(down_done, t + 1)
                    nc.vector.tensor_tensor(k.x[:, t, :], k.x[:, t, :], Y[j % 2], ALU.add).then_inc(x_done, 1)
            for v in range(TILES // HALF):
                half(v)

        @block.sync
        def _(sp):
            for t in range(TILES):
                sp.wait_ge(x_done, t + 1)
                sp.dma_start(tiles_of(out)[:, t, :], k.x[:, t, :]).then_inc(stored, 16)
            sp.wait_ge(stored, TILES * 16)


def route(k, turning, first):
    nc, sem = k.nc, k.sem
    scored, parted, turned, own_steps, copied = (sem("r_" + n) for n in "scored parted turned own_steps copied".split())
    LB, CB = k.psum[:, 5, 0:TILES * E], k.psum[0:3 * E, 6, :].bitcast(BF16)
    with nc.Block() as block:
        @block.scalar
        def _(act):
            nc.scalar.activation(k.score[:, :], LB, ACT.Sigmoid).then_inc(scored, 1)
            turning.scalar(act, first)

        @block.vector
        def _(dve):
            own = Steps(dve, own_steps, 0, 13)
            score = k.score[:, :].rearrange("p (t e) -> p t e", e=E)
            pick = k.pick[:, :].rearrange("p (t e) -> p t e", e=E)
            dve.wait_ge(scored, 1)
            own(nc.vector.tensor_tensor(pick, score, k.ebias[:, :].unsqueeze(1).broadcast_to([P, TILES, E]), ALU.add))
            for t in range(TILES):
                ins = nc.vector.max(k.best[:, t, :], pick[:, t, :])
            own(ins)
            for t in range(TILES):
                ins = nc.vector.max_index(k.besti[:, t, :], k.best[:, t, :], pick[:, t, :])
            own(ins)
            own(nc.vector.tensor_copy(k.bestf[:, :, :], k.besti[:, :, 0:TOPK]))
            own(nc.vector.tensor_tensor(k.hit[:, :, :, :], k.bestf[:, :, :].unsqueeze(3).broadcast_to([P, TILES, TOPK, E]),
                                        k.iota[:, :].unsqueeze(1).unsqueeze(1).broadcast_to([P, TILES, TOPK, E]), ALU.is_equal))
            own(nc.vector.tensor_reduce(pick, k.hit[:, :, :, :].rearrange("p t r e -> p t e r"), AX.X, ALU.add))
            own(nc.vector.tensor_tensor(k.pick[:, :], k.pick[:, :], k.score[:, :], ALU.mult))
            own(nc.vector.tensor_reduce(k.wsum[:, :, 0], pick, AX.X, ALU.add))
            own(nc.vector.tensor_scalar(k.wsum[:, :, 0], k.wsum[:, :, 0], 1e-20, None, ALU.add))
            own(nc.vector.reciprocal(k.wsum[:, :, 1], k.wsum[:, :, 0]))
            own(nc.vector.tensor_tensor(pick, pick, k.wsum[:, :, 1:2].broadcast_to([P, TILES, E]), ALU.mult))
            parts = k.parts[:, :, :, :]
            nc.vector.tensor_copy(parts[:, :, 0, :], pick).then_inc(own_steps, 1)
            own.n += 1
            dve.wait_ge(own_steps, own.n)
            own(nc.vector.tensor_tensor(pick, pick, parts[:, :, 0, :], ALU.subtract))
            own.end()
            nc.vector.tensor_copy(parts[:, :, 1, :], pick).then_inc(parted, 1)
            dve.wait_ge(parted, 1)
            nc.vector.tensor_tensor(parts[:, :, 2, :], pick, parts[:, :, 1, :], ALU.subtract).then_inc(parted, 1)

            turning.vector(dve)
            dve.wait_ge(turned, 1)
            nc.vector.tensor_copy(k.combT[:, :], CB[:, :]).then_inc(copied, 1)

        @block.tensor
        def _(pe):
            turning.tensor(pe, first)
            pe.wait_ge(parted, 2)
            for t in range(TILES):
                last = nc.tensor.transpose(CB[:, t * P:(t + 1) * P], k.parts[:, t, :, :].rearrange("p s e -> p (s e)"), k.identb[:, :])
            last.then_inc(turned, 1)


def tiles_of(ap):
    return ap.rearrange("b s n -> (b s) n").rearrange("(t p) n -> p t n", p=P)


def rows_of(ap):
    return ap.rearrange("(j p) n -> p j n", p=P)


ATT_RAW = ("L0_attn_Wq", "L0_attn_Wk", "L0_attn_Wv", "L0_attn_Wo", "L1_attn_Wq", "L1_attn_Wk", "L1_attn_Wv", "L1_attn_Wo",
           "L1_xattn_wq", "L1_xattn_wk", "L1_xattn_wv", "L1_xattn_wo")


def load_experts(k, sp):
    d, loads = k.dram, 0
    for u in range(2):
        for f in range(4):
            i = 0
            while i < EI:
                row = EI * f + i
                n = min(EI - i, P - row % P)
                src = d["L1_ffn_gate_up_proj"][:, u * EI + i:u * EI + i + n, :].rearrange("(g f) i n -> f i g n", f=4)[f]
                sp.dma_start(k.raw_gu[row % P:row % P + n, u, row // P:MC:3, :], src).then_inc(k.moe_in, 16)
                loads += 1
                i += n
    for u, n in enumerate(("L1_ffn_shared_gate_w", "L1_ffn_shared_up_w")):
        sp.dma_start(k.raw_gu[0:EI, u, MC, :], d[n]).then_inc(k.moe_in, 16)
    for nb in range(KC):
        sp.dma_start(k.raw_d[:, nb, 0:MC * P].rearrange("p (e i) -> p e i", i=EI),
                     d["L1_ffn_down_proj"][:, nb * P:(nb + 1) * P, :].rearrange("e p i -> p e i")).then_inc(k.moe_in, 16)
    sp.dma_start(k.raw_d[:, :, MC * P:], rows_of(d["L1_ffn_shared_down_w"])).then_inc(k.moe_in, 16)
    sp.dma_start(k.raw_r[:, :], d["L1_ffn_router_w"]).then_inc(k.moe_in, 16)
    sp.dma_start(k.ebias[:, :], d["L1_ffn_e_bias"].partition_broadcast(P)).then_inc(k.moe_in, 16)
    sp.dma_start(k.iota[:, :], d["c_iota"]).then_inc(k.moe_in, 16)
    sp.dma_start(k.expert[:, :], d["c_expert"]).then_inc(k.moe_in, 16)
    k.moe_loads = loads + 2 + KC + 5


def setup(k):
    nc, d = k.nc, k.dram
    k.raw = {n: k.raw_first[:, i] for i, n in enumerate(ATT_RAW[0:4])}
    k.raw.update({n: k.raw_att[:, i] for i, n in enumerate(ATT_RAW[4:])})
    k.w1_bqk, k.w1_bv, k.w1_bo = k.sb("w1_bqk", [P, 4]), k.sb("w1_bv", [P, D]), k.sb("w1_bo", [P, D])
    k.w2_bq, k.w2_bk, k.w2_bv, k.w2_bo = k.sb("w2_bq", [P, D]), k.sb("w2_bk", [P, 2]), k.sb("w2_bv", [P, D]), k.sb("w2_bo", [P, D])
    k.bias_in, k.ffn_in, k.moe_in = k.sem("bias_in"), k.sem("ffn_in"), k.sem("moe_in")
    k.first_in, k.ctx_in, k.att_in, k.made = k.sem("first_in"), k.sem("ctx_in"), k.sem("att_in"), k.sem("made")
    with nc.Block() as block:
        @block.sync
        def _(sp):
            for n in ATT_RAW[0:4]:
                sp.dma_start(k.raw[n][:, :, :], rows_of(d[n])).then_inc(k.first_in, 16)
            sp.dma_start(k.ident[:, :], d["c_ident"]).then_inc(k.first_in, 16)
            sp.dma_start(k.x[:, :, :], tiles_of(d["x"])).then_inc(k.first_in, 16)
            sp.dma_start(k.rope[:, :, :], d["c_rope"].rearrange("p (a f) -> p a f", a=2)).then_inc(k.first_in, 16)
            sp.dma_start(k.causal[:, :], d["c_causal"]).then_inc(k.first_in, 16)
            sp.dma_start(k.parity[:, :], d["c_parity"]).then_inc(k.first_in, 16)
            sp.wait_ge(k.first_in, 9 * 16)

        @block.vector
        def _(dve):
            nc.vector.memset(k.halfpow[:, :], -0.5)
            nc.vector.memset(k.zero[:, :], 0.0)
            nc.vector.memset(k.ones[:, :], 1.0)
            nc.vector.memset(k.unround[:, :], -ROUND)
            for s in range(2):
                ins = nc.vector.memset(k.vblk[s][:, :, :, :], 0.0)
            ins.then_inc(k.made, 1)
            dve.wait_ge(k.made, 1)
            for s in range(2):
                nc.vector.memset(k.vblk[s][0:64, :, :, 32:33], 1.0)
                nc.vector.memset(k.vblk[s][64:128, :, :, 33:34], 1.0)
            dve.wait_ge(k.first_in, 9 * 16)
            nc.vector.tensor_copy(k.identb[:, :], k.ident[:, :])


def load_later_weights(k, sp):
    nc, d = k.nc, k.dram
    sp.dma_start(k.ctx[:, :, :], tiles_of(d["ctx_2048"])).then_inc(k.ctx_in, 16)
    sp.dma_start(k.place[:, :], d["c_place"]).then_inc(k.ctx_in, 16)
    sp.dma_start(k.mask[:, :, :], tiles_of(d["mask_BxSxS2_ff0"])).then_inc(k.ctx_in, 16)
    for n in ATT_RAW[4:]:
        sp.dma_start(k.raw[n][:, :, :], rows_of(d[n])).then_inc(k.att_in, 16)
    for buf, n in ((k.w1_bv, "L1_attn_bv"), (k.w1_bo, "L1_attn_bo"), (k.w2_bq, "L1_xattn_bq"), (k.w2_bv, "L1_xattn_bv"), (k.w2_bo, "L1_xattn_bo"), (k.gamma, "L0_xattn_gamma")):
        sp.dma_start(buf[:, :], d[n].partition_broadcast(P)).then_inc(k.bias_in, 16)
    with nc.allow_non_contiguous_dma(reason="256 biases, one to a partition"):
        for buf, n in ((k.w1_bqk[:, 0:2], "L1_attn_bq"), (k.w1_bqk[:, 2:4], "L1_attn_bk"), (k.w2_bk[:, :], "L1_xattn_bk")):
            sp.dma_start(buf, d[n].rearrange("(c p) -> p c", p=P)).then_inc(k.bias_in, 16)
    for n, i in (("L0_ffn_w_gate", "gate"), ("L0_ffn_w_up", "up")):
        sp.dma_start(k.w_ffn[i], rows_of(d[n])).then_inc(k.ffn_in, 16)
    sp.dma_start(k.w_ffn["down"].rearrange("p g i n -> p g (i n)"),
                 d["L0_ffn_w_down"].rearrange("(g p i) n -> p g (i n)", g=GB, i=PL)).then_inc(k.ffn_in, 16)
    sp.wait_ge(k.ctx_in, 3 * 16)
    sp.wait_ge(k.bias_in, 9 * 16)


class Quantising:

    def __init__(self, k, raws, scales):
        self.k, self.raws, self.scales = k, raws, scales
        self.steps_done, self.diag_ready, self.spread_done, self.done = (k.sem("wq_" + n) for n in "steps_done diag_ready spread_done done".split())
        self.banks = [k.psum[:, 4 + i, :] for i in range(len(raws))]

    def vector(self, dve):
        k, nc, raws = self.k, self.k.nc, self.raws
        dve.wait_ge(k.att_in, 8 * 16)
        own = Steps(dve, self.steps_done, 0, 6)
        for i, raw in enumerate(raws):
            nc.vector.tensor_reduce(k.wabs[:, 2 * i:2 * i + 2], raw[:, :, :], AX.X, ALU.max, apply_absolute_value=True)
        for by, bk in ((k.w1_bkm, k.w1_bqk[:, 2:4]), (k.w2_bkm, k.w2_bk[:, :])):
            for par in range(2):
                nc.vector.tensor_scalar(by[:, par, :], bk, k.parity[:, par:par + 1], None, ALU.mult)
        n = 2 * len(raws)
        own(nc.vector.memset(k.pause[:, :], 0.0))
        own(nc.vector.tensor_scalar(k.wscale[:, 0:n], k.wabs[:, 0:n], 1.0 / 127.0, Q_EPS, ALU.mult, ALU.max))
        own(nc.vector.reciprocal(k.wabs[:, 0:n], k.wscale[:, 0:n]))
        for first, last, op0, op1 in ((None, ROUND, ALU.mult, ALU.add), (ROUND, 127.0, ALU.subtract, ALU.min), (-127.0, None, ALU.max, None)):
            for i, raw in enumerate(raws):
                for j in range(KC):
                    row = raw[:, j, :]
                    by = k.wabs[:, 2 * i + j:2 * i + j + 1] if first is None else first
                    ins = nc.vector.tensor_scalar(row, row, by, last, op0, *([op1] if op1 else []))
            own(ins)
        for i in range(n):
            ins = nc.vector.tensor_scalar(k.diag[:, i, :], k.ident[:, :], k.wscale[:, i:i + 1], None, ALU.mult)
        ins.then_inc(self.diag_ready, 1)
        dve.wait_ge(self.spread_done, 1)
        for bank, scale in zip(self.banks, self.scales):
            ins = nc.vector.tensor_copy(scale[:, :], bank[:, 0:D])
        ins.then_inc(self.done, 1)
        own.end()

    def tensor(self, pe):
        k, nc = self.k, self.k.nc
        pe.wait_ge(self.diag_ready, 1)
        for i in range(2 * len(self.raws)):
            ins = nc.tensor.matmul(self.banks[i // 2][:, (i % 2) * P:(i % 2 + 1) * P], k.ones[:, :], k.diag[:, i, :], start=True, stop=True)
        ins.then_inc(self.spread_done, 1)


def attention_weights(k, w0):
    raw, sb = k.raw, k.sb
    k.w1_bkm, k.w2_bkm = sb("w1_bkm", [P, 2, 2]), sb("w2_bkm", [P, 2, 2])
    w1 = {"qk": w0["qk"], "v": w0["v"], "o": w0["o"], "bq": k.w1_bqk[:, 0:2], "bkm": k.w1_bkm, "bv": k.w1_bv, "bo": k.w1_bo}
    w2 = {"q": sb("w2_q", [P, KC, D], BF16), "k": sb("w2_k", [P, KC, D]), "v": sb("w2_v", [P, KC, D]), "o": sb("w2_o", [P, KC, D], BF16),
          "swq": sb("w2_swq", [P, D]), "swo": sb("w2_swo", [P, D]), "bq": k.w2_bq, "bkm": k.w2_bkm, "bv": k.w2_bv, "bo": k.w2_bo}
    k.wabs, k.wscale, k.diag = sb("wabs", [P, 4]), sb("wscale", [P, 4]), sb("diag", [P, 4, P])
    quantising = Quantising(k, [raw["L1_xattn_wq"], raw["L1_xattn_wo"]], [w2["swq"], w2["swo"]])
    groups = []
    for n, dst in (("L1_attn_Wq", w1["qk"][:, :, 0:D]), ("L1_attn_Wk", w1["qk"][:, :, D:2 * D]), ("L1_attn_Wv", w1["v"]), ("L1_attn_Wo", w1["o"]),
                   ("L1_xattn_wk", w2["k"]), ("L1_xattn_wv", w2["v"]), ("L1_xattn_wq", w2["q"]), ("L1_xattn_wo", w2["o"])):
        groups += square_groups(raw[n], dst)
    return w1, w2, quantising, WeightTurning(k, "w1", groups, by_dve=range(len(groups) - 4, len(groups), 2))


def decoder(nc, dram, out):
    with ExitStack() as ctx:
        k = allocate(nc, ctx, dram)
        setup(k)
        w0 = {"qk": k.sb("w0_qk", [P, KC, 2 * D]), "v": k.sb("w0_v", [P, KC, D]), "o": k.sb("w0_o", [P, KC, D])}
        raw = k.raw
        transpose_weights(k, "w0", square_groups(raw["L0_attn_Wq"], w0["qk"][:, :, 0:D]) + square_groups(raw["L0_attn_Wk"], w0["qk"][:, :, D:2 * D])
                          + square_groups(raw["L0_attn_Wv"], w0["v"]) + square_groups(raw["L0_attn_Wo"], w0["o"]))
        attention(k, "a0", ROPE, w0, lambda sp: load_later_weights(k, sp), lambda pool: set_ones(k, pool))
        w1, w2, quantising, turning = attention_weights(k, w0)
        channel_attention(k, quantising, turning)
        sparse_ffn(k, k.w_ffn)
        release(k, "c0")
        attention(k, "a1", SELF, w1, lambda sp: load_experts(k, sp))
        attention(k, "a2", CROSS, w2)
        experts(k, out)



_INS = ['x', 'ctx_2048', 'mask_BxSxS2_ff0', 'L0_attn_Wq', 'L0_attn_Wk', 'L0_attn_Wv', 'L0_attn_Wo', 'L0_xattn_gamma',
        'L0_ffn_w_gate', 'L0_ffn_w_up', 'L0_ffn_w_down', 'L1_attn_Wq', 'L1_attn_bq', 'L1_attn_Wk', 'L1_attn_bk',
        'L1_attn_Wv', 'L1_attn_bv', 'L1_attn_Wo', 'L1_attn_bo', 'L1_xattn_wq', 'L1_xattn_bq', 'L1_xattn_wk',
        'L1_xattn_bk', 'L1_xattn_wv', 'L1_xattn_bv', 'L1_xattn_wo', 'L1_xattn_bo', 'L1_ffn_router_w', 'L1_ffn_e_bias',
        'L1_ffn_gate_up_proj', 'L1_ffn_down_proj', 'L1_ffn_shared_gate_w', 'L1_ffn_shared_up_w', 'L1_ffn_shared_down_w']


def kernel(**inputs):
    import concourse.bacc as bacc
    from concourse.bass_utils import run_bass_kernel_spmd as run

    nc = bacc.Bacc("TRN2", target_bir_lowering=False, num_devices=1)
    arrays, dram = {}, {}
    for name, a in {**{n: inputs[n] for n in _INS}, **constants()}.items():
        a = np.ascontiguousarray(a)
        arrays[name + "_dram"] = a
        dram[name] = nc.dram_tensor(name + "_dram", a.shape, mybir.dt.from_np(a.dtype), kind="ExternalInput").ap()
    out = nc.dram_tensor("out_dram", (B, S, D), F32, kind="ExternalOutput").ap()
    decoder(nc, dram, out)
    return run(nc, [arrays], core_ids=[0]).results[0]["out_dram"]
```
